# Optimizing a Trainium2 kernel written in Bass

```python
import numpy as np
import jax
import jax.numpy as jnp

def _softmax(x, axis=-1):
    return jax.nn.softmax(x, axis=axis)

def _gelu(x):
    return jax.nn.gelu(x, approximate=True)

def _silu(x):
    return jax.nn.silu(x)

def _sigmoid(x):
    return jax.nn.sigmoid(x)

def _layernorm(x, axis=-1, eps=1e-05):
    m = jnp.mean(x, axis=axis, keepdims=True)
    v = jnp.var(x, axis=axis, keepdims=True)
    return (x - m) / jnp.sqrt(v + eps)

def _scatter_add(tgt, idx, src, axis=0):
    return tgt.at[idx].add(src)

def _segment_sum(src, seg, n):
    return jax.ops.segment_sum(src, seg, n)
kernel_name = 'mk_flamingo_gated_d2_seqx_r8_c50eca'

def setup_inputs(seed: int=0):
    np.random.seed(seed)
    _w = jnp.asarray

    def _rec_inputs():
        import jax
        import jax.numpy as jnp
        _rk = jax.random.key(seed)
        x = -0.0003929 + 0.9999 * jax.random.normal(jax.random.fold_in(_rk, 1), (16, 56, 256), jnp.float32)
        _lenS = 56 - jax.random.randint(jax.random.fold_in(_rk, 7), (16,), 0, max(1, 56 // 4) + 1, jnp.int32)
        _lenS2 = 1500 - jax.random.randint(jax.random.fold_in(_rk, 8), (16,), 0, max(1, 1500 // 4) + 1, jnp.int32)
        _ctx_1024P = jax.random.normal(jax.random.fold_in(_rk, 11), (16, 16, 128), jnp.float32)
        _ctx_1024c = jax.random.dirichlet(jax.random.fold_in(_rk, 511), 0.3 * jnp.ones((16,), jnp.float32), (16, 1500))
        _ctx_1024t = jnp.einsum('bsk,bkd->bsd', _ctx_1024c, _ctx_1024P)
        _ctx_1024t = _ctx_1024t * jax.lax.rsqrt(jnp.mean(jnp.square(_ctx_1024t)) + 1e-12) * 0.953939
        ctx_1024 = -0.000494167 + 1.00018 * (_ctx_1024t + 0.3 * jax.random.normal(jax.random.fold_in(_rk, 611), (16, 1500, 128), jnp.float32))
        _validS = jnp.arange(56)[None, :] < _lenS[:, None]
        _validS2 = jnp.arange(1500)[None, :] < _lenS2[:, None]
        _causal = jnp.tril(jnp.ones((56, 56), dtype=bool))
        mask_BxS2_bf1 = jnp.ones((16, 1500), dtype=bool)
        _g = jax.random.normal(jax.random.fold_in(_rk, 9001), (2, 2), jnp.float32)
        _g = jnp.sign(_g) * jnp.maximum(jnp.abs(_g), 1.0) + (_g == 0) * 1.0
        g_xattn = _g[0]
        g_ffn = _g[1]
        return (x, ctx_1024, mask_BxS2_bf1, g_xattn, g_ffn)
    x, ctx_1024, mask_BxS2_bf1, g_xattn, g_ffn = _rec_inputs()

    def _L0_xattn_setup():
        import jax, jax.numpy as jnp
        import numpy as np
        N_HEADS = 16
        N_KV_HEADS = 8
        HEAD_DIM = 128
        D_TEXT = 256
        D_VISION = 128
        GROUPS = N_HEADS // N_KV_HEADS
        key = jax.random.key(seed)
        ks = jax.random.split(key, 6)
        B, T_text, T_vis = (4, 256, 72)
        text_hidden = jax.random.normal(ks[0], (B, T_text, D_TEXT), dtype=jnp.float32)
        vision_tokens = jax.random.normal(ks[1], (B, T_vis, D_VISION), dtype=jnp.float32)
        vision_mask = jnp.ones((B, T_vis), dtype=bool)
        s = 0.02
        Wq = jax.random.normal(ks[2], (D_TEXT, N_HEADS * HEAD_DIM), dtype=jnp.float32) * s
        Wk = jax.random.normal(ks[3], (D_VISION, N_KV_HEADS * HEAD_DIM), dtype=jnp.float32) * s
        Wv = jax.random.normal(ks[4], (D_VISION, N_KV_HEADS * HEAD_DIM), dtype=jnp.float32) * s
        Wo = jax.random.normal(ks[5], (N_HEADS * HEAD_DIM, D_TEXT), dtype=jnp.float32) * s
        return {'text_hidden': text_hidden, 'vision_tokens': vision_tokens, 'vision_mask': vision_mask, 'Wq': Wq, 'Wk': Wk, 'Wv': Wv, 'Wo': Wo}
    _L0_xattn_all = _L0_xattn_setup()
    _L0_xattn_in = {k: v for k, v in _L0_xattn_all.items() if k in ('Wq', 'Wk', 'Wv', 'Wo')}
    del _L0_xattn_all

    def _L0_ffn_setup():
        import jax, jax.numpy as jnp
        import numpy as np
        B, S, D, H = (4, 256, 256, 1024)

        def fwht(x):
            orig_shape = x.shape
            n = orig_shape[-1]
            x = x.reshape(-1, n)
            h = 1
            while h < n:
                xb = x.reshape(-1, n // (2 * h), 2, h)
                a = xb[:, :, 0, :]
                b = xb[:, :, 1, :]
                x = jnp.stack([a + b, a - b], axis=2).reshape(-1, n)
                h *= 2
            scale = jnp.asarray(1.0 / np.sqrt(n), dtype=x.dtype)
            return (x * scale).reshape(orig_shape)
        key = jax.random.key(seed)
        kx, k1, k2, k3 = jax.random.split(key, 4)
        x = jax.random.normal(kx, (B, S, D), dtype=jnp.float32)
        W1 = jax.random.normal(k1, (H, D), dtype=jnp.float32) * (1.0 / np.sqrt(D))
        W2 = jax.random.normal(k2, (D, H), dtype=jnp.float32) * (1.0 / np.sqrt(H))
        W3 = jax.random.normal(k3, (H, D), dtype=jnp.float32) * (1.0 / np.sqrt(D))
        return {'x': x, 'W1': W1, 'W2': W2, 'W3': W3}
    _L0_ffn_all = _L0_ffn_setup()
    _L0_ffn_in = {k: v for k, v in _L0_ffn_all.items() if k in ('W1', 'W2', 'W3')}
    del _L0_ffn_all

    def _L1_xattn_setup():
        import jax, jax.numpy as jnp
        import numpy as np
        B, S1, S2, DCA = (2, 256, 128, 16)
        QDIM, KDIM, H = (256, 128, 16)
        HD = QDIM // H
        SCALE = HD ** (-0.5)
        EPS = 1e-06
        DCA_WEIGHT = 1.0

        def _ln(t, w, b):
            m = jnp.mean(t, axis=-1, keepdims=True)
            v = jnp.var(t, axis=-1, keepdims=True)
            return (t - m) * jax.lax.rsqrt(v + EPS) * w + b

        def _attn(q, k, v):
            s = jnp.einsum('bhqd,bhkd->bhqk', q, k) * SCALE
            p = jax.nn.softmax(s, axis=-1)
            return jnp.einsum('bhqk,bhkd->bhqd', p, v)
        key = jax.random.key(seed)
        ks = jax.random.split(key, 8)
        w = lambda k, shape: jax.random.normal(k, shape, jnp.float32) * 0.02
        return {'x': jax.random.normal(ks[0], (B, S1, QDIM), jnp.float32), 'y': jax.random.normal(ks[1], (B, S2 + DCA, KDIM), jnp.float32), 'Wq': w(ks[2], (QDIM, QDIM)), 'bq': jnp.zeros((QDIM,), jnp.float32), 'Wk': w(ks[3], (KDIM, QDIM)), 'bk': jnp.zeros((QDIM,), jnp.float32), 'Wv': w(ks[4], (KDIM, QDIM)), 'bv': jnp.zeros((QDIM,), jnp.float32), 'Wkv_dca': w(ks[5], (KDIM, 2 * QDIM)), 'bkv_dca': jnp.zeros((2 * QDIM,), jnp.float32), 'qn_w': jnp.ones((HD,), jnp.float32), 'qn_b': jnp.zeros((HD,), jnp.float32), 'kn_w': jnp.ones((HD,), jnp.float32), 'kn_b': jnp.zeros((HD,), jnp.float32), 'kn_dca_w': jnp.ones((HD,), jnp.float32), 'kn_dca_b': jnp.zeros((HD,), jnp.float32), 'Wo': w(ks[6], (QDIM, QDIM)), 'bo': jnp.zeros((QDIM,), jnp.float32)}
    _L1_xattn_all = _L1_xattn_setup()
    _L1_xattn_in = {k: v for k, v in _L1_xattn_all.items() if k in ('Wq', 'bq', 'Wk', 'bk', 'Wv', 'bv', 'Wkv_dca', 'bkv_dca', 'qn_w', 'qn_b', 'kn_w', 'kn_b', 'kn_dca_w', 'kn_dca_b', 'Wo', 'bo')}
    del _L1_xattn_all

    def _L1_ffn_setup():
        import jax, jax.numpy as jnp
        import numpy as np
        B, S, D = (2, 256, 256)
        I = 128
        E = 32
        K = 4
        NS = 1
        ALPHA = 7.0

        def _clamped_swiglu(x, wg, wu, wd):
            g = jnp.clip(x @ wg.T, -ALPHA, ALPHA)
            u = jnp.clip(x @ wu.T, -ALPHA, ALPHA)
            return jax.nn.silu(g) * u @ wd.T
        key = jax.random.key(seed)
        ks = jax.random.split(key, 9)
        s = 0.02
        return {'hidden': jax.random.normal(ks[0], (B, S, D), jnp.float32), 'router_w': jax.random.normal(ks[1], (E, D), jnp.float32) * s, 'expert_bias': jax.random.normal(ks[2], (E,), jnp.float32) * s, 'gate_w': jax.random.normal(ks[3], (E, I, D), jnp.float32) * s, 'up_w': jax.random.normal(ks[4], (E, I, D), jnp.float32) * s, 'down_w': jax.random.normal(ks[5], (E, D, I), jnp.float32) * s, 'shared_gate_w': jax.random.normal(ks[6], (NS * I, D), jnp.float32) * s, 'shared_up_w': jax.random.normal(ks[7], (NS * I, D), jnp.float32) * s, 'shared_down_w': jax.random.normal(ks[8], (D, NS * I), jnp.float32) * s}
    _L1_ffn_all = _L1_ffn_setup()
    _L1_ffn_in = {k: v for k, v in _L1_ffn_all.items() if k in ('router_w', 'expert_bias', 'gate_w', 'up_w', 'down_w', 'shared_gate_w', 'shared_up_w', 'shared_down_w')}
    del _L1_ffn_all
    return {'x': x, 'ctx_1024': ctx_1024, 'mask_BxS2_bf1': mask_BxS2_bf1, 'g_xattn': g_xattn, 'g_ffn': g_ffn, 'L0_xattn_Wq': _L0_xattn_in['Wq'], 'L0_xattn_Wk': _L0_xattn_in['Wk'], 'L0_xattn_Wv': _L0_xattn_in['Wv'], 'L0_xattn_Wo': _L0_xattn_in['Wo'], 'L0_ffn_W1': _L0_ffn_in['W1'], 'L0_ffn_W2': _L0_ffn_in['W2'], 'L0_ffn_W3': _L0_ffn_in['W3'], 'L1_xattn_Wq': _L1_xattn_in['Wq'], 'L1_xattn_bq': _L1_xattn_in['bq'], 'L1_xattn_Wk': _L1_xattn_in['Wk'], 'L1_xattn_bk': _L1_xattn_in['bk'], 'L1_xattn_Wv': _L1_xattn_in['Wv'], 'L1_xattn_bv': _L1_xattn_in['bv'], 'L1_xattn_Wkv_dca': _L1_xattn_in['Wkv_dca'], 'L1_xattn_bkv_dca': _L1_xattn_in['bkv_dca'], 'L1_xattn_qn_w': _L1_xattn_in['qn_w'], 'L1_xattn_qn_b': _L1_xattn_in['qn_b'], 'L1_xattn_kn_w': _L1_xattn_in['kn_w'], 'L1_xattn_kn_b': _L1_xattn_in['kn_b'], 'L1_xattn_kn_dca_w': _L1_xattn_in['kn_dca_w'], 'L1_xattn_kn_dca_b': _L1_xattn_in['kn_dca_b'], 'L1_xattn_Wo': _L1_xattn_in['Wo'], 'L1_xattn_bo': _L1_xattn_in['bo'], 'L1_ffn_router_w': _L1_ffn_in['router_w'], 'L1_ffn_expert_bias': _L1_ffn_in['expert_bias'], 'L1_ffn_gate_w': _L1_ffn_in['gate_w'], 'L1_ffn_up_w': _L1_ffn_in['up_w'], 'L1_ffn_down_w': _L1_ffn_in['down_w'], 'L1_ffn_shared_gate_w': _L1_ffn_in['shared_gate_w'], 'L1_ffn_shared_up_w': _L1_ffn_in['shared_up_w'], 'L1_ffn_shared_down_w': _L1_ffn_in['shared_down_w']}

def reference(x, ctx_1024, mask_BxS2_bf1, g_xattn, g_ffn, L0_xattn_Wq, L0_xattn_Wk, L0_xattn_Wv, L0_xattn_Wo, L0_ffn_W1, L0_ffn_W2, L0_ffn_W3, L1_xattn_Wq, L1_xattn_bq, L1_xattn_Wk, L1_xattn_bk, L1_xattn_Wv, L1_xattn_bv, L1_xattn_Wkv_dca, L1_xattn_bkv_dca, L1_xattn_qn_w, L1_xattn_qn_b, L1_xattn_kn_w, L1_xattn_kn_b, L1_xattn_kn_dca_w, L1_xattn_kn_dca_b, L1_xattn_Wo, L1_xattn_bo, L1_ffn_router_w, L1_ffn_expert_bias, L1_ffn_gate_w, L1_ffn_up_w, L1_ffn_down_w, L1_ffn_shared_gate_w, L1_ffn_shared_up_w, L1_ffn_shared_down_w):
    import jax
    import jax.numpy as jnp

    def _L0_xattn_ref(text_hidden, vision_tokens, vision_mask, Wq, Wk, Wv, Wo):
        import jax, jax.numpy as jnp
        import numpy as np
        N_HEADS = 16
        N_KV_HEADS = 8
        HEAD_DIM = 128
        D_TEXT = 256
        D_VISION = 128
        GROUPS = N_HEADS // N_KV_HEADS
        B, T_text, _ = text_hidden.shape
        T_vis = vision_tokens.shape[1]
        scale = jnp.float32(np.sqrt(HEAD_DIM))
        q = (text_hidden @ Wq).reshape(B, T_text, N_HEADS, HEAD_DIM).transpose(0, 2, 1, 3)
        k = (vision_tokens @ Wk).reshape(B, T_vis, N_KV_HEADS, HEAD_DIM).transpose(0, 2, 1, 3)
        v = (vision_tokens @ Wv).reshape(B, T_vis, N_KV_HEADS, HEAD_DIM).transpose(0, 2, 1, 3)
        k = jnp.repeat(k, GROUPS, axis=1)
        v = jnp.repeat(v, GROUPS, axis=1)
        scores = jnp.einsum('bhtd,bhsd->bhts', q, k) / scale
        mask = vision_mask[:, None, None, :]
        scores = jnp.where(mask, scores, -jnp.inf)
        attn = jax.nn.softmax(scores, axis=-1)
        attn = jnp.nan_to_num(attn, nan=0.0)
        out = jnp.einsum('bhts,bhsd->bhtd', attn, v)
        out = out.transpose(0, 2, 1, 3).reshape(B, T_text, N_HEADS * HEAD_DIM)
        return out @ Wo

    def _L0_ffn_ref(x, W1, W2, W3):
        import jax, jax.numpy as jnp
        import numpy as np
        B, S, D, H = (4, 256, 256, 1024)

        def fwht(x):
            orig_shape = x.shape
            n = orig_shape[-1]
            x = x.reshape(-1, n)
            h = 1
            while h < n:
                xb = x.reshape(-1, n // (2 * h), 2, h)
                a = xb[:, :, 0, :]
                b = xb[:, :, 1, :]
                x = jnp.stack([a + b, a - b], axis=2).reshape(-1, n)
                h *= 2
            scale = jnp.asarray(1.0 / np.sqrt(n), dtype=x.dtype)
            return (x * scale).reshape(orig_shape)
        up_gate = jnp.einsum('bsd,hd->bsh', x, W1)
        up_lin = jnp.einsum('bsd,hd->bsh', x, W3)
        hidden = jax.nn.silu(up_gate) * up_lin
        hidden = fwht(hidden)
        out = jnp.einsum('bsh,dh->bsd', hidden, W2)
        return out

    def _L1_xattn_ref(x, y, Wq, bq, Wk, bk, Wv, bv, Wkv_dca, bkv_dca, qn_w, qn_b, kn_w, kn_b, kn_dca_w, kn_dca_b, Wo, bo):
        import jax, jax.numpy as jnp
        import numpy as np
        B, S1, S2, DCA = (2, 256, 128, 16)
        QDIM, KDIM, H = (256, 128, 16)
        HD = QDIM // H
        SCALE = HD ** (-0.5)
        EPS = 1e-06
        DCA_WEIGHT = 1.0

        def _ln(t, w, b):
            m = jnp.mean(t, axis=-1, keepdims=True)
            v = jnp.var(t, axis=-1, keepdims=True)
            return (t - m) * jax.lax.rsqrt(v + EPS) * w + b

        def _attn(q, k, v):
            s = jnp.einsum('bhqd,bhkd->bhqk', q, k) * SCALE
            p = jax.nn.softmax(s, axis=-1)
            return jnp.einsum('bhqk,bhkd->bhqd', p, v)
        b, s1, _ = x.shape
        y_dca = y[:, -DCA:, :]
        y_main = y[:, :-DCA, :]
        kv_dca = (y_dca @ Wkv_dca + bkv_dca).reshape(b, DCA, 2, H, HD)
        k_dca = _ln(kv_dca[:, :, 0], kn_dca_w, kn_dca_b)
        v_dca = kv_dca[:, :, 1]
        s2 = y_main.shape[1]
        q = _ln((x @ Wq + bq).reshape(b, s1, H, HD), qn_w, qn_b)
        kv = jnp.concatenate([y_main @ Wk + bk, y_main @ Wv + bv], axis=-1)
        kv = kv.reshape(b, s2, H, 2 * HD)
        k = _ln(kv[..., :HD], kn_w, kn_b)
        v = kv[..., HD:]
        qT = q.transpose(0, 2, 1, 3)
        ctx = _attn(qT, k.transpose(0, 2, 1, 3), v.transpose(0, 2, 1, 3))
        ctx = ctx.transpose(0, 2, 1, 3).reshape(b, s1, QDIM)
        ctx_dca = _attn(qT, k_dca.transpose(0, 2, 1, 3), v_dca.transpose(0, 2, 1, 3))
        ctx_dca = ctx_dca.transpose(0, 2, 1, 3).reshape(b, s1, QDIM)
        ctx = ctx + DCA_WEIGHT * ctx_dca
        return ctx @ Wo + bo

    def _L1_ffn_ref(hidden, router_w, expert_bias, gate_w, up_w, down_w, shared_gate_w, shared_up_w, shared_down_w):
        import jax, jax.numpy as jnp
        import numpy as np
        B, S, D = (2, 256, 256)
        I = 128
        E = 32
        K = 4
        NS = 1
        ALPHA = 7.0

        def _clamped_swiglu(x, wg, wu, wd):
            g = jnp.clip(x @ wg.T, -ALPHA, ALPHA)
            u = jnp.clip(x @ wu.T, -ALPHA, ALPHA)
            return jax.nn.silu(g) * u @ wd.T
        Bb, Ss, Dd = hidden.shape
        flat = hidden.reshape(-1, Dd)
        T = flat.shape[0]
        logits = flat @ router_w.T
        scores = jnp.sqrt(jax.nn.softplus(logits))
        _, idx = jax.lax.top_k(scores + expert_bias, K)
        topv = jnp.take_along_axis(scores, idx, axis=1)
        topv = topv / (topv.sum(axis=-1, keepdims=True) + 1e-20)
        probs = jnp.zeros((T, E), flat.dtype).at[jnp.arange(T)[:, None], idx].set(topv)

        def body(acc, xs):
            wg, wu, wd, p = xs
            return (acc + p[:, None] * _clamped_swiglu(flat, wg, wu, wd), None)
        out, _ = jax.lax.scan(body, jnp.zeros_like(flat), (gate_w, up_w, down_w, probs.T))
        out = out + _clamped_swiglu(flat, shared_gate_w, shared_up_w, shared_down_w)
        return out.reshape(Bb, Ss, Dd)
    x = x + jnp.tanh(g_xattn[0]) * _L0_xattn_ref(_layernorm(x, axis=-1), ctx_1024, mask_BxS2_bf1, L0_xattn_Wq, L0_xattn_Wk, L0_xattn_Wv, L0_xattn_Wo)
    x = x + jnp.tanh(g_ffn[0]) * _L0_ffn_ref(_layernorm(x, axis=-1), L0_ffn_W1, L0_ffn_W2, L0_ffn_W3)
    x = x + jnp.tanh(g_xattn[1]) * _L1_xattn_ref(_layernorm(x, axis=-1), ctx_1024, L1_xattn_Wq, L1_xattn_bq, L1_xattn_Wk, L1_xattn_bk, L1_xattn_Wv, L1_xattn_bv, L1_xattn_Wkv_dca, L1_xattn_bkv_dca, L1_xattn_qn_w, L1_xattn_qn_b, L1_xattn_kn_w, L1_xattn_kn_b, L1_xattn_kn_dca_w, L1_xattn_kn_dca_b, L1_xattn_Wo, L1_xattn_bo)
    x = x + jnp.tanh(g_ffn[1]) * _L1_ffn_ref(_layernorm(x, axis=-1), L1_ffn_router_w, L1_ffn_expert_bias, L1_ffn_gate_w, L1_ffn_up_w, L1_ffn_down_w, L1_ffn_shared_gate_w, L1_ffn_shared_up_w, L1_ffn_shared_down_w)
    return x

_drawn_inputs = setup_inputs


def setup_inputs(seed=0):
    import zlib

    import numpy as np

    out = dict(_drawn_inputs(seed))
    spreads = {'g_ffn': (-1.0, 0.6),
     'L1_xattn_bq': (0.0, 0.8),
     'L1_xattn_bk': (0.0, 0.419),
     'L1_xattn_bv': (0.0, 0.451),
     'L1_xattn_bkv_dca': (0.0, 0.283),
     'L1_xattn_qn_w': (1.0, 0.6),
     'L1_xattn_qn_b': (0.0, 0.8),
     'L1_xattn_kn_w': (1.0, 0.6),
     'L1_xattn_kn_b': (0.0, 0.8),
     'L1_xattn_kn_dca_w': (1.0, 0.6),
     'L1_xattn_kn_dca_b': (0.0, 0.8),
     'L1_xattn_bo': (0.0, 0.1)}
    factors = {'L0_xattn_Wq': 8.0,
     'L0_xattn_Wk': 8.0,
     'L1_xattn_Wq': 3.064,
     'L1_ffn_router_w': 8.0,
     'L1_ffn_expert_bias': 8.0,
     'L1_ffn_gate_w': 8.0,
     'L1_ffn_up_w': 8.0,
     'L1_ffn_down_w': 8.0,
     'L1_ffn_shared_gate_w': 6.855,
     'L1_ffn_shared_up_w': 6.747,
     'L1_ffn_shared_down_w': 6.806}
    for name, (base, spread) in spreads.items():
        noise = np.random.default_rng([zlib.crc32(name.encode()), seed]).standard_normal(out[name].shape)
        drawn = base * np.exp(spread * noise) if base else spread * noise
        out[name] = jnp.asarray(drawn.astype(out[name].dtype))
    for name, factor in factors.items():
        out[name] = (out[name] * factor).astype(out[name].dtype)
    return out
```

```python
from contextlib import ExitStack

import concourse.bass as bass
from concourse import mybir

F32 = mybir.dt.float32
F32R = mybir.dt.float32r
BF16 = mybir.dt.bfloat16
I32 = mybir.dt.int32
U8 = mybir.dt.uint8
ALU = mybir.AluOpType
ACT = mybir.ActivationFunctionType
AX = mybir.AxisListType

B, S, D = 16, 56, 256
SK, DC = 1500, 128
H0, G0, HD0 = 16, 2, 128
H1, HD1, DCA = 16, 16, 16
FF = 1024
E, I, TOPK = 32, 128, 4
ALPHA = 7.0
NT = B * S
TT = 2 * S
NTILE = NT // TT
CH = D // 128
KT, NKT = 125, SK // 125
CK, NCH = 500, SK // 500
HALF = 448
BIG = 3.0e38
EPS_LN, EPS_HEAD = 1e-5, 1e-6


def wait(eng, sem, value):
    if isinstance(value, int) and value <= 0:
        return
    eng.wait_ge(sem, value)


def upper_part(pool, out, x, ones):
    return pool.tensor_tensor(out, x, ones[0:x.shape[0], 0:1].broadcast_to(x.shape), ALU.mult)


class Chain:

    def __init__(self, eng, sem, base=0):
        self.eng, self.sem, self.base, self.n = eng, sem, base, 0

    def done(self, ins):
        ins.then_inc(self.sem, 1)
        self.n += 1

    def settle(self):
        wait(self.eng, self.sem, self.base + self.n)

    def link(self, ins):
        self.done(ins)
        self.settle()


def rsqrt(ch, y, v, half_v, t):
    dve = ch.eng
    ch.done(dve.tensor_scalar(half_v, v, -0.5, None, ALU.mult))
    ch.link(dve.tensor_scalar(y.bitcast(I32), v.bitcast(I32), 1, None, ALU.logical_shift_right))
    ch.link(dve.tensor_scalar(y.bitcast(I32), y.bitcast(I32), -1.0, float(0x5F3759DF), ALU.mult, ALU.add))
    for _ in range(3):
        ch.link(dve.tensor_tensor(t, y, y, ALU.mult))
        ch.link(dve.tensor_tensor(t, t, half_v, ALU.mult))
        ch.link(dve.scalar_tensor_tensor(y, t, 1.5, y, ALU.add, ALU.mult))


def layer_norm(ch, xn, x, stats, mv, rs, tmp1, tmp2, rows, ready):
    dve = ch.eng
    tiles = x.shape[1]
    for t in range(tiles):
        ch.done(dve.bn_stats(stats[0:rows, t, :], x[:, t, :]))
    ch.settle()
    for t in range(tiles):
        ch.done(dve.bn_aggr(mv[0:rows, t, :], stats[0:rows, t, :]))
    ch.settle()
    ch.link(dve.tensor_scalar(rs[0:rows, :], mv[0:rows, :, 1], EPS_LN, None, ALU.add))
    rsqrt(ch, mv[0:rows, :, 1], rs[0:rows, :], tmp1[0:rows, :], tmp2[0:rows, :])
    for t in range(tiles):
        dve.tensor_scalar(xn[:, t, :], x[:, t, :], mv[0:rows, t, 0:1], mv[0:rows, t, 1:2],
                          ALU.subtract, ALU.mult).then_inc(ready, 1)


class Scope:

    def __init__(self, nc, ctx, tag):
        self.nc, self.ctx, self.tag = nc, ctx, tag

    def sb(self, name, shape, dt=F32):
        return self.ctx.enter_context(self.nc.sbuf_tensor(f"{self.tag}_{name}", shape, dt))

    def ps(self, name, shape, dt=F32):
        return self.ctx.enter_context(self.nc.psum_tensor(f"{self.tag}_{name}", shape, dt))

    def sem(self, name):
        return self.ctx.enter_context(self.nc.semaphore(f"{self.tag}_{name}"))


def ln_scratch(sc):
    return (sc.sb("ln_stats", [TT, NTILE, 6]), sc.sb("ln_mv", [TT, NTILE, 2]), sc.sb("ln_rs", [TT, NTILE]),
            sc.sb("ln_t1", [TT, NTILE]), sc.sb("ln_t2", [TT, NTILE]))


def project_queries(nc, x_in, wqT, wkT, ident_in, q_hi_d, q_lo_d):
    with ExitStack() as ctx:
        sc = Scope(nc, ctx, "pq")
        ident = sc.sb("ident", [128, 128])
        wqT_sb = sc.sb("wqT", [128, H0, D])
        wkT_sb = sc.sb("wkT", [128, H0 // G0, DC])
        wqk = sc.sb("wqk", [128, CH, H0, DC])
        x = sc.sb("x", [TT, NTILE, D])
        xn = sc.sb("xn", [TT, NTILE, D])
        xnT = sc.sb("xnT", [128, CH, NT])
        q_hi = sc.sb("q_hi", [128, B, H0, S], F32R)
        q_lo = sc.sb("q_lo", [128, B, H0, S], F32R)
        scratch = ln_scratch(sc)
        fold_ps = [sc.ps(f"fold{k}", [128, 512]) for k in range(2)]
        tr_ps = [sc.ps(f"tr{k}", [128, 512]) for k in range(2)]
        q_ps = [sc.ps(f"q{k}", [128, 512]) for k in range(4)]
        x_loaded, wq_loaded, wk_loaded, id_loaded = (sc.sem(n) for n in ("x_ld", "wq_ld", "wk_ld", "id_ld"))
        dve_steps, xn_ready = sc.sem("dve_steps"), sc.sem("xn_ready")
        folded, fold_kept = sc.sem("folded"), sc.sem("fold_kept")
        turned, turn_kept = sc.sem("turned"), sc.sem("turn_kept")
        q_made, q_hi_kept, q_kept, q_stored = (sc.sem(n) for n in ("q_made", "q_hi_kept", "q_kept", "q_stored"))
        NFOLD = H0 // 2
        FILLS = 2 * CH
        block = ctx.enter_context(nc.Block())

        @block.sync
        def _(sp):
            sp.dma_start(x[:, :, :], x_in.rearrange("(n p) d -> p n d", p=TT)).then_inc(x_loaded, 16)
            sp.dma_start(wkT_sb[:, :, :], wkT.rearrange("(h p) c -> p h c", p=HD0)).then_inc(wk_loaded, 16)
            sp.dma_start(wqT_sb[:, :, :], wqT.rearrange("(h p) d -> p h d", p=HD0)).then_inc(wq_loaded, 16)
            sp.dma_start(ident[:, :], ident_in).then_inc(id_loaded, 16)
            for half in range(2):
                sp.wait_ge(q_kept, H0 * (half + 1))
                bs = slice(half * B // 2, (half + 1) * B // 2)
                sp.dma_start(q_hi_d[:, bs], q_hi[:, bs].bitcast(F32)).then_inc(q_stored, 16)
                sp.dma_start(q_lo_d[:, bs], q_lo[:, bs].bitcast(F32)).then_inc(q_stored, 16)
            sp.wait_ge(q_stored, 64)

        @block.tensor
        def _(pe):
            pe.wait_ge(wk_loaded, 16)
            pe.wait_ge(wq_loaded, 16)
            for n in range(NFOLD):
                if n >= 2:
                    pe.wait_ge(fold_kept, n - 1)
                for k in range(2):
                    h = 2 * n + k
                    for c in range(CH):
                        mm = pe.matmul(fold_ps[n % 2][:, (k * CH + c) * 128:(k * CH + c + 1) * 128],
                                       wqT_sb[:, h, c * 128:(c + 1) * 128], wkT_sb[:, h // G0, :],
                                       start=True, stop=True)
                mm.then_inc(folded, 1)
            pe.wait_ge(id_loaded, 16)
            for f in range(FILLS):
                if f >= 2:
                    pe.wait_ge(turn_kept, f - 1)
                half, c = f // CH, f % CH
                pe.wait_ge(xn_ready, 4 * (half + 1))
                for k in range(4):
                    mm = pe.transpose(tr_ps[f % 2][:, k * TT:(k + 1) * TT],
                                      xn[:, 4 * half + k, c * 128:(c + 1) * 128], ident[0:TT, 0:TT])
                mm.then_inc(turned, 1)
            pe.wait_ge(fold_kept, NFOLD)
            for half in range(2):
                pe.wait_ge(turn_kept, CH * (half + 1))
                for h in range(H0):
                    n = half * H0 + h
                    if n >= 4:
                        pe.wait_ge(q_kept, n - 3)
                    for c in range(CH):
                        mm = pe.matmul(q_ps[n % 4][:, 0:HALF], wqk[:, c, h, :],
                                       xnT[:, c, half * HALF:(half + 1) * HALF], start=(c == 0), stop=(c == CH - 1))
                    mm.then_inc(q_made, 1)

        @block.scalar
        def _(act):
            for n in range(NFOLD):
                act.wait_ge(folded, n + 1)
                act.copy(wqk[:, :, 2 * n:2 * n + 2, :].rearrange("p c k n -> p k c n"),
                         fold_ps[n % 2][:, :].rearrange("p (k c n) -> p k c n", k=2, c=CH)).then_inc(fold_kept, 1)
            for f in range(FILLS):
                act.wait_ge(turned, f + 1)
                half, c = f // CH, f % CH
                act.copy(xnT[:, c, half * HALF:(half + 1) * HALF], tr_ps[f % 2][:, 0:HALF]).then_inc(turn_kept, 1)
            for n in range(2 * H0):
                half, h = n // H0, n % H0
                act.wait_ge(q_made, n + 1)
                act.copy(q_hi[:, half * B // 2:(half + 1) * B // 2, h, :],
                         q_ps[n % 4][:, 0:HALF].rearrange("p (b t) -> p b t", t=S)).then_inc(q_hi_kept, 1)

        @block.vector
        def _(dve):
            ch = Chain(dve, dve_steps)
            dve.wait_ge(x_loaded, 16)
            layer_norm(ch, xn[:, :, :], x[:, :, :], *scratch, TT, xn_ready)
            for n in range(2 * H0):
                half, h = n // H0, n % H0
                bs = slice(half * B // 2, (half + 1) * B // 2)
                dve.wait_ge(q_hi_kept, n + 1)
                dve.tensor_tensor(q_lo[:, bs, h, :], q_ps[n % 4][:, 0:HALF].rearrange("p (b t) -> p b t", t=S),
                                  q_hi[:, bs, h, :].bitcast(F32), ALU.subtract).then_inc(q_kept, 1)


def three_passes(pe, out, w_hi, w_lo, m_hi, m_lo, first, last):
    pe.matmul(out, w_hi, m_hi, start=first, stop=False)
    pe.matmul(out, w_hi, m_lo, start=False, stop=False)
    return pe.matmul(out, w_lo, m_hi, start=False, stop=last)


UNIT = 4


def attend_context(nc, ctx_in, ctxT_in, mask_in, ident_in, q_hi_d, q_lo_d, o_d):
    SCALE = float(HD0) ** -0.5
    NS = 4
    STEPS = 2 * 2 * UNIT
    with ExitStack() as ctx:
        sc = Scope(nc, ctx, "a0")
        ident = sc.sb("ident", [128, 128])
        ones = sc.sb("ones", [128, 128])
        raw = sc.sb("raw", [KT, NKT, DC])
        rawT = sc.sb("rawT", [DC, SK])
        c_hi = [sc.sb(f"c_hi{p}", [KT, NKT, DC], F32R) for p in range(2)]
        c_lo = [sc.sb(f"c_lo{p}", [KT, NKT, DC], F32R) for p in range(2)]
        cT_hi = [sc.sb(f"cT_hi{p}", [DC, SK], F32R) for p in range(2)]
        cT_lo = [sc.sb(f"cT_lo{p}", [DC, SK], F32R) for p in range(2)]
        q_hi = [sc.sb(f"q_hi{p}", [DC, H0 * S], F32R) for p in range(2)]
        q_lo = [sc.sb(f"q_lo{p}", [DC, H0 * S], F32R) for p in range(2)]
        mask_u8 = sc.sb("mask_u8", [TT, SK], U8)
        mask_add = [sc.sb(f"mask_add{p}", [TT, SK]) for p in range(2)]
        any_key = sc.sb("any_key", [TT, 2])
        probs = [sc.sb(f"probs{p}", [TT, SK]) for p in range(2)]
        pT_hi = [sc.sb(f"pT_hi{p}", [KT, NKT, HALF], F32R) for p in range(2)]
        pT_lo = [sc.sb(f"pT_lo{p}", [KT, NKT, HALF], F32R) for p in range(2)]
        part_min = sc.sb("part_min", [TT, 2, NCH])
        row_min = sc.sb("row_min", [TT, 2])
        carrier = sc.sb("carrier", [1, 2, NCH])
        sums = sc.sb("sums", [TT, 2, UNIT])
        inv = sc.sb("inv", [TT, UNIT])
        inv_diag = sc.sb("inv_diag", [TT, UNIT, TT])
        inv_all = sc.sb("inv_all", [128, HALF])
        o_sb = sc.sb("o", [DC, HALF])
        s_ps = [sc.ps(f"s{k}", [128, 512]) for k in range(NS)]
        t_ps = [sc.ps(f"t{k}", [128, 512]) for k in range(2)]
        o_ps = sc.ps("o_ps", [128, 512])
        i_ps = sc.ps("i_ps", [128, 512])

        id_loaded, ones_set = sc.sem("id_ld"), sc.sem("ones")
        ctx_loaded, mask_loaded = sc.sem("ctx_ld"), sc.sem("mask_ld")
        q_loaded = [sc.sem(f"q_ld{p}") for p in range(2)]
        pool_steps = sc.sem("pool_steps")
        scored, score_kept = sc.sem("scored"), sc.sem("score_kept")
        row_max, dve_steps = sc.sem("row_max"), sc.sem("dve_steps")
        probs_made = sc.sem("probs_made")
        turned, turn_hi, turn_kept = sc.sem("turned"), sc.sem("turn_hi"), sc.sem("turn_kept")
        diag_made, inv_spread, inv_kept = sc.sem("diag_made"), sc.sem("inv_spread"), sc.sem("inv_kept")
        summed, o_kept, o_stored = sc.sem("summed"), sc.sem("o_kept"), sc.sem("o_stored")
        POOL_B = 5
        block = ctx.enter_context(nc.Block())

        def bodies(eng, body, last):
            body(0, True)
            with eng.Fori(1, B // 2) as i:
                body(i, False)
            last()

        @block.sync
        def _(sp):
            sp.dma_start(ident[:, :], ident_in).then_inc(id_loaded, 16)

            def load(i, p):
                b = 2 * i + p
                wait(sp, pool_steps, POOL_B * b)
                sp.dma_start(rawT[:, :], ctxT_in[bass.ds(b, 1)].rearrange("b c k -> c (b k)")).then_inc(ctx_loaded, 16)
                sp.dma_start(raw[:, :, :], ctx_in[bass.ds(b, 1)].rearrange("b (n p) c -> p (b n) c", p=KT)
                             ).then_inc(ctx_loaded, 16)
                sp.dma_start(mask_u8[:, :], mask_in[bass.ds(b, 1)].rearrange("b k -> (b k)").partition_broadcast(TT)
                             ).then_inc(mask_loaded, 16)
                wait(sp, scored, 8 * NCH * (b - 1))
                sp.dma_start(q_hi[p][:, :].bitcast(F32), q_hi_d[:, bass.ds(b, 1)].rearrange("c b h t -> c (b h t)")
                             ).then_inc(q_loaded[p], 16)
                sp.dma_start(q_lo[p][:, :].bitcast(F32), q_lo_d[:, bass.ds(b, 1)].rearrange("c b h t -> c (b h t)")
                             ).then_inc(q_loaded[p], 16)

            def body(i, first):
                for p in range(2):
                    load(i, p)

            bodies(sp, body, lambda: None)

        @block.gpsimd
        def _(pool):
            pool.memset(ones[:, :], 1.0).then_inc(ones_set, 1)
            pool.wait_ge(ones_set, 1)

            def split(i, p):
                b = 2 * i + p
                done = POOL_B * b
                pool.wait_ge(ctx_loaded, 32 * (b + 1))
                pool.wait_ge(mask_loaded, 16 * (b + 1))
                wait(pool, scored, 8 * NCH * (b - 1))
                wait(pool, score_kept, 8 * NCH * (b - 1))
                upper_part(pool, cT_hi[p][:, :], rawT[:, :], ones).then_inc(pool_steps, 1)
                pool.tensor_scalar(mask_add[p][:, :], mask_u8[:, :], 1.0, BIG, ALU.subtract, ALU.mult
                                   ).then_inc(pool_steps, 1)
                pool.wait_ge(pool_steps, done + 1)
                pool.tensor_tensor(cT_lo[p][:, :], rawT[:, :], cT_hi[p][:, :].bitcast(F32), ALU.subtract
                                   ).then_inc(pool_steps, 1)
                wait(pool, summed, 2 * (b - 1))
                upper_part(pool, c_hi[p][:, :, :].rearrange("p n c -> p (n c)"),
                           raw[:, :, :].rearrange("p n c -> p (n c)"), ones).then_inc(pool_steps, 1)
                pool.wait_ge(pool_steps, done + 4)
                pool.tensor_tensor(c_lo[p][:, :, :], raw[:, :, :], c_hi[p][:, :, :].bitcast(F32), ALU.subtract
                                   ).then_inc(pool_steps, 1)

            def body(i, first):
                for p in range(2):
                    split(i, p)

            bodies(pool, body, lambda: None)

        @block.tensor
        def _(pe):
            pe.wait_ge(id_loaded, 16)
            pe.wait_ge(ones_set, 1)

            def scores(g, s):
                p, r = s // (2 * UNIT), s % (2 * UNIT)
                rows = slice(r * TT, (r + 1) * TT)
                for c in range(NCH):
                    n = NCH * g + c
                    slot = (NCH * s + c) % NS
                    wait(pe, score_kept, n - NS + 1)
                    keys = slice(c * CK, (c + 1) * CK)
                    three_passes(pe, s_ps[slot][0:TT, 0:CK], q_hi[p][:, rows], q_lo[p][:, rows],
                                 cT_hi[p][:, keys], cT_lo[p][:, keys], True, True).then_inc(scored, 1)

            def turn(g, s):
                pe.wait_ge(probs_made, g + 1)
                for f in range(NCH):
                    n = NCH * g + f
                    wait(pe, turn_kept, n - 1)
                    for k in range(4):
                        j = 4 * f + k
                        mm = pe.transpose(t_ps[(NCH * s + f) % 2][0:KT, k * TT:(k + 1) * TT],
                                          probs[s % 2][:, j * KT:(j + 1) * KT], ident[0:TT, 0:TT])
                    mm.then_inc(turned, 1)

            def weigh(u, s):
                p, half = s // (2 * UNIT), (s // UNIT) % 2
                pe.wait_ge(diag_made, u + 1)
                wait(pe, inv_kept, u)
                pe.matmul(i_ps[:, 0:HALF], ones[0:TT, :], inv_diag[:, :, :].rearrange("p k t -> p (k t)"),
                          start=True, stop=True).then_inc(inv_spread, 1)
                wait(pe, o_kept, u)
                for j in range(NKT):
                    if j % 4 == 0:
                        pe.wait_ge(turn_kept, NCH * UNIT * u + NCH * (UNIT - 1) + j // 4 + 1)
                    mm = three_passes(pe, o_ps[:, 0:HALF], c_hi[p][:, j, :], c_lo[p][:, j, :],
                                      pT_hi[half][:, j, :], pT_lo[half][:, j, :], j == 0, j == NKT - 1)
                mm.then_inc(summed, 1)

            def body(i, first):
                for s in range(STEPS):
                    g = STEPS * i + s
                    if s % (2 * UNIT) == 0:
                        p = s // (2 * UNIT)
                        b = 2 * i + p
                        pe.wait_ge(pool_steps, POOL_B * (b + 1))
                        pe.wait_ge(q_loaded[p], 32 * (i + 1))
                    scores(g, s)
                    if not (first and s == 0):
                        turn(g - 1, (s - 1) % STEPS)
                    if s % UNIT == 0 and not (first and s == 0):
                        weigh(STEPS // UNIT * i + s // UNIT - 1, (s - 1) % STEPS)

            def last():
                turn(8 * B - 1, STEPS - 1)
                weigh(2 * B - 1, STEPS - 1)

            bodies(pe, body, last)

        @block.scalar
        def _(act):
            def upper(g, s, u):
                half, r = (s // UNIT) % 2, s % UNIT
                for f in range(NCH):
                    act.wait_ge(turned, NCH * g + f + 1)
                    if f == 0 and r == 0:
                        wait(act, summed, u - 1)
                    act.copy(pT_hi[half][:, 4 * f:4 * f + 4, r * TT:(r + 1) * TT],
                             t_ps[(NCH * s + f) % 2][0:KT, 0:HALF].rearrange("p (k t) -> p k t", t=TT)
                             ).then_inc(turn_hi, 1)

            def spread(u):
                act.wait_ge(inv_spread, u + 1)
                wait(act, o_kept, u)
                act.copy(inv_all[:, :], i_ps[:, 0:HALF]).then_inc(inv_kept, 1)

            def store(u, b, half):
                act.wait_ge(o_kept, u + 1)
                act.dma_start(o_d[:, half * 8:half * 8 + 8, bass.ds(b * S, S)],
                              o_sb[:, :].rearrange("c (h t) -> c h t", t=S)).then_inc(o_stored, 16)

            def body(i, first):
                for s in range(STEPS):
                    g = STEPS * i + s
                    if not (first and s == 0):
                        upper(g - 1, (s - 1) % STEPS, STEPS // UNIT * i + (s - 1) // UNIT)
                    if s % UNIT == 2 and not (first and s == 2):
                        v = s // UNIT - 1
                        store(STEPS // UNIT * i + v, 2 * i + v // 2, v % 2)
                    act.wait_ge(row_max, g + 1)
                    act.activation(probs[s % 2][:, :], probs[s % 2][:, :], ACT.Exp, scale=-1.0,
                                   bias=row_min[:, s % 2:s % 2 + 1],
                                   accum_out=sums[:, (s // UNIT) % 2, s % UNIT:s % UNIT + 1]
                                   ).then_inc(probs_made, 1)
                    if s % UNIT == 0 and not (first and s == 0):
                        spread(STEPS // UNIT * i + s // UNIT - 1)

            def last():
                upper(8 * B - 1, STEPS - 1, 2 * B - 1)
                spread(2 * B - 1)
                store(2 * B - 1, B - 1, 1)
                act.wait_ge(o_stored, 16 * 2 * B)

            bodies(act, body, last)

        @block.vector
        def _(dve):
            BATCH_N, UNIT_N = 2, 2
            PER_BODY = 2 * BATCH_N + (STEPS // UNIT) * UNIT_N

            def masked(g, s, i, ch):
                p = s // (2 * UNIT)
                wait(dve, turned, NCH * (g - 1))
                for c in range(NCH):
                    keys = slice(c * CK, (c + 1) * CK)
                    dve.wait_ge(scored, NCH * g + c + 1)
                    dve.memset(carrier[:, s % 2, c:c + 1], 0.0)
                    ins = dve.tensor_tensor_reduce(
                        probs[s % 2][:, keys], s_ps[(NCH * s + c) % NS][0:TT, 0:CK], mask_add[p][:, keys],
                        -SCALE, BIG, ALU.add, ALU.min, part_min[:, s % 2, c:c + 1])
                    ins.then_inc(score_kept, 1)
                dve.wait_ge(score_kept, NCH * g + NCH)
                dve.tensor_reduce(row_min[:, s % 2:s % 2 + 1], part_min[:, s % 2, :], AX.X, ALU.min
                                  ).then_inc(row_max, 1)

            def rest(g, s):
                half, r = (s // UNIT) % 2, s % UNIT
                for f in range(NCH):
                    dve.wait_ge(turn_hi, NCH * g + f + 1)
                    rows = slice(r * TT, (r + 1) * TT)
                    dve.tensor_tensor(pT_lo[half][:, 4 * f:4 * f + 4, rows],
                                      t_ps[(NCH * s + f) % 2][0:KT, 0:HALF].rearrange("p (k t) -> p k t", t=TT),
                                      pT_hi[half][:, 4 * f:4 * f + 4, rows].bitcast(F32), ALU.subtract
                                      ).then_inc(turn_kept, 1)

            def invert(u, s, ch):
                p, half = s // (2 * UNIT), (s // UNIT) % 2
                ch.link(dve.reciprocal(inv[:, :], sums[:, half, :]))
                ch.link(dve.tensor_scalar(inv[:, :], inv[:, :], any_key[:, p:p + 1], None, ALU.mult))
                wait(dve, inv_spread, u)
                dve.tensor_tensor(inv_diag[:, :, :],
                                  ident[0:TT, 0:TT].rearrange("p (a t) -> p a t", a=1).broadcast_to([TT, UNIT, TT]),
                                  inv[:, :].rearrange("p (k a) -> p k a", a=1).broadcast_to([TT, UNIT, TT]),
                                  ALU.mult).then_inc(diag_made, 1)

            def finish(u):
                dve.wait_ge(summed, u + 1)
                dve.wait_ge(inv_kept, u + 1)
                wait(dve, o_stored, 16 * u)
                dve.tensor_tensor(o_sb[:, :], o_ps[:, 0:HALF], inv_all[:, :], ALU.mult).then_inc(o_kept, 1)

            def body(i, first):
                base = PER_BODY * i - (0 if first else UNIT_N)
                ch = Chain(dve, dve_steps, base)
                for s in range(STEPS):
                    g = STEPS * i + s
                    if s % (2 * UNIT) == 0:
                        p = s // (2 * UNIT)
                        b = 2 * i + p
                        dve.wait_ge(pool_steps, POOL_B * (b + 1))
                    masked(g, s, i, ch)
                    if s % (2 * UNIT) == 1:
                        p = s // (2 * UNIT)
                        ch.link(dve.tensor_reduce(any_key[:, p:p + 1], mask_add[p][:, :], AX.X, ALU.max))
                        ch.link(dve.tensor_scalar(any_key[:, p:p + 1], any_key[:, p:p + 1], 0.0, None, ALU.is_ge))
                    if s % UNIT == 0 and not (first and s == 0):
                        u = STEPS // UNIT * i + s // UNIT - 1
                        dve.wait_ge(probs_made, g)
                        invert(u, (s - 1) % STEPS, ch)
                    if s % UNIT == 1 and not (first and s == 1):
                        finish(STEPS // UNIT * i + s // UNIT - 1)
                    if not (first and s == 0):
                        rest(g - 1, (s - 1) % STEPS)

            def last():
                ch = Chain(dve, dve_steps, PER_BODY * (B // 2) - UNIT_N)
                dve.wait_ge(probs_made, 8 * B)
                invert(2 * B - 1, STEPS - 1, ch)
                rest(8 * B - 1, STEPS - 1)
                finish(2 * B - 1)

            bodies(dve, body, last)


def close_attention(nc, o_d, x_in, wvT, wo, gates_in, xs, gate):
    with ExitStack() as ctx:
        sc = Scope(nc, ctx, "c0")
        wvT_sb = sc.sb("wvT", [128, H0 // G0, DC])
        wo_sb = sc.sb("wo", [128, H0, D])
        wvo = sc.sb("wvo", [DC, H0, D])
        oT = sc.sb("oT", [DC, H0, NT])
        x = sc.sb("x", [TT, NTILE, D])
        gates = sc.sb("gates", [TT, 4])
        f_ps = [sc.ps(f"f{k}", [128, 512]) for k in range(4)]
        y_ps = [sc.ps(f"y{k}", [128, 512]) for k in range(4)]
        w_loaded, x_loaded, g_loaded = sc.sem("w_ld"), sc.sem("x_ld"), sc.sem("g_ld")
        o_loaded = [sc.sem(f"o_ld{k}") for k in range(4)]
        folded, fold_kept, gate_made = sc.sem("folded"), sc.sem("fold_kept"), sc.sem("gate_made")
        projected, added = sc.sem("projected"), sc.sem("added")
        block = ctx.enter_context(nc.Block())

        @block.sync
        def _(sp):
            sp.dma_start(wvT_sb[:, :, :], wvT.rearrange("(g p) c -> p g c", p=HD0)).then_inc(w_loaded, 16)
            sp.dma_start(wo_sb[:, :, :], wo.rearrange("(h p) d -> p h d", p=HD0)).then_inc(w_loaded, 16)
            for k in range(4):
                cols = slice(2 * k * TT, 2 * (k + 1) * TT)
                sp.dma_start(oT[:, :, cols], o_d[:, :, cols]).then_inc(o_loaded[k], 16)
            sp.dma_start(x[:, :, :], x_in.rearrange("(n p) d -> p n d", p=TT)).then_inc(x_loaded, 16)
            sp.dma_start(gates[:, :], gates_in.partition_broadcast(TT)).then_inc(g_loaded, 16)

        @block.tensor
        def _(pe):
            pe.wait_ge(w_loaded, 32)
            for n in range(H0 // 2):
                if n >= 4:
                    pe.wait_ge(fold_kept, n - 3)
                for k in range(2):
                    h = 2 * n + k
                    mm = pe.matmul(f_ps[n % 4][:, k * D:(k + 1) * D], wvT_sb[:, h // G0, :], wo_sb[:, h, :],
                                   start=True, stop=True)
                mm.then_inc(folded, 1)
            pe.wait_ge(fold_kept, H0 // 2)
            for t in range(NTILE):
                pe.wait_ge(o_loaded[t // 2], 16)
                if t >= 4:
                    pe.wait_ge(added, t - 3)
                for h in range(H0):
                    mm = pe.matmul(y_ps[t % 4][0:TT, 0:D], oT[:, h, t * TT:(t + 1) * TT], wvo[:, h, :],
                                   start=(h == 0), stop=(h == H0 - 1))
                mm.then_inc(projected, 1)

        @block.scalar
        def _(act):
            act.wait_ge(g_loaded, 16)
            act.activation(gate[:, :], gates[:, :], ACT.Tanh).then_inc(gate_made, 1)
            for n in range(H0 // 2):
                act.wait_ge(folded, n + 1)
                act.copy(wvo[:, 2 * n:2 * n + 2, :], f_ps[n % 4][:, :].rearrange("p (k d) -> p k d", k=2)
                         ).then_inc(fold_kept, 1)

        @block.vector
        def _(dve):
            dve.wait_ge(gate_made, 1)
            dve.wait_ge(x_loaded, 16)
            for t in range(NTILE):
                dve.wait_ge(projected, t + 1)
                dve.scalar_tensor_tensor(xs[:, t, :], y_ps[t % 4][0:TT, 0:D], gate[:, 0:1], x[:, t, :],
                                         ALU.mult, ALU.add).then_inc(added, 1)


def turn_tokens(pe, act, xn, xnT, banks, ident, ready, turned, kept):
    if pe is not None:
        for f in range(2 * CH):
            half, c = f // CH, f % CH
            pe.wait_ge(ready, 4 * (half + 1))
            if f >= 2:
                pe.wait_ge(kept, f - 1)
            for k in range(4):
                mm = pe.transpose(banks[f % 2][:, k * TT:(k + 1) * TT], xn[:, 4 * half + k, c * 128:(c + 1) * 128],
                                  ident[0:TT, 0:TT])
            mm.then_inc(turned, 1)
    if act is not None:
        for f in range(2 * CH):
            half, c = f // CH, f % CH
            act.wait_ge(turned, f + 1)
            act.copy(xnT[:, c, half * HALF:(half + 1) * HALF], banks[f % 2][:, 0:HALF]).then_inc(kept, 1)


def feed_forward(nc, w1T, w3T, w2T, hadamard_in, ident_in, xs, gate):
    NH = FF // 128
    with ExitStack() as ctx:
        sc = Scope(nc, ctx, "ff")
        ident = sc.sb("ident", [128, 128])
        had = sc.sb("had", [128, 128])
        w1 = sc.sb("w1", [128, CH, FF])
        w3 = sc.sb("w3", [128, CH, FF])
        w2 = sc.sb("w2", [128, NH, D])
        fly = [sc.sb(f"fly{k}", [128, NH, D]) for k in range(2)]
        xn = sc.sb("xn", [TT, NTILE, D])
        xnT = sc.sb("xnT", [128, CH, NT])
        act_g = [sc.sb(f"act_g{k}", [128, HALF]) for k in range(2)]
        hidden = sc.sb("hidden", [128, NH, NT])
        scratch = ln_scratch(sc)
        banks = [sc.ps(f"b{k}", [128, 512]) for k in range(8)]
        in_loaded, w2_loaded, id_loaded, w_loaded = (sc.sem(n) for n in ("in_ld", "w2_ld", "id_ld", "w_ld"))
        dve_steps, xn_ready = sc.sem("dve_steps"), sc.sem("xn_ready")
        mixed, mix_kept = sc.sem("mixed"), sc.sem("mix_kept")
        turned, turn_kept = sc.sem("turned"), sc.sem("turn_kept")
        gate_up, silu_made, hidden_made = sc.sem("gate_up"), sc.sem("silu_made"), sc.sem("hidden_made")
        w2_ready = sc.sem("w2_ready")
        projected, added = sc.sem("projected"), sc.sem("added")
        block = ctx.enter_context(nc.Block())

        @block.sync
        def _(sp):
            sp.dma_start(ident[:, :], ident_in).then_inc(id_loaded, 16)
            sp.dma_start(had[:, :], hadamard_in).then_inc(w2_loaded, 16)
            sp.dma_start(w2[:, :, :], w2T.rearrange("(k p) d -> p k d", p=128)).then_inc(w2_loaded, 16)
            sp.dma_start(w1[:, :, :], w1T.rearrange("(c p) h -> p c h", p=128)).then_inc(w_loaded, 16)
            sp.dma_start(w3[:, :, :], w3T.rearrange("(c p) h -> p c h", p=128)).then_inc(w_loaded, 16)

        @block.tensor
        def _(pe):
            pe.wait_ge(id_loaded, 16)
            pe.wait_ge(w2_loaded, 32)
            for k in range(NH // 2):
                for c in range(2):
                    mm = pe.matmul(banks[4 + k][:, c * D:(c + 1) * D], had[:, :], w2[:, 2 * k + c, :],
                                   start=True, stop=True)
                mm.then_inc(mixed, 1)
            turn_tokens(pe, None, xn, xnT, banks[0:2], ident, xn_ready, turned, turn_kept)
            pe.wait_ge(w_loaded, 32)
            pe.wait_ge(turn_kept, 2 * CH)
            pe.wait_ge(mix_kept, NH // 2)
            for n in range(2 * NH):
                half, k = n // NH, n % NH
                if n >= 4:
                    pe.wait_ge(hidden_made, n - 3)
                for w, bank in ((w1, banks[n % 4]), (w3, banks[4 + n % 4])):
                    for c in range(CH):
                        mm = pe.matmul(bank[:, 0:HALF], w[:, c, k * 128:(k + 1) * 128],
                                       xnT[:, c, half * HALF:(half + 1) * HALF], start=(c == 0), stop=(c == CH - 1))
                mm.then_inc(gate_up, 1)
            pe.wait_ge(w2_ready, 1)
            for t in range(NTILE):
                pe.wait_ge(hidden_made, NH * (t // 4 + 1) if t >= 4 else 2 * NH)
                if t >= 4:
                    pe.wait_ge(added, t - 3)
                for k in range(NH):
                    mm = pe.matmul(banks[t % 4][0:TT, 0:D], hidden[:, k, t * TT:(t + 1) * TT], fly[1][:, k, :],
                                   start=(k == 0), stop=(k == NH - 1))
                mm.then_inc(projected, 1)

        @block.scalar
        def _(act):
            for k in range(NH // 2):
                act.wait_ge(mixed, k + 1)
                act.mul(fly[0][:, 2 * k:2 * k + 2, :], banks[4 + k][:, :].rearrange("p (c d) -> p c d", c=2),
                        float(FF) ** -0.5).then_inc(mix_kept, 1)
            turn_tokens(None, act, xn, xnT, banks[0:2], ident, xn_ready, turned, turn_kept)
            for n in range(2 * NH):
                act.wait_ge(gate_up, n + 1)
                if n >= 2:
                    act.wait_ge(hidden_made, n - 1)
                act.activation(act_g[n % 2][:, :], banks[n % 4][:, 0:HALF], ACT.Silu).then_inc(silu_made, 1)

        @block.vector
        def _(dve):
            ch = Chain(dve, dve_steps)
            layer_norm(ch, xn[:, :, :], xs[:, :, :], *scratch, TT, xn_ready)
            dve.wait_ge(mix_kept, NH // 2)
            src, dst = 0, 1
            for st in range(3):
                w = 1 << st
                a = fly[src][:, :, :].rearrange("p (n s w) d -> p n s (w d)", s=2, w=w)
                b = fly[dst][:, :, :].rearrange("p (n s w) d -> p n s (w d)", s=2, w=w)
                ins1 = dve.tensor_tensor(b[:, :, 0, :], a[:, :, 0, :], a[:, :, 1, :], ALU.add)
                ins2 = dve.tensor_tensor(b[:, :, 1, :], a[:, :, 0, :], a[:, :, 1, :], ALU.subtract)
                ch.done(ins1)
                if st < 2:
                    ch.link(ins2)
                else:
                    ch.settle()
                    ins2.then_inc(w2_ready, 1)
                src, dst = dst, src
            for n in range(2 * NH):
                half, k = n // NH, n % NH
                dve.wait_ge(silu_made, n + 1)
                dve.tensor_tensor(hidden[:, k, half * HALF:(half + 1) * HALF], banks[4 + n % 4][:, 0:HALF],
                                  act_g[n % 2][:, :], ALU.mult).then_inc(hidden_made, 1)
            for t in range(NTILE):
                dve.wait_ge(projected, t + 1)
                dve.scalar_tensor_tensor(xs[:, t, :], banks[t % 4][0:TT, 0:D], gate[:, 1:2], xs[:, t, :],
                                         ALU.mult, ALU.add).then_inc(added, 1)


GH = H1 // 2
WG = GH * HD1


def project_heads(nc, wq, bq, qn_w, qn_b, ident_in, xs, qT):
    NG = NTILE * H1
    with ExitStack() as ctx:
        sc = Scope(nc, ctx, "p1")
        ident = sc.sb("ident", [128, 128])
        wq_sb = sc.sb("wq", [128, CH, D])
        bq_sb = sc.sb("bq", [TT, D])
        w_sb = sc.sb("w", [TT, HD1])
        b_sb = sc.sb("b", [TT, HD1])
        xn = sc.sb("xn", [TT, NTILE, D])
        xnT = sc.sb("xnT", [128, CH, NT])
        q = sc.sb("q", [TT, NTILE, D])
        sq = sc.sb("sq", [TT, NTILE, D])
        mean, var, r, t1, t2 = (sc.sb(n, [TT, NG]) for n in ("mean", "var", "r", "t1", "t2"))
        scratch = ln_scratch(sc)
        banks = [sc.ps(f"b{k}", [128, 512]) for k in range(6)]
        loaded, v_loaded = sc.sem("ld"), sc.sem("v_ld")
        dve_steps, xn_ready = sc.sem("dve_steps"), sc.sem("xn_ready")
        turned, turn_kept = sc.sem("turned"), sc.sem("turn_kept")
        projected, q_kept, q_ready = sc.sem("projected"), sc.sem("q_kept"), sc.sem("q_ready")
        q_turned, q_turn_kept = sc.sem("q_turned"), sc.sem("q_turn_kept")
        block = ctx.enter_context(nc.Block())

        @block.sync
        def _(sp):
            sp.dma_start(ident[:, :], ident_in).then_inc(loaded, 16)
            sp.dma_start(wq_sb[:, :, :], wq.rearrange("(c p) d -> p c d", p=128)).then_inc(loaded, 16)
            sp.dma_start(bq_sb[:, :], bq.partition_broadcast(TT)).then_inc(v_loaded, 16)
            sp.dma_start(w_sb[:, :], qn_w.partition_broadcast(TT)).then_inc(v_loaded, 16)
            sp.dma_start(b_sb[:, :], qn_b.partition_broadcast(TT)).then_inc(v_loaded, 16)

        @block.tensor
        def _(pe):
            pe.wait_ge(loaded, 32)
            turn_tokens(pe, None, xn, xnT, banks[0:2], ident, xn_ready, turned, turn_kept)
            for t in range(NTILE):
                pe.wait_ge(turn_kept, CH * (t // 4 + 1))
                if t >= 4:
                    pe.wait_ge(q_kept, t - 3)
                for c in range(CH):
                    mm = pe.matmul(banks[2 + t % 4][0:TT, 0:D], xnT[:, c, t * TT:(t + 1) * TT], wq_sb[:, c, :],
                                   start=(c == 0), stop=(c == CH - 1))
                mm.then_inc(projected, 1)
            turn_tokens(pe, None, q, qT, banks[0:2], ident, q_ready, q_turned, q_turn_kept)

        @block.scalar
        def _(act):
            turn_tokens(None, act, xn, xnT, banks[0:2], ident, xn_ready, turned, turn_kept)
            turn_tokens(None, act, q, qT, banks[0:2], ident, q_ready, q_turned, q_turn_kept)

        @block.vector
        def _(dve):
            ch = Chain(dve, dve_steps)
            layer_norm(ch, xn[:, :, :], xs[:, :, :], *scratch, TT, xn_ready)
            dve.wait_ge(v_loaded, 48)
            for t in range(NTILE):
                dve.wait_ge(projected, t + 1)
                dve.tensor_tensor(q[:, t, :], banks[2 + t % 4][0:TT, 0:D], bq_sb[:, :], ALU.add).then_inc(q_kept, 1)
            dve.wait_ge(q_kept, NTILE)

            def heads(x):
                return x[:, :, :].rearrange("p n (h e) -> p (n h) e", e=HD1)

            def of_head(x):
                return x[:, :].rearrange("p (g a) -> p g a", a=1).broadcast_to([TT, NG, HD1])

            def of_column(x):
                return x[:, :].rearrange("p (a e) -> p a e", a=1).broadcast_to([TT, NG, HD1])

            ch.link(dve.tensor_reduce(mean[:, :], heads(q), AX.X, ALU.add))
            ch.link(dve.tensor_scalar(mean[:, :], mean[:, :], 1.0 / HD1, None, ALU.mult))
            ch.link(dve.tensor_tensor(heads(q), heads(q), of_head(mean), ALU.subtract))
            ch.link(dve.tensor_tensor(heads(sq), heads(q), heads(q), ALU.mult))
            ch.link(dve.tensor_reduce(var[:, :], heads(sq), AX.X, ALU.add))
            ch.link(dve.tensor_scalar(var[:, :], var[:, :], 1.0 / HD1, EPS_HEAD, ALU.mult, ALU.add))
            rsqrt(ch, r[:, :], var[:, :], t1[:, :], t2[:, :])
            ch.link(dve.tensor_tensor(heads(q), heads(q), of_head(r), ALU.mult))
            ch.link(dve.tensor_tensor(heads(q), heads(q), of_column(w_sb), ALU.mult))
            ch.link(dve.tensor_tensor(heads(q), heads(q), of_column(b_sb), ALU.add))
            dve.sem_inc(q_ready, NTILE)


def attend_heads(nc, ctxT_in, wkv, bk, affine_in, blocks_in, ident_in, qT):
    SCALE = float(HD1) ** -0.5
    NS = 3
    STEPS = 2 * UNIT
    with ExitStack() as ctx:
        sc = Scope(nc, ctx, "a1")
        ident = sc.sb("ident", [128, 128])
        w_hi = sc.sb("w_hi", [DC, 2, 2 * WG], F32R)
        w_lo = sc.sb("w_lo", [DC, 2, 2 * WG], F32R)
        w_dca = sc.sb("w_dca", [DC, 2, 2 * WG])
        bias_rows = sc.sb("bias_rows", [96, 2, 2, WG], BF16)
        one_rows = sc.sb("one_rows", [96, 128], BF16)
        affine = sc.sb("affine", [128, 4])
        blocks = sc.sb("blocks", [128, GH])
        ones = sc.sb("ones", [128, 128])

        with ExitStack() as prep:
            pc = Scope(nc, prep, "w1")
            w = pc.sb("w", [DC, 2, 2, 2 * WG])
            bias = pc.sb("bias", [96, 2, 2, WG])
            part = pc.sb("part", [96, 2, 2, WG], BF16)
            mean = pc.sb("mean", [128, 4, GH])
            bmean = pc.sb("bmean", [96, 4, GH])
            loaded, b_loaded, cleared = pc.sem("ld"), pc.sem("b_ld"), pc.sem("cleared")
            dve_steps, consts = pc.sem("dve_steps"), pc.sem("consts")
            block = prep.enter_context(nc.Block())

            @block.sync
            def _(sp):
                sp.dma_start(w[:, :, :, :], wkv).then_inc(loaded, 16)
                sp.dma_start(ident[:, :], ident_in).then_inc(loaded, 16)
                sp.dma_start(affine[:, :], affine_in).then_inc(loaded, 16)
                sp.dma_start(blocks[:, :], blocks_in).then_inc(loaded, 16)
                sp.wait_ge(cleared, 2)
                for row in (0, 32, 64):
                    sp.dma_start(bias[row:row + 1, :, :, :].rearrange("p a b c -> p (a b c)"),
                                 bk.rearrange("(o a) -> o a", o=1)).then_inc(b_loaded, 16)

            @block.gpsimd
            def _(pool):
                pool.memset(bias[:, :, :, :], 0.0).then_inc(cleared, 1)
                pool.memset(bias_rows[:, :, :, :], 0.0).then_inc(cleared, 1)
                pool.memset(one_rows[:, :], 1.0).then_inc(consts, 1)
                pool.memset(ones[:, :], 1.0).then_inc(consts, 1)

            @block.vector
            def _(dve):
                ch = Chain(dve, dve_steps)
                dve.wait_ge(loaded, 64)
                dve.wait_ge(b_loaded, 48)
                for m, x, n in ((mean, w, 128), (bmean, bias, 96)):
                    for k in range(4):
                        keys = x[:, k // 2, k % 2, 0:WG].rearrange("p (h e) -> p h e", e=HD1)
                        ch.link(dve.tensor_reduce(m[:, k, :], keys, AX.X, ALU.add))
                        ch.link(dve.tensor_scalar(m[:, k, :], m[:, k, :], 1.0 / HD1, None, ALU.mult))
                        ch.link(dve.tensor_tensor(keys, keys, m[:, k, :].rearrange("p (h a) -> p h a", a=1)
                                                  .broadcast_to([n, GH, HD1]), ALU.subtract))
                ch.link(dve.tensor_copy(w_hi[:, :, :], w[:, 0]))
                ch.done(dve.tensor_tensor(w_lo[:, :, :], w[:, 0], w_hi[:, :, :].bitcast(F32), ALU.subtract))
                ch.done(dve.tensor_copy(w_dca[:, :, :], w[:, 1]))
                for row in (0, 32, 64):
                    ch.link(dve.tensor_copy(part[:, :, :, :], bias[:, :, :, :]))
                    ch.done(dve.tensor_copy(bias_rows[row:row + 1], part[row:row + 1]))
                    ch.link(dve.tensor_tensor(bias[:, :, :, :], bias[:, :, :, :], part[:, :, :, :], ALU.subtract))

        rawT = sc.sb("rawT", [DC, SK])
        dcaT = sc.sb("dcaT", [DC, DCA])
        cT_hi = sc.sb("cT_hi", [DC, SK], F32R)
        cT_lo = sc.sb("cT_lo", [DC, SK], F32R)
        k_hi = [sc.sb(f"k_hi{p}", [WG, SK], F32R) for p in range(2)]
        k_lo = [sc.sb(f"k_lo{p}", [WG, SK], F32R) for p in range(2)]
        v_hi = [sc.sb(f"v_hi{p}", [KT, NKT, WG], F32R) for p in range(2)]
        v_lo = [sc.sb(f"v_lo{p}", [KT, NKT, WG], F32R) for p in range(2)]
        q_block = sc.sb("q_block", [WG, GH, S])
        q_hi = [sc.sb(f"q_hi{p}", [WG, GH * S], F32R) for p in range(2)]
        q_lo = [sc.sb(f"q_lo{p}", [WG, GH * S], F32R) for p in range(2)]
        k_raw = sc.sb("k_raw", [KT, 4, WG])
        k_sq = sc.sb("k_sq", [KT, 4, WG])
        k_norm = sc.sb("k_norm", [KT, 4, WG])
        k_full = sc.sb("k_full", [WG, CK])
        var, k_r, t1, t2 = (sc.sb(n, [KT, 4 * GH]) for n in ("var", "k_r", "n1", "n2"))
        probs = [sc.sb(f"probs{p}", [TT, SK]) for p in range(2)]
        pT_hi = [sc.sb(f"pT_hi{p}", [KT, NKT, HALF], F32R) for p in range(2)]
        pT_lo = [sc.sb(f"pT_lo{p}", [KT, NKT, HALF], F32R) for p in range(2)]
        part_min = sc.sb("part_min", [TT, 2, NCH])
        row_min = sc.sb("row_min", [TT, 2])
        dca_s = sc.sb("dca_s", [TT, 2, DCA])
        dca_e = sc.sb("dca_e", [TT, 2, DCA])
        dca_min, dca_sum, dca_inv = (sc.sb(n, [TT, 2]) for n in ("dca_min", "dca_sum", "dca_inv"))
        sums = sc.sb("sums", [TT, 2, UNIT])
        inv = sc.sb("inv", [TT, UNIT])
        inv_diag = sc.sb("inv_diag", [TT, UNIT, TT])
        inv_block = sc.sb("inv_block", [WG, GH, S])
        s_ps = [sc.ps(f"s{k}", [128, 512]) for k in range(NS)]
        t_ps = [sc.ps(f"t{k}", [128, 512]) for k in range(2)]
        o_ps = sc.ps("o_ps", [128, 512])
        kv_ps = sc.ps("kv_ps", [128, 512])
        x_ps = sc.ps("x_ps", [128, 512])

        ctx_loaded = sc.sem("ctx_ld")
        hi_split, split_done = sc.sem("hi_split"), sc.sem("split_done")
        q_steps, q_ready = sc.sem("q_steps"), sc.sem("q_ready")
        kv_made, v_hi_kept, kv_kept = sc.sem("kv_made"), sc.sem("v_hi_kept"), sc.sem("kv_kept")
        k_raw_kept, squared, k_normed = sc.sem("k_raw_kept"), sc.sem("squared"), sc.sem("k_normed")
        k_turned, k_scaled = sc.sem("k_turned"), sc.sem("k_scaled")
        k_hi_made, keys_ready = sc.sem("k_hi_made"), sc.sem("keys_ready")
        scored, score_kept, dca_kept = sc.sem("scored"), sc.sem("score_kept"), sc.sem("dca_kept")
        row_max, dve_steps = sc.sem("row_max"), sc.sem("dve_steps")
        dca_exp, probs_made, dca_ready = sc.sem("dca_exp"), sc.sem("probs_made"), sc.sem("dca_ready")
        turned, turn_hi, turn_kept = sc.sem("turned"), sc.sem("turn_hi"), sc.sem("turn_kept")
        diag_made, inv_spread, inv_kept = sc.sem("diag_made"), sc.sem("inv_spread"), sc.sem("inv_kept")
        summed, o_kept, o_done = sc.sem("summed"), sc.sem("o_kept"), sc.sem("o_done")
        SCALED = NCH + 1
        block = ctx.enter_context(nc.Block())

        def bodies(eng, start, body, last):
            start()
            body(0, True, False)
            with eng.Fori(1, B - 1) as i:
                body(i, False, False)
            body(B - 1, False, True)
            last()

        @block.sync
        def _(sp):
            def load(b):
                wait(sp, split_done, NCH * b)
                sp.dma_start(rawT[:, :], ctxT_in[bass.ds(b, 1)].rearrange("b c k -> c (b k)")).then_inc(ctx_loaded, 16)

            def body(b, first, final):
                if not final:
                    load(b + 1)

            bodies(sp, lambda: load(0), body, lambda: None)

        @block.gpsimd
        def _(pool):
            def split(b, c):
                cols = slice(c * CK, (c + 1) * CK)
                pool.wait_ge(ctx_loaded, 16 * (b + 1))
                wait(pool, kv_made, 2 * (NCH * (2 * b - 1) + c + 1))
                if c == 0:
                    upper_part(pool, dcaT[:, :], rawT[:, 0:DCA], ones).then_inc(hi_split, 1)
                upper_part(pool, cT_hi[:, cols], rawT[:, cols], ones).then_inc(hi_split, 1)
                pool.wait_ge(hi_split, (NCH + 1) * b + c + 2)
                pool.tensor_tensor(cT_lo[:, cols], rawT[:, cols], cT_hi[:, cols].bitcast(F32), ALU.subtract
                                   ).then_inc(split_done, 1)

            def queries(v, b, g):
                wait(pool, scored, UNIT * NCH * (v - 1))
                wait(pool, q_ready, v)
                pool.tensor_tensor(
                    q_block[:, :, :],
                    qT[:, g, bass.ds(b * S, S)].rearrange("p (a t) -> p a t", a=1).broadcast_to([WG, GH, S]),
                    blocks[:, :].rearrange("p (h a) -> p h a", a=1).broadcast_to([WG, GH, S]), ALU.mult
                ).then_inc(q_steps, 1)
                pool.wait_ge(q_steps, 2 * v + 1)
                q = q_block[:, :, :].rearrange("p h t -> p (h t)")
                upper_part(pool, q_hi[g][:, :], q, ones).then_inc(q_steps, 1)
                pool.wait_ge(q_steps, 2 * v + 2)
                pool.tensor_tensor(q_lo[g][:, :], q, q_hi[g][:, :].bitcast(F32), ALU.subtract).then_inc(q_ready, 1)

            def keys(v, g, c):
                cols = slice(c * CK, (c + 1) * CK)
                pool.wait_ge(k_scaled, SCALED * v + c + 2)
                if c == 0:
                    wait(pool, scored, UNIT * NCH * (v - 1))
                upper_part(pool, k_hi[g][:, cols], k_full[:, :], ones).then_inc(k_hi_made, 1)
                pool.wait_ge(k_hi_made, NCH * v + c + 1)
                pool.tensor_tensor(k_lo[g][:, cols], k_full[:, :], k_hi[g][:, cols].bitcast(F32), ALU.subtract
                                   ).then_inc(keys_ready, 1)

            def start():
                for c in range(NCH):
                    split(0, c)
                queries(0, 0, 0)
                for c in range(NCH):
                    keys(0, 0, c)

            def body(b, first, final):
                for g in range(2):
                    if final and g == 1:
                        continue
                    v, vg = 2 * b + g + 1, (g + 1) % 2
                    queries(v, b + g, vg)
                    for c in range(NCH):
                        if g == 0 and not final:
                            split(b + 1, c)
                        keys(v, vg, c)

            bodies(pool, start, body, lambda: None)

        @block.tensor
        def _(pe):
            def project(v, b, g, c, pair):
                if pair == 0:
                    pe.wait_ge(split_done, NCH * b + c + 1)
                wait(pe, kv_kept, 2 * (NCH * v + c) + pair)
                for k in range(2):
                    j = 4 * c + 2 * pair + k
                    cols = slice(j * KT, (j + 1) * KT)
                    out = kv_ps[0:KT, k * 2 * WG:(k + 1) * 2 * WG]
                    pe.matmul(out, cT_hi[:, cols], w_hi[:, g, :], start=True, stop=False)
                    pe.matmul(out[:, 0:WG], one_rows[:, 0:KT], bias_rows[:, 0, g, :], start=False, stop=False)
                    pe.matmul(out, cT_hi[:, cols], w_lo[:, g, :], start=False, stop=False)
                    mm = pe.matmul(out, cT_lo[:, cols], w_hi[:, g, :], start=False, stop=True)
                    if j == 0:
                        top = kv_ps[0:DCA, :]
                        pe.matmul(top[:, WG:2 * WG], dcaT[:, :], w_dca[:, g, WG:2 * WG], start=True, stop=True)
                        pe.matmul(top[:, 0:WG], dcaT[:, :], w_dca[:, g, 0:WG], start=True, stop=False)
                        pe.matmul(top[:, 0:WG], one_rows[:, 0:DCA], bias_rows[:, 1, g, :], start=False, stop=True)
                mm.then_inc(kv_made, 1)

            def turn_keys(v, c):
                pe.wait_ge(k_normed, NCH * v + c + 1)
                wait(pe, k_scaled, SCALED * v + c + 1 if c else SCALED * v)
                for k in range(4):
                    mm = pe.transpose(x_ps[:, k * KT:(k + 1) * KT], k_norm[:, k, :], ident[0:KT, 0:KT])
                mm.then_inc(k_turned, 1)

            def scores(n, s):
                g, r = s // UNIT, s % UNIT
                rows = slice(r * TT, (r + 1) * TT)
                for c in range(NCH):
                    m = NCH * n + c
                    wait(pe, score_kept, m - NS + 1)
                    if c == 0:
                        wait(pe, dca_kept, n)
                    keys = slice(c * CK, (c + 1) * CK)
                    three_passes(pe, s_ps[c][0:TT, 0:CK], q_hi[g][:, rows], q_lo[g][:, rows],
                                 k_hi[g][:, keys], k_lo[g][:, keys], True, True).then_inc(scored, 1)

            def turn(n, s):
                pe.wait_ge(probs_made, n + 1)
                pe.wait_ge(dca_ready, n + 1)
                for f in range(NCH):
                    m = NCH * n + f
                    wait(pe, turn_kept, m - 1)
                    for k in range(4):
                        j = 4 * f + k
                        mm = pe.transpose(t_ps[(NCH * s + f) % 2][0:KT, k * TT:(k + 1) * TT],
                                          probs[s % 2][:, j * KT:(j + 1) * KT], ident[0:TT, 0:TT])
                    mm.then_inc(turned, 1)

            def weigh(u, s, keys_taken):
                g = s // UNIT
                pe.wait_ge(diag_made, u + 1)
                pe.wait_ge(k_scaled, keys_taken)
                pe.matmul(x_ps[:, 0:HALF], ones[0:TT, :], inv_diag[:, :, :].rearrange("p k t -> p (k t)"),
                          start=True, stop=True).then_inc(inv_spread, 1)
                wait(pe, o_kept, u)
                for j in range(NKT):
                    if j % 4 == 0:
                        pe.wait_ge(turn_kept, NCH * UNIT * u + NCH * (UNIT - 1) + j // 4 + 1)
                    mm = three_passes(pe, o_ps[:, 0:HALF], v_hi[g][:, j, :], v_lo[g][:, j, :],
                                      pT_hi[g][:, j, :], pT_lo[g][:, j, :], j == 0, j == NKT - 1)
                mm.then_inc(summed, 1)

            def start():
                for c in range(NCH):
                    for pair in range(2):
                        project(0, 0, 0, c, pair)
                    turn_keys(0, c)

            def body(b, first, final):
                for s in range(STEPS):
                    n, g, r = STEPS * b + s, s // UNIT, s % UNIT
                    u = 2 * b + g
                    v, vb, vg = u + 1, b + g, (g + 1) % 2
                    more = not (final and g == 1)
                    if r == 0:
                        pe.wait_ge(q_ready, u + 1)
                        pe.wait_ge(keys_ready, NCH * (u + 1))
                    if 0 < r < NCH and more:
                        project(v, vb, vg, r, 0)
                    scores(n, s)
                    if 0 < r < NCH and more:
                        project(v, vb, vg, r, 1)
                    if not (first and s == 0):
                        turn(n - 1, (s - 1) % STEPS)
                    if r == 0:
                        if not (first and s == 0):
                            weigh(u - 1, (s - 1) % STEPS, SCALED * (u + 1))
                        if more:
                            project(v, vb, vg, 0, 0)
                            project(v, vb, vg, 0, 1)
                    if r >= 1 and more:
                        if r == 1:
                            wait(pe, inv_kept, u)
                        turn_keys(v, r - 1)

            def last():
                turn(STEPS * B - 1, STEPS - 1)
                weigh(2 * B - 1, STEPS - 1, SCALED * 2 * B)

            bodies(pe, start, body, last)

        @block.scalar
        def _(act):
            def keep(v, g, c, pair):
                act.wait_ge(kv_made, 2 * (NCH * v + c) + pair + 1)
                if pair == 0:
                    wait(act, k_normed, NCH * v + c)
                    if c == 0:
                        wait(act, summed, v - 1)
                j = 4 * c + 2 * pair
                kv = kv_ps[0:KT, :].rearrange("p (k n) -> p k n", k=2)
                act.copy(k_raw[:, 2 * pair:2 * pair + 2, :], kv[:, :, 0:WG]).then_inc(k_raw_kept, 1)
                act.copy(v_hi[g][:, j:j + 2, :], kv[:, :, WG:2 * WG]).then_inc(v_hi_kept, 1)
                if pair == 1:
                    act.wait_ge(k_raw_kept, 2 * (NCH * v + c + 1))
                    act.activation(k_sq[:, :, :], k_raw[:, :, :], ACT.Square).then_inc(squared, 1)

            def scale_keys(v, c):
                act.wait_ge(k_turned, NCH * v + c + 1)
                wait(act, keys_ready, NCH * v + c)
                lo = DCA if c == 0 else 0
                if c == 0:
                    act.activation(k_full[:, 0:DCA], x_ps[:, 0:DCA], ACT.Identity, scale=affine[:, 2:3],
                                   bias=affine[:, 3:4]).then_inc(k_scaled, 1)
                act.activation(k_full[:, lo:CK], x_ps[:, lo:CK], ACT.Identity, scale=affine[:, 0:1],
                               bias=affine[:, 1:2]).then_inc(k_scaled, 1)

            def upper(n, s, u):
                g, r = s // UNIT, s % UNIT
                for f in range(NCH):
                    act.wait_ge(turned, NCH * n + f + 1)
                    if f == 0 and r == 0:
                        wait(act, summed, u - 1)
                    act.copy(pT_hi[g][:, 4 * f:4 * f + 4, r * TT:(r + 1) * TT],
                             t_ps[(NCH * s + f) % 2][0:KT, 0:HALF].rearrange("p (k t) -> p k t", t=TT)
                             ).then_inc(turn_hi, 1)

            def exps(n, s):
                p = s % 2
                act.wait_ge(row_max, n + 1)
                act.activation(dca_e[:, p, :], dca_s[:, p, :], ACT.Exp, scale=-1.0, bias=dca_min[:, p:p + 1],
                               accum_out=dca_sum[:, p:p + 1]).then_inc(dca_exp, 1)
                act.activation(probs[p][:, DCA:SK], probs[p][:, DCA:SK], ACT.Exp, scale=-1.0,
                               bias=row_min[:, p:p + 1],
                               accum_out=sums[:, s // UNIT, s % UNIT:s % UNIT + 1]).then_inc(probs_made, 1)

            def start():
                for c in range(NCH):
                    for pair in range(2):
                        keep(0, 0, c, pair)
                    scale_keys(0, c)

            def body(b, first, final):
                for s in range(STEPS):
                    n, g, r = STEPS * b + s, s // UNIT, s % UNIT
                    u = 2 * b + g
                    v, vg = u + 1, (g + 1) % 2
                    more = not (final and g == 1)
                    if 0 < r < NCH and more:
                        keep(v, vg, r, 0)
                        keep(v, vg, r, 1)
                    if not (first and s == 0):
                        upper(n - 1, (s - 1) % STEPS, 2 * b + (s - 1) // UNIT)
                    exps(n, s)
                    if r == 0 and more:
                        keep(v, vg, 0, 0)
                        keep(v, vg, 0, 1)
                    if r >= 1 and more:
                        scale_keys(v, r - 1)

            def last():
                upper(STEPS * B - 1, STEPS - 1, 2 * B - 1)

            bodies(act, start, body, last)

        @block.vector
        def _(dve):
            THIRD_N = 14
            UNIT_N = 1
            TILE_N = 1

            def values(v, g, c, pair):
                dve.wait_ge(v_hi_kept, 2 * (NCH * v + c) + pair + 1)
                j = 4 * c + 2 * pair
                kv = kv_ps[0:KT, :].rearrange("p (k n) -> p k n", k=2)
                dve.tensor_tensor(v_lo[g][:, j:j + 2, :], kv[:, :, WG:2 * WG],
                                  v_hi[g][:, j:j + 2, :].bitcast(F32), ALU.subtract).then_inc(kv_kept, 1)

            def normalise(v, c, ch):
                n0 = ch.n
                dve.wait_ge(squared, NCH * v + c + 1)
                wait(dve, k_turned, NCH * v + c)
                ch.link(dve.tensor_reduce(var[:, :], k_sq[:, :, :].rearrange("p n (h e) -> p (n h) e", e=HD1),
                                          AX.X, ALU.add))
                ch.link(dve.tensor_scalar(var[:, :], var[:, :], 1.0 / HD1, EPS_HEAD, ALU.mult, ALU.add))
                rsqrt(ch, k_r[:, :], var[:, :], t1[:, :], t2[:, :])
                dve.tensor_tensor(k_norm[:, :, :].rearrange("p n (h e) -> p (n h) e", e=HD1),
                                  k_raw[:, :, :].rearrange("p n (h e) -> p (n h) e", e=HD1),
                                  k_r[:, :].rearrange("p (g a) -> p g a", a=1).broadcast_to([KT, 4 * GH, HD1]),
                                  ALU.mult).then_inc(k_normed, 1)
                assert ch.n - n0 == THIRD_N

            def negated(n, s):
                p = s % 2
                wait(dve, turned, NCH * (n - 1))
                for c in range(NCH):
                    dve.wait_ge(scored, NCH * n + c + 1)
                    lo = DCA if c == 0 else 0
                    if c == 0:
                        dve.tensor_scalar(dca_s[:, p, :], s_ps[0][0:TT, 0:DCA], -SCALE, BIG, ALU.mult, ALU.min,
                                          accum_out=dca_min[:, p:p + 1]).then_inc(dca_kept, 1)
                    dve.tensor_scalar(probs[p][:, c * CK + lo:(c + 1) * CK], s_ps[c][0:TT, lo:CK], -SCALE, BIG,
                                      ALU.mult, ALU.min, accum_out=part_min[:, p, c:c + 1]).then_inc(score_kept, 1)
                dve.wait_ge(score_kept, NCH * n + NCH)
                dve.wait_ge(dca_kept, n + 1)
                dve.tensor_reduce(row_min[:, p:p + 1], part_min[:, p, :], AX.X, ALU.min).then_inc(row_max, 1)

            def extra(n, s, ch):
                p = s % 2
                dve.wait_ge(dca_exp, n + 1)
                ch.link(dve.reciprocal(dca_inv[:, p:p + 1], dca_sum[:, p:p + 1]))
                dve.wait_ge(probs_made, n + 1)
                dve.tensor_scalar(probs[p][:, 0:DCA], dca_e[:, p, :], dca_inv[:, p:p + 1],
                                  sums[:, s // UNIT, s % UNIT:s % UNIT + 1], ALU.mult, ALU.mult
                                  ).then_inc(dca_ready, 1)

            def rest(n, s):
                g, r = s // UNIT, s % UNIT
                rows = slice(r * TT, (r + 1) * TT)
                for f in range(NCH):
                    dve.wait_ge(turn_hi, NCH * n + f + 1)
                    dve.tensor_tensor(pT_lo[g][:, 4 * f:4 * f + 4, rows],
                                      t_ps[(NCH * s + f) % 2][0:KT, 0:HALF].rearrange("p (k t) -> p k t", t=TT),
                                      pT_hi[g][:, 4 * f:4 * f + 4, rows].bitcast(F32), ALU.subtract
                                      ).then_inc(turn_kept, 1)

            def invert(u, s, ch):
                ch.link(dve.reciprocal(inv[:, :], sums[:, s // UNIT, :]))
                wait(dve, inv_spread, u)
                dve.tensor_tensor(inv_diag[:, :, :],
                                  ident[0:TT, 0:TT].rearrange("p (a t) -> p a t", a=1).broadcast_to([TT, UNIT, TT]),
                                  inv[:, :].rearrange("p (k a) -> p k a", a=1).broadcast_to([TT, UNIT, TT]),
                                  ALU.mult).then_inc(diag_made, 1)

            def take_inverse(u):
                dve.wait_ge(inv_spread, u + 1)
                wait(dve, o_kept, u)
                dve.tensor_tensor(inv_block[:, :, :], x_ps[:, 0:HALF].rearrange("p (h t) -> p h t", t=S),
                                  blocks[:, :].rearrange("p (h a) -> p h a", a=1).broadcast_to([WG, GH, S]),
                                  ALU.mult).then_inc(inv_kept, 1)

            def finish(u, b, g):
                dve.wait_ge(summed, u + 1)
                dve.wait_ge(inv_kept, u + 1)
                blk = inv_block[:, :, :]
                dve.tensor_tensor(blk, o_ps[:, 0:HALF].rearrange("p (h t) -> p h t", t=S), blk, ALU.mult
                                  ).then_inc(o_kept, 1)
                dve.wait_ge(o_kept, u + 1)
                dve.tensor_reduce(qT[:, g, bass.ds(b * S, S)], blk.rearrange("p h t -> p t h"), AX.X, ALU.add
                                  ).then_inc(o_done, 1)
                dve.wait_ge(o_done, u + 1)

            def start():
                ch = Chain(dve, dve_steps)
                for c in range(NCH):
                    for pair in range(2):
                        values(0, 0, c, pair)
                    normalise(0, c, ch)

            PER_BODY = 2 * (NCH * THIRD_N + UNIT_N) + STEPS * TILE_N

            def body(b, first, final):
                ch = Chain(dve, dve_steps, NCH * THIRD_N + PER_BODY * b - (0 if first else UNIT_N))
                for s in range(STEPS):
                    n, g, r = STEPS * b + s, s // UNIT, s % UNIT
                    u = 2 * b + g
                    v, vg = u + 1, (g + 1) % 2
                    more = not (final and g == 1)
                    if 0 < r < NCH and more:
                        values(v, vg, r, 0)
                    negated(n, s)
                    if 0 < r < NCH and more:
                        values(v, vg, r, 1)
                    if r == 0 and not (first and s == 0):
                        invert(u - 1, (s - 1) % STEPS, ch)
                    if r == 1 and not (first and s == 1):
                        finish(u - 1, b + g - 1, (g + 1) % 2)
                    if not (first and s == 0):
                        rest(n - 1, (s - 1) % STEPS)
                    if r == 0 and not (first and s == 0):
                        take_inverse(u - 1)
                    if r > 0 and r < NCH and more:
                        normalise(v, r, ch)
                    extra(n, s, ch)
                    if r == 0 and more:
                        values(v, vg, 0, 0)
                        values(v, vg, 0, 1)
                        normalise(v, 0, ch)

            def last():
                ch = Chain(dve, dve_steps, NCH * THIRD_N * (2 * B) + STEPS * TILE_N * B + UNIT_N * (2 * B - 1))
                invert(2 * B - 1, STEPS - 1, ch)
                rest(STEPS * B - 1, STEPS - 1)
                take_inverse(2 * B - 1)
                finish(2 * B - 1, B - 1, 1)

            bodies(dve, start, body, last)


def close_heads(nc, wo, bv, bo, x2_d, qT, xs, gate):
    with ExitStack() as ctx:
        sc = Scope(nc, ctx, "c1")
        wo_sb = sc.sb("wo", [128, CH, D])
        bv_sb = sc.sb("bv", [128, 2, CH])
        bsum = sc.sb("bsum", [128, CH])
        bo_sb = sc.sb("bo", [TT, D])
        y = [sc.sb(f"y{k}", [TT, D]) for k in range(2)]
        y_ps = [sc.ps(f"y_ps{k}", [128, 512]) for k in range(4)]
        w_loaded, v_loaded, x_loaded = sc.sem("w_ld"), sc.sem("v_ld"), sc.sem("x_ld")
        dve_steps, biased = sc.sem("dve_steps"), sc.sem("biased")
        projected, with_bias, added = sc.sem("projected"), sc.sem("with_bias"), sc.sem("added")
        block = ctx.enter_context(nc.Block())

        @block.sync
        def _(sp):
            sp.dma_start(bv_sb[:, :, :], bv).then_inc(v_loaded, 16)
            sp.dma_start(wo_sb[:, :, :], wo.rearrange("(c p) d -> p c d", p=128)).then_inc(w_loaded, 16)
            sp.dma_start(bo_sb[:, :], bo.partition_broadcast(TT)).then_inc(v_loaded, 16)
            sp.dma_start(xs[:, :, :], x2_d.rearrange("(n p) d -> p n d", p=TT)).then_inc(x_loaded, 16)

        @block.tensor
        def _(pe):
            pe.wait_ge(w_loaded, 16)
            pe.wait_ge(biased, CH)
            for t in range(NTILE):
                if t >= 4:
                    pe.wait_ge(with_bias, t - 3)
                for c in range(CH):
                    mm = pe.matmul(y_ps[t % 4][0:TT, 0:D], qT[:, c, t * TT:(t + 1) * TT], wo_sb[:, c, :],
                                   start=(c == 0), stop=(c == CH - 1))
                mm.then_inc(projected, 1)

        @block.vector
        def _(dve):
            ch = Chain(dve, dve_steps)
            dve.wait_ge(v_loaded, 32)
            ch.link(dve.tensor_tensor(bsum[:, :], bv_sb[:, 0, :], bv_sb[:, 1, :], ALU.add))
            for c in range(CH):
                dve.tensor_scalar(qT[:, c, :], qT[:, c, :], bsum[:, c:c + 1], None, ALU.add).then_inc(biased, 1)
            dve.wait_ge(x_loaded, 16)
            for t in range(NTILE):
                dve.wait_ge(projected, t + 1)
                if t >= 2:
                    dve.wait_ge(added, t - 1)
                dve.tensor_tensor(y[t % 2][:, :], y_ps[t % 4][0:TT, 0:D], bo_sb[:, :], ALU.add).then_inc(with_bias, 1)
                dve.wait_ge(with_bias, t + 1)
                dve.scalar_tensor_tensor(xs[:, t, :], y[t % 2][:, :], gate[:, 2:3], xs[:, t, :],
                                         ALU.mult, ALU.add).then_inc(added, 1)


def route(nc, router_wT, expert_bias, ident_in, xs, x_hi, x_lo, p_d):
    with ExitStack() as ctx:
        sc = Scope(nc, ctx, "rt")
        ident = sc.sb("ident", [128, 128])
        wr = sc.sb("wr", [128, CH, E])
        eb = sc.sb("eb", [TT, E])
        xn = sc.sb("xn", [TT, NTILE, D])
        xnT = sc.sb("xnT", [128, CH, NT])
        z, e, s2, p, pw, score, choice, keep, tie, cnt, cnt2 = (
            sc.sb(n, [TT, NTILE, E]) for n in ("z", "e", "s2", "p", "pw", "score", "choice", "keep", "tie", "cnt", "cnt2"))
        top = sc.sb("top", [TT, NTILE, 8])
        room, total = sc.sb("room", [TT, NTILE]), sc.sb("total", [TT, NTILE])
        one = sc.sb("one", [1, NT])
        pT = sc.sb("pT", [E, NT])
        scratch = ln_scratch(sc)
        banks = [sc.ps(f"b{k}", [128, 512]) for k in range(5)]
        loaded, b_loaded = sc.sem("ld"), sc.sem("b_ld")
        dve_steps, xn_ready = sc.sem("dve_steps"), sc.sem("xn_ready")
        turned, turn_kept, split_hi, split_lo = (sc.sem(n) for n in ("turned", "turn_kept", "split_hi", "split_lo"))
        logits_made, abs_made, exp_made = sc.sem("logits_made"), sc.sem("abs_made"), sc.sem("exp_made")
        shares, p_turned, p_kept, p_stored, ones_set = (
            sc.sem(n) for n in ("shares", "p_turned", "p_kept", "p_stored", "ones_set"))
        block = ctx.enter_context(nc.Block())

        @block.sync
        def _(sp):
            sp.dma_start(ident[:, :], ident_in).then_inc(loaded, 16)
            sp.dma_start(wr[:, :, :], router_wT.rearrange("(c p) e -> p c e", p=128)).then_inc(loaded, 16)
            sp.dma_start(eb[:, :], expert_bias.partition_broadcast(TT)).then_inc(b_loaded, 16)
            sp.wait_ge(ones_set, 1)
            sp.dma_start(p_d[0:1, :], one[:, :]).then_inc(p_stored, 16)
            sp.wait_ge(p_kept, 2)
            sp.dma_start(p_d[1:E + 1, :], pT[:, :]).then_inc(p_stored, 16)
            sp.wait_ge(p_stored, 32)

        @block.gpsimd
        def _(pool):
            pool.memset(one[:, :], 1.0).then_inc(ones_set, 1)

        @block.tensor
        def _(pe):
            pe.wait_ge(loaded, 32)
            turn_tokens(pe, None, xn, xnT, banks[0:2], ident, xn_ready, turned, turn_kept)
            pe.wait_ge(turn_kept, 2 * CH)
            for t in range(NTILE):
                for c in range(CH):
                    mm = pe.matmul(banks[2][0:TT, t * E:(t + 1) * E], xnT[:, c, t * TT:(t + 1) * TT], wr[:, c, :],
                                   start=(c == 0), stop=(c == CH - 1))
            mm.then_inc(logits_made, 1)
            pe.wait_ge(shares, 1)
            for half in range(2):
                for k in range(4):
                    mm = pe.transpose(banks[3 + half][0:E, k * TT:(k + 1) * TT], p[:, 4 * half + k, :],
                                      ident[0:TT, 0:TT])
                mm.then_inc(p_turned, 1)

        @block.scalar
        def _(act):
            turn_tokens(None, act, xn, xnT, banks[0:2], ident, xn_ready, turned, turn_kept)
            act.wait_ge(turn_kept, 2 * CH)
            act.copy(x_hi[:, :, :], xnT[:, :, :]).then_inc(split_hi, 1)
            act.wait_ge(abs_made, 1)
            act.activation(e[:, :, :], z[:, :, :], ACT.Exp).then_inc(exp_made, 1)
            for half in range(2):
                act.wait_ge(p_turned, half + 1)
                act.copy(pT[:, half * HALF:(half + 1) * HALF], banks[3 + half][0:E, 0:HALF]).then_inc(p_kept, 1)

        @block.vector
        def _(dve):
            ch = Chain(dve, dve_steps)
            layer_norm(ch, xn[:, :, :], xs[:, :, :], *scratch, TT, xn_ready)
            dve.wait_ge(split_hi, 1)
            dve.tensor_tensor(x_lo[:, :, :], xnT[:, :, :], x_hi[:, :, :].bitcast(F32), ALU.subtract
                              ).then_inc(split_lo, 1)
            lg = banks[2][0:TT, 0:NTILE * E].rearrange("p (n e) -> p n e", e=E)

            def flat(x):
                return x[:, :, :]

            dve.wait_ge(logits_made, 1)
            ch.link(dve.tensor_copy(flat(s2), lg))
            ch.link(dve.tensor_scalar(flat(z), flat(s2), -1.0, None, ALU.mult))
            dve.tensor_tensor(flat(z), flat(s2), flat(z), ALU.min).then_inc(abs_made, 1)
            ch.link(dve.tensor_scalar(flat(score), flat(s2), 0.0, None, ALU.max))
            dve.wait_ge(exp_made, 1)
            ch.link(dve.tensor_scalar(flat(p), flat(e), 2.0, None, ALU.add))
            ch.link(dve.reciprocal(flat(p), flat(p)))
            ch.link(dve.tensor_tensor(flat(e), flat(e), flat(p), ALU.mult))
            ch.link(dve.tensor_tensor(flat(s2), flat(e), flat(e), ALU.mult))
            ch.link(dve.tensor_scalar(flat(pw), flat(s2), 2.0 / 17, 2.0 / 15, ALU.mult, ALU.add))
            for k in (13, 11, 9, 7, 5, 3, 1):
                ch.link(dve.tensor_tensor(flat(pw), flat(pw), flat(s2), ALU.mult))
                ch.link(dve.tensor_scalar(flat(pw), flat(pw), 2.0 / k, None, ALU.add))
            ch.link(dve.tensor_tensor(flat(pw), flat(pw), flat(e), ALU.mult))
            ch.link(dve.tensor_tensor(flat(z), flat(score), flat(pw), ALU.add))
            rsqrt(ch, flat(p), flat(z), flat(s2), flat(pw))
            ch.link(dve.tensor_tensor(flat(score), flat(z), flat(p), ALU.mult))
            dve.wait_ge(b_loaded, 16)
            ch.link(dve.tensor_tensor(flat(choice), flat(score),
                                      eb[:, :].rearrange("p (a e) -> p a e", a=1).broadcast_to([TT, NTILE, E]),
                                      ALU.add))
            for t in range(NTILE):
                ch.done(dve.max(top[:, t, :], choice[:, t, :]))
            ch.settle()
            fourth = top[:, :, TOPK - 1:TOPK].broadcast_to([TT, NTILE, E])
            ch.link(dve.tensor_tensor(flat(keep), flat(choice), fourth, ALU.is_gt))
            ch.link(dve.tensor_tensor(flat(tie), flat(choice), fourth, ALU.is_equal))
            ch.link(dve.tensor_reduce(room[:, :], flat(keep), AX.X, ALU.add))
            ch.link(dve.tensor_scalar(room[:, :], room[:, :], -1.0, float(TOPK), ALU.mult, ALU.add))
            a, b = tie, cnt
            for w in (1, 2, 4, 8, 16):
                ch.done(dve.tensor_copy(b[:, :, 0:w], a[:, :, 0:w]))
                ch.link(dve.tensor_tensor(b[:, :, w:E], a[:, :, w:E], a[:, :, 0:E - w], ALU.add))
                a, b = b, (cnt2 if b is cnt else cnt)
            ch.link(dve.tensor_tensor(flat(a), flat(a), room[:, :].rearrange("p (n a) -> p n a", a=1)
                                      .broadcast_to([TT, NTILE, E]), ALU.is_le))
            ch.link(dve.tensor_tensor(flat(tie), flat(tie), flat(a), ALU.mult))
            ch.link(dve.tensor_tensor(flat(keep), flat(keep), flat(tie), ALU.add))
            ch.link(dve.tensor_tensor(flat(score), flat(score), flat(keep), ALU.mult))
            ch.link(dve.tensor_reduce(total[:, :], flat(score), AX.X, ALU.add))
            ch.link(dve.tensor_scalar(total[:, :], total[:, :], 1e-20, None, ALU.add))
            ch.link(dve.reciprocal(total[:, :], total[:, :]))
            dve.tensor_tensor(flat(p), flat(score), total[:, :].rearrange("p (n a) -> p n a", a=1)
                              .broadcast_to([TT, NTILE, E]), ALU.mult).then_inc(shares, 1)


def experts(nc, weights_in, p_d, x_hi, x_lo, xs, gate, out):
    UP, DOWN = CH * I, 2 * CH * I
    WCOLS = DOWN + D
    LAG = 3
    NE = E + 1
    BODY = 3
    SLOTS = 2 * BODY
    assert NE % BODY == 0
    with ExitStack() as ctx:
        sc = Scope(nc, ctx, "ex")
        raw = [sc.sb(f"raw{p}", [128, WCOLS]) for p in range(BODY)]
        w_hi = [sc.sb(f"w_hi{p}", [128, WCOLS], F32R) for p in range(BODY)]
        w_lo = [sc.sb(f"w_lo{p}", [128, WCOLS], F32R) for p in range(BODY)]
        share = [sc.sb(f"share{p}", [128, NT]) for p in range(BODY)]
        zeros = sc.sb("zeros", [128, 512], BF16)
        gate_c, up_c, silu, up_p, h = ([sc.sb(f"{n}{p}", [I, HALF]) for p in range(2)]
                                       for n in ("gate_c", "up_c", "silu", "up_p", "h"))
        h_hi = [sc.sb(f"h_hi{p}", [I, HALF], F32R) for p in range(LAG)]
        h_lo = [sc.sb(f"h_lo{p}", [I, HALF], F32R) for p in range(LAG)]
        y_ps = [sc.ps(f"y{k}", [128, 512]) for k in range(4)]
        g_ps = [sc.ps(f"g{k}", [128, 512]) for k in range(2)]
        u_ps = [sc.ps(f"u{k}", [128, 512]) for k in range(2)]
        w_loaded = [sc.sem(f"w_ld{p}") for p in range(BODY)]
        p_loaded = [sc.sem(f"p_ld{p}") for p in range(BODY)]
        cleared, w_hi_made, w_ready = sc.sem("cleared"), sc.sem("w_hi_made"), sc.sem("w_ready")
        made, gate_clipped, clipped = sc.sem("made"), sc.sem("gate_clipped"), sc.sem("clipped")
        silu_made, scaled, h_made, h_hi_made, h_ready = (
            sc.sem(n) for n in ("silu_made", "scaled", "h_made", "h_hi_made", "h_ready"))
        downed, added, stored = sc.sem("downed"), sc.sem("added"), sc.sem("stored")
        block = ctx.enter_context(nc.Block())

        def bodies(eng, body, last):
            body(0, True, False)
            with eng.Fori(1, NE // BODY - 1) as i:
                body(i, False, False)
            body(NE // BODY - 1, False, True)
            last()

        @block.sync
        def _(sp):
            def body(i, first, final):
                for p in range(BODY):
                    e = BODY * i + p
                    wait(sp, w_ready, e - BODY + 1)
                    sp.dma_start(raw[p][:, :], weights_in[bass.ds(e, 1)].rearrange("e p w -> p (e w)")
                                 ).then_inc(w_loaded[p], 16)
                    wait(sp, scaled, 2 * (e - BODY) + 2)
                    sp.dma_start(share[p][:, :], p_d[bass.ds(e, 1)].rearrange("e t -> (e t)").partition_broadcast(128)
                                 ).then_inc(p_loaded[p], 16)

            def last():
                for t in range(NTILE):
                    sp.wait_ge(added, t + 1)
                    sp.dma_start(out[t * TT:(t + 1) * TT, :], xs[:, t, :]).then_inc(stored, 16)
                sp.wait_ge(stored, 16 * NTILE)

            bodies(sp, body, last)

        @block.gpsimd
        def _(pool):
            def weights_rest(e, p):
                pool.wait_ge(w_hi_made, e + 1)
                pool.tensor_tensor(w_lo[p][:, :], raw[p][:, :], w_hi[p][:, :].bitcast(F32), ALU.subtract
                                   ).then_inc(w_ready, 1)

            def body(i, first, final):
                if first:
                    pool.memset(zeros[:, :], 0.0).then_inc(cleared, 1)
                    weights_rest(0, 0)
                for k in range(SLOTS):
                    m, p, half = SLOTS * i + k, k // 2, k % 2
                    if half == 0:
                        pool.wait_ge(p_loaded[p], 16 * (i + 1))
                    pool.wait_ge(clipped, m + 1)
                    wait(pool, h_made, m - 1)
                    pool.tensor_tensor(up_p[half][:, :], up_c[half][:, :],
                                       share[p][:, half * HALF:(half + 1) * HALF], ALU.mult).then_inc(scaled, 1)
                    if half == 0 and not (final and p == BODY - 1):
                        weights_rest(BODY * i + p + 1, (p + 1) % BODY)

            bodies(pool, body, lambda: None)

        @block.tensor
        def _(pe):
            pe.wait_ge(cleared, 1)
            for k in range(4):
                pe.matmul(y_ps[k][0:TT, :], zeros[:, 0:TT], zeros[:, :], start=True, stop=True,
                          skip_group_check=True)

            def gate_up(e, m, p, half):
                if half == 0:
                    pe.wait_ge(w_ready, e + 1)
                wait(pe, clipped, m - 1)
                cols = slice(half * HALF, (half + 1) * HALF)
                for bank, base in ((g_ps[half], 0), (u_ps[half], UP)):
                    for c in range(CH):
                        w = slice(base + c * I, base + (c + 1) * I)
                        mm = three_passes(pe, bank[:, 0:HALF], w_hi[p][:, w], w_lo[p][:, w],
                                          x_hi[:, c, cols], x_lo[:, c, cols], c == 0, c == CH - 1)
                mm.then_inc(made, 1)

            def down(m, k):
                p, half, place = k // 2, k % 2, k % LAG
                pe.wait_ge(h_ready, m + 1)
                for t in range(4):
                    tile = 4 * half + t
                    rows = slice(t * TT, (t + 1) * TT)
                    y = y_ps[tile // 2][0:TT, (tile % 2) * D:(tile % 2 + 1) * D]
                    for a, b in ((h_hi, w_hi), (h_hi, w_lo), (h_lo, w_hi)):
                        mm = pe.matmul(y, a[place][:, rows], b[p][:, DOWN:WCOLS], start=False, stop=False,
                                       skip_group_check=True)
                mm.then_inc(downed, 1)

            def body(i, first, final):
                for k in range(SLOTS):
                    m = SLOTS * i + k
                    gate_up(BODY * i + k // 2, m, k // 2, k % 2)
                    if not (first and k < LAG):
                        down(m - LAG, (k - LAG) % SLOTS)

            def last():
                for k in range(SLOTS - LAG, SLOTS):
                    down(2 * NE - SLOTS + k, k)

            bodies(pe, body, last)

        @block.scalar
        def _(act):
            def weights_upper(e, i, p):
                act.wait_ge(w_loaded[p], 16 * (i + 1))
                wait(act, downed, 2 * (e - BODY) + 2)
                act.copy(w_hi[p][:, :], raw[p][:, :]).then_inc(w_hi_made, 1)

            def upper(m, k):
                act.wait_ge(h_made, m + 1)
                wait(act, downed, m - LAG + 1)
                act.copy(h_hi[k % LAG][:, :], h[k % 2][:, :]).then_inc(h_hi_made, 1)

            def body(i, first, final):
                if first:
                    weights_upper(0, 0, 0)
                for k in range(SLOTS):
                    m, p, half = SLOTS * i + k, k // 2, k % 2
                    act.wait_ge(gate_clipped, m + 1)
                    wait(act, h_made, m - 1)
                    act.activation(silu[half][:, :], gate_c[half][:, :], ACT.Silu).then_inc(silu_made, 1)
                    if not (first and k == 0):
                        upper(m - 1, (k - 1) % SLOTS)
                    if half == 0 and not (final and p == BODY - 1):
                        weights_upper(BODY * i + p + 1, i + (p + 1) // BODY, (p + 1) % BODY)

            bodies(act, body, lambda: upper(2 * NE - 1, SLOTS - 1))

        @block.vector
        def _(dve):
            def clip(m, k):
                half = k % 2
                dve.wait_ge(made, m + 1)
                wait(dve, silu_made, m - 1)
                dve.tensor_scalar(gate_c[half][:, :], g_ps[half][:, 0:HALF], -ALPHA, ALPHA, ALU.max, ALU.min
                                  ).then_inc(gate_clipped, 1)
                wait(dve, scaled, m - 1)
                dve.tensor_scalar(up_c[half][:, :], u_ps[half][:, 0:HALF], -ALPHA, ALPHA, ALU.max, ALU.min
                                  ).then_inc(clipped, 1)

            def hidden(m, k):
                half = k % 2
                dve.wait_ge(silu_made, m + 1)
                dve.wait_ge(scaled, m + 1)
                wait(dve, h_ready, m - 1)
                dve.tensor_tensor(h[half][:, :], silu[half][:, :], up_p[half][:, :], ALU.mult).then_inc(h_made, 1)

            def rest(m, k):
                dve.wait_ge(h_hi_made, m + 1)
                dve.tensor_tensor(h_lo[k % LAG][:, :], h[k % 2][:, :], h_hi[k % LAG][:, :].bitcast(F32), ALU.subtract
                                  ).then_inc(h_ready, 1)

            def body(i, first, final):
                for k in range(SLOTS):
                    m = SLOTS * i + k
                    clip(m, k)
                    if not (first and k < 2):
                        rest(m - 2, (k - 2) % SLOTS)
                    if not (first and k < 1):
                        hidden(m - 1, (k - 1) % SLOTS)

            def last():
                rest(2 * NE - 2, SLOTS - 2)
                hidden(2 * NE - 1, SLOTS - 1)
                rest(2 * NE - 1, SLOTS - 1)
                dve.wait_ge(downed, 2 * NE)
                for t in range(NTILE):
                    dve.scalar_tensor_tensor(xs[:, t, :], y_ps[t // 2][0:TT, (t % 2) * D:(t % 2 + 1) * D],
                                             gate[:, 3:4], xs[:, t, :], ALU.mult, ALU.add).then_inc(added, 1)

            bodies(dve, body, last)


def build(nc, a, out):
    def scratch(name, shape):
        return nc.dram_tensor(name, shape, F32).ap()

    q_hi_d, q_lo_d = scratch("q_hi_d", [DC, B, H0, S]), scratch("q_lo_d", [DC, B, H0, S])
    o_d, x2_d, p_d = scratch("o_d", [DC, H0, NT]), scratch("x2_d", [NT, D]), scratch("p_d", [E + 1, NT])
    project_queries(nc, a["x"], a["wqT"], a["wkT"], a["ident"], q_hi_d, q_lo_d)
    attend_context(nc, a["ctx"], a["ctxT"], a["mask"], a["ident"], q_hi_d, q_lo_d, o_d)
    with nc.sbuf_tensor("gate", [TT, 4], F32) as gate, nc.sbuf_tensor("qT", [128, CH, NT], F32) as qT:
        with nc.sbuf_tensor("x12", [TT, NTILE, D], F32) as xs, nc.semaphore("x2_stored") as x2_stored:
            close_attention(nc, o_d, a["x"], a["wvT"], a["wo0"], a["gates"], xs, gate)
            feed_forward(nc, a["w1T"], a["w3T"], a["w2T"], a["hadamard"], a["ident"], xs, gate)
            project_heads(nc, a["wq1"], a["bq1"], a["qn_w"], a["qn_b"], a["ident"], xs, qT)
            with nc.Block() as block:
                @block.sync
                def _(sp):
                    sp.dma_start(x2_d.rearrange("(n p) d -> p n d", p=TT), xs[:, :, :]).then_inc(x2_stored, 16)
                    sp.wait_ge(x2_stored, 16)
        attend_heads(nc, a["ctxT"], a["wkv"], a["bk"], a["affine"], a["blocks"], a["ident"], qT)
        with (nc.sbuf_tensor("x34", [TT, NTILE, D], F32) as xs, nc.sbuf_tensor("x_hi", [128, CH, NT], F32R) as x_hi,
              nc.sbuf_tensor("x_lo", [128, CH, NT], F32R) as x_lo):
            close_heads(nc, a["wo1"], a["bv"], a["bo"], x2_d, qT, xs, gate)
            route(nc, a["router_wT"], a["expert_bias"], a["ident"], xs, x_hi, x_lo, p_d)
            experts(nc, a["expert_w"], p_d, x_hi, x_lo, xs, gate, out)


def kernel(**inputs):
    import numpy as np
    import concourse.bacc as bacc
    from concourse.bass_utils import run_bass_kernel_spmd

    v = {k: np.asarray(x) for k, x in inputs.items()}

    def turned(x):
        return np.ascontiguousarray(np.swapaxes(x, -1, -2))

    def extra_first(x):
        return np.ascontiguousarray(np.concatenate([x[:, SK - DCA:], x[:, :SK - DCA]], axis=1))

    def main_groups(k, w):
        both = np.concatenate([k, w], axis=-1)
        n = both.shape[0]
        return both.reshape(n, 2, GH, 2, HD1).transpose(0, 1, 3, 2, 4).reshape(n, 2, 2 * WG)

    def extra_groups(w):
        n = w.shape[0]
        return w.reshape(n, 2, 2, GH, HD1).transpose(0, 2, 1, 3, 4).reshape(n, 2, 2 * WG)

    hadamard = np.ones((1, 1), np.float32)
    for _ in range(7):
        hadamard = np.block([[hadamard, hadamard], [hadamard, -hadamard]])
    context = extra_first(v["ctx_1024"])
    mask = extra_first(v["mask_BxS2_bf1"]).view(np.uint8)
    wkv = np.stack([main_groups(v["L1_xattn_Wk"], v["L1_xattn_Wv"]), extra_groups(v["L1_xattn_Wkv_dca"])], axis=1)
    bkv = np.stack([main_groups(v["L1_xattn_bk"][None], v["L1_xattn_bv"][None])[0],
                    extra_groups(v["L1_xattn_bkv_dca"][None])[0]])

    def expert_columns(gate, up, down):
        n = gate.shape[0]
        g, u = (turned(w).reshape(n, CH, 128, I).transpose(0, 2, 1, 3).reshape(n, 128, CH * I) for w in (gate, up))
        return np.concatenate([g, u, turned(down)], axis=2)

    arrays = {
        "x": v["x"].reshape(NT, D), "ctx": context, "ctxT": turned(context), "mask": mask,
        "gates": np.stack([v["g_xattn"], v["g_ffn"]], axis=1).reshape(4),
        "wqT": turned(v["L0_xattn_Wq"]), "wkT": turned(v["L0_xattn_Wk"]), "wvT": turned(v["L0_xattn_Wv"]),
        "wo0": v["L0_xattn_Wo"], "w1T": turned(v["L0_ffn_W1"]), "w3T": turned(v["L0_ffn_W3"]),
        "w2T": turned(v["L0_ffn_W2"]), "hadamard": hadamard, "ident": np.eye(128, dtype=np.float32),
        "wq1": v["L1_xattn_Wq"], "bq1": v["L1_xattn_bq"], "qn_w": v["L1_xattn_qn_w"], "qn_b": v["L1_xattn_qn_b"],
        "wkv": wkv, "bk": bkv[:, :, :WG].reshape(-1),
        "affine": np.stack([np.tile(v["L1_xattn_" + n], GH) for n in ("kn_w", "kn_b", "kn_dca_w", "kn_dca_b")], axis=1),
        "blocks": (np.arange(WG)[:, None] // HD1 == np.arange(GH)[None, :]).astype(np.float32),
        "bv": bkv[:, :, WG:].transpose(2, 0, 1), "wo1": v["L1_xattn_Wo"], "bo": v["L1_xattn_bo"],
        "router_wT": turned(v["L1_ffn_router_w"]), "expert_bias": v["L1_ffn_expert_bias"],
        "expert_w": np.concatenate([
            expert_columns(v["L1_ffn_shared_gate_w"][None], v["L1_ffn_shared_up_w"][None],
                           v["L1_ffn_shared_down_w"][None]),
            expert_columns(v["L1_ffn_gate_w"], v["L1_ffn_up_w"], v["L1_ffn_down_w"])]),
    }
    arrays = {f"in_{k}": np.ascontiguousarray(x) for k, x in arrays.items()}
    nc = bacc.Bacc("TRN2", target_bir_lowering=False, num_devices=1)
    tensors = {k[3:]: nc.dram_tensor(k, x.shape, mybir.dt.from_np(x.dtype), kind="ExternalInput").ap()
               for k, x in arrays.items()}
    out = nc.dram_tensor("out", (NT, D), F32, kind="ExternalOutput").ap()
    build(nc, tensors, out)
    r = run_bass_kernel_spmd(nc, [arrays], core_ids=[0])
    return r.results[0]["out"].reshape(B, S, D)
```

```python
from contextlib import ExitStack

import concourse.bass as bass
from concourse import mybir

F32 = mybir.dt.float32
F32R = mybir.dt.float32r
BF16 = mybir.dt.bfloat16
I32 = mybir.dt.int32
U8 = mybir.dt.uint8
ALU = mybir.AluOpType
ACT = mybir.ActivationFunctionType
AX = mybir.AxisListType

B, S, D = 16, 56, 256
SK, DC = 1500, 128
H0, G0, HD0 = 16, 2, 128
H1, HD1, DCA = 16, 16, 16
FF = 1024
E, I, TOPK = 32, 128, 4
ALPHA = 7.0
NT = B * S
TT = 2 * S
NTILE = NT // TT
CH = D // 128
KT, NKT = 125, SK // 125
CK, NCH = 500, SK // 500
HALF = 448
BIG = 3.0e38
EPS_LN, EPS_HEAD = 1e-5, 1e-6


def wait(eng, sem, value):
    if isinstance(value, int) and value <= 0:
        return
    eng.wait_ge(sem, value)


def upper_part(pool, out, x, ones):
    return pool.tensor_tensor(out, x, ones[0:x.shape[0], 0:1].broadcast_to(x.shape), ALU.mult)


class Chain:

    def __init__(self, eng, sem, base=0):
        self.eng, self.sem, self.base, self.n = eng, sem, base, 0

    def done(self, ins):
        ins.then_inc(self.sem, 1)
        self.n += 1

    def settle(self):
        wait(self.eng, self.sem, self.base + self.n)

    def link(self, ins):
        self.done(ins)
        self.settle()


RSQRT = 64.0 / 9.0


def rsqrt(ch, y, v, half_v, t, between=lambda k: None):
    dve = ch.eng
    ch.done(dve.tensor_scalar(half_v, v, -0.5, None, ALU.mult))
    ch.link(dve.tensor_scalar(y.bitcast(I32), v.bitcast(I32), -0.5, float(0x5F3759DF), ALU.mult, ALU.add))
    between(0)
    ch.link(dve.tensor_tensor(t, y, y, ALU.mult))
    ch.link(dve.tensor_tensor(t, t, half_v, ALU.mult))
    ch.link(dve.scalar_tensor_tensor(y, t, 1.5, y, ALU.add, ALU.mult))
    between(1)
    ch.link(dve.tensor_tensor(t, y, y, ALU.mult))
    ch.link(dve.tensor_tensor(t, t, v, ALU.mult))
    between(2)
    ch.link(dve.scalar_tensor_tensor(t, t, -10.0 / 3.0, t, ALU.add, ALU.mult))
    ch.link(dve.scalar_tensor_tensor(y, t, 5.0, y, ALU.add, ALU.mult))


def layer_norm(ch, xn, x, stats, mv, rs, tmp1, tmp2, rows, ready):
    dve = ch.eng
    tiles = x.shape[1]
    for t in range(tiles):
        ch.done(dve.bn_stats(stats[0:rows, t, :], x[:, t, :]))
    ch.settle()
    for t in range(tiles):
        ch.done(dve.bn_aggr(mv[0:rows, t, :], stats[0:rows, t, :]))
    ch.settle()
    ch.link(dve.tensor_scalar(rs[0:rows, :], mv[0:rows, :, 1], RSQRT, EPS_LN * RSQRT,
                              ALU.mult, ALU.add))
    rsqrt(ch, mv[0:rows, :, 1], rs[0:rows, :], tmp1[0:rows, :], tmp2[0:rows, :])
    for t in range(tiles):
        dve.tensor_scalar(xn[:, t, :], x[:, t, :], mv[0:rows, t, 0:1], mv[0:rows, t, 1:2],
                          ALU.subtract, ALU.mult).then_inc(ready, 1)


class Scope:

    def __init__(self, nc, ctx, tag):
        self.nc, self.ctx, self.tag = nc, ctx, tag

    def sb(self, name, shape, dt=F32):
        return self.ctx.enter_context(self.nc.sbuf_tensor(f"{self.tag}_{name}", shape, dt))

    def ps(self, name, shape, dt=F32):
        return self.ctx.enter_context(self.nc.psum_tensor(f"{self.tag}_{name}", shape, dt))

    def sem(self, name):
        return self.ctx.enter_context(self.nc.semaphore(f"{self.tag}_{name}"))


def ln_scratch(sc):
    return (sc.sb("ln_stats", [TT, NTILE, 6]), sc.sb("ln_mv", [TT, NTILE, 2]), sc.sb("ln_rs", [TT, NTILE]),
            sc.sb("ln_t1", [TT, NTILE]), sc.sb("ln_t2", [TT, NTILE]))


def project_queries(nc, x_in, wqT, wkT, ident_in, q_hi_d, q_lo_d):
    with ExitStack() as ctx:
        sc = Scope(nc, ctx, "pq")
        ident = sc.sb("ident", [128, 128])
        wqT_sb = sc.sb("wqT", [128, H0, D])
        wkT_sb = sc.sb("wkT", [128, H0 // G0, DC])
        wqk = sc.sb("wqk", [128, CH, H0, DC])
        x = sc.sb("x", [TT, NTILE, D])
        xn = sc.sb("xn", [TT, NTILE, D])
        xnT = sc.sb("xnT", [128, CH, NT])
        q_hi = sc.sb("q_hi", [128, B, H0, S], F32R)
        q_lo = sc.sb("q_lo", [128, B, H0, S], F32R)
        scratch = ln_scratch(sc)
        fold_ps = [sc.ps(f"fold{k}", [128, 512]) for k in range(2)]
        tr_ps = [sc.ps(f"tr{k}", [128, 512]) for k in range(2)]
        q_ps = [sc.ps(f"q{k}", [128, 512]) for k in range(4)]
        x_loaded, wq_loaded, wk_loaded, id_loaded = (sc.sem(n) for n in ("x_ld", "wq_ld", "wk_ld", "id_ld"))
        dve_steps, xn_ready = sc.sem("dve_steps"), sc.sem("xn_ready")
        folded, fold_kept = sc.sem("folded"), sc.sem("fold_kept")
        turned, turn_kept = sc.sem("turned"), sc.sem("turn_kept")
        q_made, q_hi_kept, q_kept, q_stored = (sc.sem(n) for n in ("q_made", "q_hi_kept", "q_kept", "q_stored"))
        NFOLD = H0 // 2
        FILLS = 2 * CH
        block = ctx.enter_context(nc.Block())

        @block.sync
        def _(sp):
            sp.dma_start(x[:, :, :], x_in.rearrange("(n p) d -> p n d", p=TT)).then_inc(x_loaded, 16)
            sp.dma_start(wkT_sb[:, :, :], wkT.rearrange("(h p) c -> p h c", p=HD0)).then_inc(wk_loaded, 16)
            sp.dma_start(wqT_sb[:, :, :], wqT.rearrange("(h p) d -> p h d", p=HD0)).then_inc(wq_loaded, 16)
            sp.dma_start(ident[:, :], ident_in).then_inc(id_loaded, 16)
            for half in range(2):
                sp.wait_ge(q_kept, H0 * (half + 1))
                bs = slice(half * B // 2, (half + 1) * B // 2)
                sp.dma_start(q_hi_d[:, bs], q_hi[:, bs].bitcast(F32)).then_inc(q_stored, 16)
                sp.dma_start(q_lo_d[:, bs], q_lo[:, bs].bitcast(F32)).then_inc(q_stored, 16)
            sp.wait_ge(q_stored, 64)

        @block.tensor
        def _(pe):
            pe.wait_ge(wk_loaded, 16)
            pe.wait_ge(wq_loaded, 16)
            for n in range(NFOLD):
                if n >= 2:
                    pe.wait_ge(fold_kept, n - 1)
                for k in range(2):
                    h = 2 * n + k
                    for c in range(CH):
                        mm = pe.matmul(fold_ps[n % 2][:, (k * CH + c) * 128:(k * CH + c + 1) * 128],
                                       wqT_sb[:, h, c * 128:(c + 1) * 128], wkT_sb[:, h // G0, :],
                                       start=True, stop=True)
                mm.then_inc(folded, 1)
            pe.wait_ge(id_loaded, 16)
            for f in range(FILLS):
                if f >= 2:
                    pe.wait_ge(turn_kept, f - 1)
                half, c = f // CH, f % CH
                pe.wait_ge(xn_ready, 4 * (half + 1))
                for k in range(4):
                    mm = pe.transpose(tr_ps[f % 2][:, k * TT:(k + 1) * TT],
                                      xn[:, 4 * half + k, c * 128:(c + 1) * 128], ident[0:TT, 0:TT])
                mm.then_inc(turned, 1)
            pe.wait_ge(fold_kept, NFOLD)
            for half in range(2):
                pe.wait_ge(turn_kept, CH * (half + 1))
                for h in range(H0):
                    n = half * H0 + h
                    if n >= 4:
                        pe.wait_ge(q_kept, n - 3)
                    for c in range(CH):
                        mm = pe.matmul(q_ps[n % 4][:, 0:HALF], wqk[:, c, h, :],
                                       xnT[:, c, half * HALF:(half + 1) * HALF], start=(c == 0), stop=(c == CH - 1))
                    mm.then_inc(q_made, 1)

        @block.scalar
        def _(act):
            for n in range(NFOLD):
                act.wait_ge(folded, n + 1)
                act.copy(wqk[:, :, 2 * n:2 * n + 2, :].rearrange("p c k n -> p k c n"),
                         fold_ps[n % 2][:, :].rearrange("p (k c n) -> p k c n", k=2, c=CH)).then_inc(fold_kept, 1)
            for f in range(FILLS):
                act.wait_ge(turned, f + 1)
                half, c = f // CH, f % CH
                act.copy(xnT[:, c, half * HALF:(half + 1) * HALF], tr_ps[f % 2][:, 0:HALF]).then_inc(turn_kept, 1)
            for n in range(2 * H0):
                half, h = n // H0, n % H0
                act.wait_ge(q_made, n + 1)
                act.copy(q_hi[:, half * B // 2:(half + 1) * B // 2, h, :],
                         q_ps[n % 4][:, 0:HALF].rearrange("p (b t) -> p b t", t=S)).then_inc(q_hi_kept, 1)

        @block.vector
        def _(dve):
            ch = Chain(dve, dve_steps)
            dve.wait_ge(x_loaded, 16)
            layer_norm(ch, xn[:, :, :], x[:, :, :], *scratch, TT, xn_ready)
            for n in range(2 * H0):
                half, h = n // H0, n % H0
                bs = slice(half * B // 2, (half + 1) * B // 2)
                dve.wait_ge(q_hi_kept, n + 1)
                dve.tensor_tensor(q_lo[:, bs, h, :], q_ps[n % 4][:, 0:HALF].rearrange("p (b t) -> p b t", t=S),
                                  q_hi[:, bs, h, :].bitcast(F32), ALU.subtract).then_inc(q_kept, 1)


def three_passes(pe, out, w_hi, w_lo, m_hi, m_lo, first, last):
    pe.matmul(out, w_hi, m_hi, start=first, stop=False)
    pe.matmul(out, w_hi, m_lo, start=False, stop=False)
    return pe.matmul(out, w_lo, m_hi, start=False, stop=last)


UNIT = 4
QT = NKT // UNIT


def attend_context(nc, ctx_in, ctxT_in, mask_in, ident_in, q_hi_d, q_lo_d, o_d):
    SCALE = float(HD0) ** -0.5
    NS = 3
    STEPS = 2 * 2 * UNIT
    with ExitStack() as ctx:
        sc = Scope(nc, ctx, "a0")
        ident = sc.sb("ident", [128, 128])
        ones = sc.sb("ones", [128, 128])
        raw = sc.sb("raw", [KT, NKT, DC])
        rawT = sc.sb("rawT", [DC, SK])
        c_hi = [sc.sb(f"c_hi{p}", [KT, NKT, DC], F32R) for p in range(2)]
        c_lo = [sc.sb(f"c_lo{p}", [KT, NKT, DC], F32R) for p in range(2)]
        cT_hi = [sc.sb(f"cT_hi{p}", [DC, SK], F32R) for p in range(2)]
        cT_lo = [sc.sb(f"cT_lo{p}", [DC, SK], F32R) for p in range(2)]
        q_hi = [sc.sb(f"q_hi{p}", [DC, H0 * S], F32R) for p in range(2)]
        q_lo = [sc.sb(f"q_lo{p}", [DC, H0 * S], F32R) for p in range(2)]
        mask_u8 = sc.sb("mask_u8", [TT, SK], U8)
        mask_add = [sc.sb(f"mask_add{p}", [TT, SK]) for p in range(2)]
        any_key = sc.sb("any_key", [TT, 2])
        probs = [sc.sb(f"probs{p}", [TT, SK]) for p in range(2)]
        pT_hi = [sc.sb(f"pT_hi{p}", [KT, NKT, HALF], F32R) for p in range(2)]
        pT_lo = [sc.sb(f"pT_lo{p}", [KT, NKT, HALF], F32R) for p in range(2)]
        part_min = sc.sb("part_min", [TT, 2, NCH])
        row_min = sc.sb("row_min", [TT, 2])
        carrier = sc.sb("carrier", [1, 2, NCH])
        sums = sc.sb("sums", [TT, 2, UNIT])
        inv = sc.sb("inv", [TT, UNIT])
        inv_diag = sc.sb("inv_diag", [TT, UNIT, TT])
        inv_all = sc.sb("inv_all", [128, HALF])
        o_sb = sc.sb("o", [DC, HALF])
        s_ps = [sc.ps(f"s{k}", [128, 512]) for k in range(NS)]
        t_ps = [sc.ps(f"t{k}", [128, 512]) for k in range(NS)]
        o_ps = sc.ps("o_ps", [128, 512])
        i_ps = sc.ps("i_ps", [128, 512])

        id_loaded, ones_set = sc.sem("id_ld"), sc.sem("ones")
        ctx_loaded, mask_loaded = sc.sem("ctx_ld"), sc.sem("mask_ld")
        q_loaded = [sc.sem(f"q_ld{p}") for p in range(2)]
        pool_steps = sc.sem("pool_steps")
        scored, score_kept = sc.sem("scored"), sc.sem("score_kept")
        row_max, dve_steps = sc.sem("row_max"), sc.sem("dve_steps")
        probs_made = sc.sem("probs_made")
        turned, turn_hi, turn_kept = sc.sem("turned"), sc.sem("turn_hi"), sc.sem("turn_kept")
        diag_made, inv_spread, inv_kept = sc.sem("diag_made"), sc.sem("inv_spread"), sc.sem("inv_kept")
        summed, o_kept, o_stored = sc.sem("summed"), sc.sem("o_kept"), sc.sem("o_stored")
        POOL_B = 5
        block = ctx.enter_context(nc.Block())

        def bodies(eng, body, last):
            body(0, True)
            with eng.Fori(1, B // 2) as i:
                body(i, False)
            last()

        @block.sync
        def _(sp):
            sp.dma_start(ident[:, :], ident_in).then_inc(id_loaded, 16)

            def load(i, p):
                b = 2 * i + p
                wait(sp, pool_steps, POOL_B * b)
                sp.dma_start(rawT[:, :], ctxT_in[bass.ds(b, 1)].rearrange("b c k -> c (b k)")).then_inc(ctx_loaded, 16)
                sp.dma_start(raw[:, :, :], ctx_in[bass.ds(b, 1)].rearrange("b (n p) c -> p (b n) c", p=KT)
                             ).then_inc(ctx_loaded, 16)
                sp.dma_start(mask_u8[:, :], mask_in[bass.ds(b, 1)].rearrange("b k -> (b k)").partition_broadcast(TT)
                             ).then_inc(mask_loaded, 16)
                wait(sp, scored, 8 * NCH * (b - 1))
                sp.dma_start(q_hi[p][:, :].bitcast(F32), q_hi_d[:, bass.ds(b, 1)].rearrange("c b h t -> c (b h t)")
                             ).then_inc(q_loaded[p], 16)
                sp.dma_start(q_lo[p][:, :].bitcast(F32), q_lo_d[:, bass.ds(b, 1)].rearrange("c b h t -> c (b h t)")
                             ).then_inc(q_loaded[p], 16)

            def body(i, first):
                for p in range(2):
                    load(i, p)

            bodies(sp, body, lambda: None)

        @block.gpsimd
        def _(pool):
            pool.memset(ones[:, :], 1.0).then_inc(ones_set, 1)
            pool.wait_ge(ones_set, 1)

            def split(i, p):
                b = 2 * i + p
                done = POOL_B * b
                pool.wait_ge(ctx_loaded, 32 * (b + 1))
                pool.wait_ge(mask_loaded, 16 * (b + 1))
                wait(pool, scored, 8 * NCH * (b - 1))
                wait(pool, score_kept, 8 * NCH * (b - 1))
                upper_part(pool, cT_hi[p][:, :], rawT[:, :], ones).then_inc(pool_steps, 1)
                pool.tensor_scalar(mask_add[p][:, :], mask_u8[:, :], 1.0, BIG, ALU.subtract, ALU.mult
                                   ).then_inc(pool_steps, 1)
                pool.wait_ge(pool_steps, done + 1)
                pool.tensor_tensor(cT_lo[p][:, :], rawT[:, :], cT_hi[p][:, :].bitcast(F32), ALU.subtract
                                   ).then_inc(pool_steps, 1)
                wait(pool, summed, 2 * (b - 1))
                upper_part(pool, c_hi[p][:, :, :].rearrange("p n c -> p (n c)"),
                           raw[:, :, :].rearrange("p n c -> p (n c)"), ones).then_inc(pool_steps, 1)
                pool.wait_ge(pool_steps, done + 4)
                pool.tensor_tensor(c_lo[p][:, :, :], raw[:, :, :], c_hi[p][:, :, :].bitcast(F32), ALU.subtract
                                   ).then_inc(pool_steps, 1)

            def body(i, first):
                for p in range(2):
                    split(i, p)

            bodies(pool, body, lambda: None)

        @block.tensor
        def _(pe):
            pe.wait_ge(id_loaded, 16)
            pe.wait_ge(ones_set, 1)

            def scores(g, s):
                p, r = s // (2 * UNIT), s % (2 * UNIT)
                rows = slice(r * TT, (r + 1) * TT)
                for c in range(NCH):
                    n = NCH * g + c
                    slot = c
                    wait(pe, score_kept, n - NS + 1)
                    keys = slice(c * CK, (c + 1) * CK)
                    three_passes(pe, s_ps[slot][0:TT, 0:CK], q_hi[p][:, rows], q_lo[p][:, rows],
                                 cT_hi[p][:, keys], cT_lo[p][:, keys], True, True).then_inc(scored, 1)

            def turn(g, s):
                pe.wait_ge(probs_made, g + 1)
                for f in range(NCH):
                    n = NCH * g + f
                    wait(pe, turn_kept, n - NS + 1)
                    for k in range(4):
                        j = 4 * f + k
                        mm = pe.transpose(t_ps[f][0:KT, k * TT:(k + 1) * TT],
                                          probs[s % 2][:, j * KT:(j + 1) * KT], ident[0:TT, 0:TT])
                    mm.then_inc(turned, 1)

            def spread(u):
                pe.wait_ge(diag_made, u + 1)
                wait(pe, inv_kept, u)
                pe.matmul(i_ps[:, 0:HALF], ones[0:TT, :], inv_diag[:, :, :].rearrange("p k t -> p (k t)"),
                          start=True, stop=True).then_inc(inv_spread, 1)
                wait(pe, o_kept, u)

            def weigh(u, s, r):
                p, half = s // (2 * UNIT), (s // UNIT) % 2
                for j in range(QT * r, QT * (r + 1)):
                    if j % 4 == 0 or j == QT * r:
                        pe.wait_ge(turn_kept, NCH * UNIT * u + NCH * (UNIT - 1) + j // 4 + 1)
                    mm = three_passes(pe, o_ps[:, 0:HALF], c_hi[p][:, j, :], c_lo[p][:, j, :],
                                      pT_hi[half][:, j, :], pT_lo[half][:, j, :], j == 0, j == NKT - 1)
                if r == UNIT - 1:
                    mm.then_inc(summed, 1)

            def body(i, first):
                for s in range(STEPS):
                    g, r = STEPS * i + s, s % UNIT
                    if s % (2 * UNIT) == 0:
                        p = s // (2 * UNIT)
                        b = 2 * i + p
                        pe.wait_ge(pool_steps, POOL_B * b + 3)
                        pe.wait_ge(q_loaded[p], 32 * (i + 1))
                    scores(g, s)
                    if not (first and s == 0):
                        turn(g - 1, (s - 1) % STEPS)
                    if not (first and s < UNIT):
                        u = STEPS // UNIT * i + s // UNIT - 1
                        if r == 0:
                            spread(u)
                            pe.wait_ge(pool_steps, POOL_B * (2 * i + (s // UNIT + 1) // 2))
                        weigh(u, (s - UNIT) % STEPS, r)

            def last():
                turn(8 * B - 1, STEPS - 1)
                spread(2 * B - 1)
                for r in range(UNIT):
                    weigh(2 * B - 1, STEPS - 1, r)

            bodies(pe, body, last)

        @block.scalar
        def _(act):
            def upper(g, s, u):
                half, r = (s // UNIT) % 2, s % UNIT
                for f in range(NCH):
                    act.wait_ge(turned, NCH * g + f + 1)
                    if f == 0 and r == 0:
                        wait(act, summed, u - 1)
                    act.copy(pT_hi[half][:, 4 * f:4 * f + 4, r * TT:(r + 1) * TT],
                             t_ps[f][0:KT, 0:HALF].rearrange("p (k t) -> p k t", t=TT)
                             ).then_inc(turn_hi, 1)

            def spread(u):
                act.wait_ge(inv_spread, u + 1)
                wait(act, o_kept, u)
                act.copy(inv_all[:, :], i_ps[:, 0:HALF]).then_inc(inv_kept, 1)

            def store(u, b, half):
                act.wait_ge(o_kept, u + 1)
                act.dma_start(o_d[:, half * 8:half * 8 + 8, bass.ds(b * S, S)],
                              o_sb[:, :].rearrange("c (h t) -> c h t", t=S)).then_inc(o_stored, 16)

            def body(i, first):
                for s in range(STEPS):
                    g = STEPS * i + s
                    if not (first and s == 0):
                        upper(g - 1, (s - 1) % STEPS, STEPS // UNIT * i + (s - 1) // UNIT)
                    if s % UNIT == 1 and not (first and s < 2 * UNIT):
                        v = s // UNIT - 2
                        store(STEPS // UNIT * i + v, 2 * i + v // 2, v % 2)
                    act.wait_ge(row_max, g + 1)
                    act.activation(probs[s % 2][:, :], probs[s % 2][:, :], ACT.Exp, scale=-1.0,
                                   bias=row_min[:, s % 2:s % 2 + 1],
                                   accum_out=sums[:, (s // UNIT) % 2, s % UNIT:s % UNIT + 1]
                                   ).then_inc(probs_made, 1)
                    if s % UNIT == 0 and not (first and s == 0):
                        spread(STEPS // UNIT * i + s // UNIT - 1)

            def last():
                store(2 * B - 2, B - 1, 0)
                upper(8 * B - 1, STEPS - 1, 2 * B - 1)
                spread(2 * B - 1)
                store(2 * B - 1, B - 1, 1)
                act.wait_ge(o_stored, 16 * 2 * B)

            bodies(act, body, last)

        @block.vector
        def _(dve):
            BATCH_N, UNIT_N = 2, 2
            PER_BODY = 2 * BATCH_N + (STEPS // UNIT) * UNIT_N

            def masked(g, s, i, ch):
                p = s // (2 * UNIT)
                wait(dve, turned, NCH * (g - 1))
                for c in range(NCH):
                    keys = slice(c * CK, (c + 1) * CK)
                    dve.wait_ge(scored, NCH * g + c + 1)
                    dve.memset(carrier[:, s % 2, c:c + 1], 0.0)
                    ins = dve.tensor_tensor_reduce(
                        probs[s % 2][:, keys], s_ps[c][0:TT, 0:CK], mask_add[p][:, keys],
                        -SCALE, BIG, ALU.add, ALU.min, part_min[:, s % 2, c:c + 1])
                    ins.then_inc(score_kept, 1)
                dve.wait_ge(score_kept, NCH * g + NCH)
                dve.tensor_reduce(row_min[:, s % 2:s % 2 + 1], part_min[:, s % 2, :], AX.X, ALU.min
                                  ).then_inc(row_max, 1)

            def rest(g, s):
                half, r = (s // UNIT) % 2, s % UNIT
                for f in range(NCH):
                    dve.wait_ge(turn_hi, NCH * g + f + 1)
                    rows = slice(r * TT, (r + 1) * TT)
                    dve.tensor_tensor(pT_lo[half][:, 4 * f:4 * f + 4, rows],
                                      t_ps[f][0:KT, 0:HALF].rearrange("p (k t) -> p k t", t=TT),
                                      pT_hi[half][:, 4 * f:4 * f + 4, rows].bitcast(F32), ALU.subtract
                                      ).then_inc(turn_kept, 1)

            def invert(u, s, ch):
                p, half = s // (2 * UNIT), (s // UNIT) % 2
                ch.link(dve.reciprocal(inv[:, :], sums[:, half, :]))
                ch.link(dve.tensor_scalar(inv[:, :], inv[:, :], any_key[:, p:p + 1], None, ALU.mult))
                wait(dve, inv_spread, u)
                dve.tensor_tensor(inv_diag[:, :, :],
                                  ident[0:TT, 0:TT].rearrange("p (a t) -> p a t", a=1).broadcast_to([TT, UNIT, TT]),
                                  inv[:, :].rearrange("p (k a) -> p k a", a=1).broadcast_to([TT, UNIT, TT]),
                                  ALU.mult).then_inc(diag_made, 1)

            def finish(u):
                dve.wait_ge(summed, u + 1)
                dve.wait_ge(inv_kept, u + 1)
                wait(dve, o_stored, 16 * u)
                dve.tensor_tensor(o_sb[:, :], o_ps[:, 0:HALF], inv_all[:, :], ALU.mult).then_inc(o_kept, 1)

            def body(i, first):
                base = PER_BODY * i - (0 if first else UNIT_N)
                ch = Chain(dve, dve_steps, base)
                for s in range(STEPS):
                    g = STEPS * i + s
                    if s % (2 * UNIT) == 0:
                        p = s // (2 * UNIT)
                        b = 2 * i + p
                        dve.wait_ge(pool_steps, POOL_B * b + 3)
                    masked(g, s, i, ch)
                    if s % (2 * UNIT) == 1:
                        p = s // (2 * UNIT)
                        ch.link(dve.tensor_reduce(any_key[:, p:p + 1], mask_add[p][:, :], AX.X, ALU.max))
                        ch.link(dve.tensor_scalar(any_key[:, p:p + 1], any_key[:, p:p + 1], 0.0, None, ALU.is_ge))
                    if s % UNIT == 0 and not (first and s == 0):
                        u = STEPS // UNIT * i + s // UNIT - 1
                        dve.wait_ge(probs_made, g)
                        invert(u, (s - 1) % STEPS, ch)
                    if s % UNIT == 0 and not (first and s < 2 * UNIT):
                        finish(STEPS // UNIT * i + s // UNIT - 2)
                    if not (first and s == 0):
                        rest(g - 1, (s - 1) % STEPS)

            def last():
                ch = Chain(dve, dve_steps, PER_BODY * (B // 2) - UNIT_N)
                finish(2 * B - 2)
                dve.wait_ge(probs_made, 8 * B)
                invert(2 * B - 1, STEPS - 1, ch)
                rest(8 * B - 1, STEPS - 1)
                finish(2 * B - 1)

            bodies(dve, body, last)


def close_attention(nc, o_d, x_in, wvT, wo, gates_in, xs, gate):
    with ExitStack() as ctx:
        sc = Scope(nc, ctx, "c0")
        wvT_sb = sc.sb("wvT", [128, H0 // G0, DC])
        wo_sb = sc.sb("wo", [128, H0, D])
        wvo = sc.sb("wvo", [DC, H0, D])
        oT = sc.sb("oT", [DC, H0, NT])
        x = sc.sb("x", [TT, NTILE, D])
        gates = sc.sb("gates", [TT, 4])
        f_ps = [sc.ps(f"f{k}", [128, 512]) for k in range(4)]
        y_ps = [sc.ps(f"y{k}", [128, 512]) for k in range(4)]
        w_loaded, x_loaded, g_loaded = sc.sem("w_ld"), sc.sem("x_ld"), sc.sem("g_ld")
        o_loaded = [sc.sem(f"o_ld{k}") for k in range(4)]
        folded, fold_kept, gate_made = sc.sem("folded"), sc.sem("fold_kept"), sc.sem("gate_made")
        projected, added = sc.sem("projected"), sc.sem("added")
        block = ctx.enter_context(nc.Block())

        @block.sync
        def _(sp):
            sp.dma_start(wvT_sb[:, :, :], wvT.rearrange("(g p) c -> p g c", p=HD0)).then_inc(w_loaded, 16)
            sp.dma_start(wo_sb[:, :, :], wo.rearrange("(h p) d -> p h d", p=HD0)).then_inc(w_loaded, 16)
            for k in range(4):
                cols = slice(2 * k * TT, 2 * (k + 1) * TT)
                sp.dma_start(oT[:, :, cols], o_d[:, :, cols]).then_inc(o_loaded[k], 16)
            sp.dma_start(x[:, :, :], x_in.rearrange("(n p) d -> p n d", p=TT)).then_inc(x_loaded, 16)
            sp.dma_start(gates[:, :], gates_in.partition_broadcast(TT)).then_inc(g_loaded, 16)

        @block.tensor
        def _(pe):
            pe.wait_ge(w_loaded, 32)
            for n in range(H0 // 2):
                if n >= 4:
                    pe.wait_ge(fold_kept, n - 3)
                for k in range(2):
                    h = 2 * n + k
                    mm = pe.matmul(f_ps[n % 4][:, k * D:(k + 1) * D], wvT_sb[:, h // G0, :], wo_sb[:, h, :],
                                   start=True, stop=True)
                mm.then_inc(folded, 1)
            pe.wait_ge(fold_kept, H0 // 2)
            for t in range(NTILE):
                pe.wait_ge(o_loaded[t // 2], 16)
                if t >= 4:
                    pe.wait_ge(added, t - 3)
                for h in range(H0):
                    mm = pe.matmul(y_ps[t % 4][0:TT, 0:D], oT[:, h, t * TT:(t + 1) * TT], wvo[:, h, :],
                                   start=(h == 0), stop=(h == H0 - 1))
                mm.then_inc(projected, 1)

        @block.scalar
        def _(act):
            act.wait_ge(g_loaded, 16)
            act.activation(gate[:, :], gates[:, :], ACT.Tanh).then_inc(gate_made, 1)
            for n in range(H0 // 2):
                act.wait_ge(folded, n + 1)
                act.copy(wvo[:, 2 * n:2 * n + 2, :], f_ps[n % 4][:, :].rearrange("p (k d) -> p k d", k=2)
                         ).then_inc(fold_kept, 1)

        @block.vector
        def _(dve):
            dve.wait_ge(gate_made, 1)
            dve.wait_ge(x_loaded, 16)
            for t in range(NTILE):
                dve.wait_ge(projected, t + 1)
                dve.scalar_tensor_tensor(xs[:, t, :], y_ps[t % 4][0:TT, 0:D], gate[:, 0:1], x[:, t, :],
                                         ALU.mult, ALU.add).then_inc(added, 1)


def turn_tokens(pe, act, xn, xnT, banks, ident, ready, turned, kept):
    if pe is not None:
        for f in range(2 * CH):
            half, c = f // CH, f % CH
            pe.wait_ge(ready, 4 * (half + 1))
            if f >= 2:
                pe.wait_ge(kept, f - 1)
            for k in range(4):
                mm = pe.transpose(banks[f % 2][:, k * TT:(k + 1) * TT], xn[:, 4 * half + k, c * 128:(c + 1) * 128],
                                  ident[0:TT, 0:TT])
            mm.then_inc(turned, 1)
    if act is not None:
        for f in range(2 * CH):
            half, c = f // CH, f % CH
            act.wait_ge(turned, f + 1)
            act.copy(xnT[:, c, half * HALF:(half + 1) * HALF], banks[f % 2][:, 0:HALF]).then_inc(kept, 1)


def feed_forward(nc, w1T, w3T, w2T, hadamard_in, ident_in, xs, gate):
    NH = FF // 128
    with ExitStack() as ctx:
        sc = Scope(nc, ctx, "ff")
        ident = sc.sb("ident", [128, 128])
        had = sc.sb("had", [128, 128])
        w1 = sc.sb("w1", [128, CH, FF])
        w3 = sc.sb("w3", [128, CH, FF])
        w2 = sc.sb("w2", [128, NH, D])
        fly = [sc.sb(f"fly{k}", [128, NH, D]) for k in range(2)]
        xn = sc.sb("xn", [TT, NTILE, D])
        xnT = sc.sb("xnT", [128, CH, NT])
        act_g = [sc.sb(f"act_g{k}", [128, HALF]) for k in range(2)]
        hidden = sc.sb("hidden", [128, NH, NT])
        scratch = ln_scratch(sc)
        banks = [sc.ps(f"b{k}", [128, 512]) for k in range(8)]
        in_loaded, w2_loaded, id_loaded, w_loaded = (sc.sem(n) for n in ("in_ld", "w2_ld", "id_ld", "w_ld"))
        dve_steps, xn_ready = sc.sem("dve_steps"), sc.sem("xn_ready")
        mixed, mix_kept = sc.sem("mixed"), sc.sem("mix_kept")
        turned, turn_kept = sc.sem("turned"), sc.sem("turn_kept")
        gate_up, silu_made, hidden_made = sc.sem("gate_up"), sc.sem("silu_made"), sc.sem("hidden_made")
        w2_ready = sc.sem("w2_ready")
        projected, added = sc.sem("projected"), sc.sem("added")
        block = ctx.enter_context(nc.Block())

        @block.sync
        def _(sp):
            sp.dma_start(ident[:, :], ident_in).then_inc(id_loaded, 16)
            sp.dma_start(had[:, :], hadamard_in).then_inc(w2_loaded, 16)
            sp.dma_start(w2[:, :, :], w2T.rearrange("(k p) d -> p k d", p=128)).then_inc(w2_loaded, 16)
            sp.dma_start(w1[:, :, :], w1T.rearrange("(c p) h -> p c h", p=128)).then_inc(w_loaded, 16)
            sp.dma_start(w3[:, :, :], w3T.rearrange("(c p) h -> p c h", p=128)).then_inc(w_loaded, 16)

        @block.tensor
        def _(pe):
            pe.wait_ge(id_loaded, 16)
            pe.wait_ge(w2_loaded, 32)
            for k in range(NH // 2):
                for c in range(2):
                    mm = pe.matmul(banks[4 + k][:, c * D:(c + 1) * D], had[:, :], w2[:, 2 * k + c, :],
                                   start=True, stop=True)
                mm.then_inc(mixed, 1)
            turn_tokens(pe, None, xn, xnT, banks[0:2], ident, xn_ready, turned, turn_kept)
            pe.wait_ge(w_loaded, 32)
            pe.wait_ge(turn_kept, 2 * CH)
            pe.wait_ge(mix_kept, NH // 2)
            for n in range(2 * NH):
                half, k = n // NH, n % NH
                if n >= 4:
                    pe.wait_ge(hidden_made, n - 3)
                for w, bank in ((w1, banks[n % 4]), (w3, banks[4 + n % 4])):
                    for c in range(CH):
                        mm = pe.matmul(bank[:, 0:HALF], w[:, c, k * 128:(k + 1) * 128],
                                       xnT[:, c, half * HALF:(half + 1) * HALF], start=(c == 0), stop=(c == CH - 1))
                mm.then_inc(gate_up, 1)
            pe.wait_ge(w2_ready, 1)
            for t in range(NTILE):
                pe.wait_ge(hidden_made, NH * (t // 4 + 1) if t >= 4 else 2 * NH)
                if t >= 4:
                    pe.wait_ge(added, t - 3)
                for k in range(NH):
                    mm = pe.matmul(banks[t % 4][0:TT, 0:D], hidden[:, k, t * TT:(t + 1) * TT], fly[1][:, k, :],
                                   start=(k == 0), stop=(k == NH - 1))
                mm.then_inc(projected, 1)

        @block.scalar
        def _(act):
            for k in range(NH // 2):
                act.wait_ge(mixed, k + 1)
                act.mul(fly[0][:, 2 * k:2 * k + 2, :], banks[4 + k][:, :].rearrange("p (c d) -> p c d", c=2),
                        float(FF) ** -0.5).then_inc(mix_kept, 1)
            turn_tokens(None, act, xn, xnT, banks[0:2], ident, xn_ready, turned, turn_kept)
            for n in range(2 * NH):
                act.wait_ge(gate_up, n + 1)
                if n >= 2:
                    act.wait_ge(hidden_made, n - 1)
                act.activation(act_g[n % 2][:, :], banks[n % 4][:, 0:HALF], ACT.Silu).then_inc(silu_made, 1)

        @block.vector
        def _(dve):
            ch = Chain(dve, dve_steps)
            layer_norm(ch, xn[:, :, :], xs[:, :, :], *scratch, TT, xn_ready)
            dve.wait_ge(mix_kept, NH // 2)
            src, dst = 0, 1
            for st in range(3):
                w = 1 << st
                a = fly[src][:, :, :].rearrange("p (n s w) d -> p n s (w d)", s=2, w=w)
                b = fly[dst][:, :, :].rearrange("p (n s w) d -> p n s (w d)", s=2, w=w)
                ins1 = dve.tensor_tensor(b[:, :, 0, :], a[:, :, 0, :], a[:, :, 1, :], ALU.add)
                ins2 = dve.tensor_tensor(b[:, :, 1, :], a[:, :, 0, :], a[:, :, 1, :], ALU.subtract)
                ch.done(ins1)
                if st < 2:
                    ch.link(ins2)
                else:
                    ch.settle()
                    ins2.then_inc(w2_ready, 1)
                src, dst = dst, src
            for n in range(2 * NH):
                half, k = n // NH, n % NH
                dve.wait_ge(silu_made, n + 1)
                dve.tensor_tensor(hidden[:, k, half * HALF:(half + 1) * HALF], banks[4 + n % 4][:, 0:HALF],
                                  act_g[n % 2][:, :], ALU.mult).then_inc(hidden_made, 1)
            for t in range(NTILE):
                dve.wait_ge(projected, t + 1)
                dve.scalar_tensor_tensor(xs[:, t, :], banks[t % 4][0:TT, 0:D], gate[:, 1:2], xs[:, t, :],
                                         ALU.mult, ALU.add).then_inc(added, 1)


GH = H1 // 2
WG = GH * HD1


def project_heads(nc, wq, bq, qn_w, qn_b, ident_in, xs, qT):
    NG = NTILE * H1
    with ExitStack() as ctx:
        sc = Scope(nc, ctx, "p1")
        ident = sc.sb("ident", [128, 128])
        wq_sb = sc.sb("wq", [128, CH, D])
        bq_sb = sc.sb("bq", [TT, D])
        w_sb = sc.sb("w", [TT, HD1])
        b_sb = sc.sb("b", [TT, HD1])
        xn = sc.sb("xn", [TT, NTILE, D])
        xnT = sc.sb("xnT", [128, CH, NT])
        q = sc.sb("q", [TT, NTILE, D])
        sq = sc.sb("sq", [TT, NTILE, D])
        mean, var, r, t1, t2 = (sc.sb(n, [TT, NG]) for n in ("mean", "var", "r", "t1", "t2"))
        scratch = ln_scratch(sc)
        banks = [sc.ps(f"b{k}", [128, 512]) for k in range(6)]
        loaded, v_loaded = sc.sem("ld"), sc.sem("v_ld")
        dve_steps, xn_ready = sc.sem("dve_steps"), sc.sem("xn_ready")
        turned, turn_kept = sc.sem("turned"), sc.sem("turn_kept")
        projected, q_kept, q_ready = sc.sem("projected"), sc.sem("q_kept"), sc.sem("q_ready")
        q_turned, q_turn_kept = sc.sem("q_turned"), sc.sem("q_turn_kept")
        block = ctx.enter_context(nc.Block())

        @block.sync
        def _(sp):
            sp.dma_start(ident[:, :], ident_in).then_inc(loaded, 16)
            sp.dma_start(wq_sb[:, :, :], wq.rearrange("(c p) d -> p c d", p=128)).then_inc(loaded, 16)
            sp.dma_start(bq_sb[:, :], bq.partition_broadcast(TT)).then_inc(v_loaded, 16)
            sp.dma_start(w_sb[:, :], qn_w.partition_broadcast(TT)).then_inc(v_loaded, 16)
            sp.dma_start(b_sb[:, :], qn_b.partition_broadcast(TT)).then_inc(v_loaded, 16)

        @block.tensor
        def _(pe):
            pe.wait_ge(loaded, 32)
            turn_tokens(pe, None, xn, xnT, banks[0:2], ident, xn_ready, turned, turn_kept)
            for t in range(NTILE):
                pe.wait_ge(turn_kept, CH * (t // 4 + 1))
                if t >= 4:
                    pe.wait_ge(q_kept, t - 3)
                for c in range(CH):
                    mm = pe.matmul(banks[2 + t % 4][0:TT, 0:D], xnT[:, c, t * TT:(t + 1) * TT], wq_sb[:, c, :],
                                   start=(c == 0), stop=(c == CH - 1))
                mm.then_inc(projected, 1)
            turn_tokens(pe, None, q, qT, banks[0:2], ident, q_ready, q_turned, q_turn_kept)

        @block.scalar
        def _(act):
            turn_tokens(None, act, xn, xnT, banks[0:2], ident, xn_ready, turned, turn_kept)
            turn_tokens(None, act, q, qT, banks[0:2], ident, q_ready, q_turned, q_turn_kept)

        @block.vector
        def _(dve):
            ch = Chain(dve, dve_steps)
            layer_norm(ch, xn[:, :, :], xs[:, :, :], *scratch, TT, xn_ready)
            dve.wait_ge(v_loaded, 48)
            for t in range(NTILE):
                dve.wait_ge(projected, t + 1)
                dve.tensor_tensor(q[:, t, :], banks[2 + t % 4][0:TT, 0:D], bq_sb[:, :], ALU.add).then_inc(q_kept, 1)
            dve.wait_ge(q_kept, NTILE)

            def heads(x):
                return x[:, :, :].rearrange("p n (h e) -> p (n h) e", e=HD1)

            def of_head(x):
                return x[:, :].rearrange("p (g a) -> p g a", a=1).broadcast_to([TT, NG, HD1])

            def of_column(x):
                return x[:, :].rearrange("p (a e) -> p a e", a=1).broadcast_to([TT, NG, HD1])

            ch.link(dve.tensor_reduce(mean[:, :], heads(q), AX.X, ALU.add))
            ch.link(dve.tensor_scalar(mean[:, :], mean[:, :], 1.0 / HD1, None, ALU.mult))
            ch.link(dve.tensor_tensor(heads(q), heads(q), of_head(mean), ALU.subtract))
            ch.link(dve.tensor_tensor(heads(sq), heads(q), heads(q), ALU.mult))
            ch.link(dve.tensor_reduce(var[:, :], heads(sq), AX.X, ALU.add))
            ch.link(dve.tensor_scalar(var[:, :], var[:, :], RSQRT / HD1, EPS_HEAD * RSQRT,
                                          ALU.mult, ALU.add))
            rsqrt(ch, r[:, :], var[:, :], t1[:, :], t2[:, :])
            ch.link(dve.tensor_tensor(heads(q), heads(q), of_head(r), ALU.mult))
            ch.link(dve.tensor_tensor(heads(q), heads(q), of_column(w_sb), ALU.mult))
            ch.link(dve.tensor_tensor(heads(q), heads(q), of_column(b_sb), ALU.add))
            dve.sem_inc(q_ready, NTILE)


def attend_heads(nc, ctxT_in, wkv, bk, affine_in, blocks_in, ident_in, qT):
    SCALE = float(HD1) ** -0.5
    NS = 3
    STEPS = 2 * UNIT
    with ExitStack() as ctx:
        sc = Scope(nc, ctx, "a1")
        ident = sc.sb("ident", [128, 128])
        w_hi = sc.sb("w_hi", [DC, 2, 2 * WG], F32R)
        w_lo = sc.sb("w_lo", [DC, 2, 2 * WG], F32R)
        w_dca = sc.sb("w_dca", [DC, 2, 2 * WG])
        bias_rows = sc.sb("bias_rows", [96, 2, 2, WG], BF16)
        one_rows = sc.sb("one_rows", [96, 128], BF16)
        affine = sc.sb("affine", [128, 4])
        blocks = sc.sb("blocks", [128, GH])
        ones = sc.sb("ones", [128, 128])

        with ExitStack() as prep:
            pc = Scope(nc, prep, "w1")
            w = pc.sb("w", [DC, 2, 2, 2 * WG])
            bias = pc.sb("bias", [96, 2, 2, WG])
            part = pc.sb("part", [96, 2, 2, WG], BF16)
            mean = pc.sb("mean", [128, 4, GH])
            bmean = pc.sb("bmean", [96, 4, GH])
            loaded, b_loaded, cleared = pc.sem("ld"), pc.sem("b_ld"), pc.sem("cleared")
            dve_steps, consts = pc.sem("dve_steps"), pc.sem("consts")
            block = prep.enter_context(nc.Block())

            @block.sync
            def _(sp):
                sp.dma_start(w[:, :, :, :], wkv).then_inc(loaded, 16)
                sp.dma_start(ident[:, :], ident_in).then_inc(loaded, 16)
                sp.dma_start(affine[:, :], affine_in).then_inc(loaded, 16)
                sp.dma_start(blocks[:, :], blocks_in).then_inc(loaded, 16)
                sp.wait_ge(cleared, 2)
                for row in (0, 32, 64):
                    sp.dma_start(bias[row:row + 1, :, :, :].rearrange("p a b c -> p (a b c)"),
                                 bk.rearrange("(o a) -> o a", o=1)).then_inc(b_loaded, 16)

            @block.gpsimd
            def _(pool):
                pool.memset(bias[:, :, :, :], 0.0).then_inc(cleared, 1)
                pool.memset(bias_rows[:, :, :, :], 0.0).then_inc(cleared, 1)
                pool.memset(one_rows[:, :], 1.0).then_inc(consts, 1)
                pool.memset(ones[:, :], 1.0).then_inc(consts, 1)

            @block.vector
            def _(dve):
                ch = Chain(dve, dve_steps)
                dve.wait_ge(loaded, 64)
                dve.wait_ge(b_loaded, 48)
                for m, x, n in ((mean, w, 128), (bmean, bias, 96)):
                    for k in range(4):
                        keys = x[:, k // 2, k % 2, 0:WG].rearrange("p (h e) -> p h e", e=HD1)
                        ch.link(dve.tensor_reduce(m[:, k, :], keys, AX.X, ALU.add))
                        ch.link(dve.tensor_scalar(m[:, k, :], m[:, k, :], 1.0 / HD1, None, ALU.mult))
                        ch.link(dve.tensor_tensor(keys, keys, m[:, k, :].rearrange("p (h a) -> p h a", a=1)
                                                  .broadcast_to([n, GH, HD1]), ALU.subtract))
                ch.link(dve.tensor_copy(w_hi[:, :, :], w[:, 0]))
                ch.done(dve.tensor_tensor(w_lo[:, :, :], w[:, 0], w_hi[:, :, :].bitcast(F32), ALU.subtract))
                ch.done(dve.tensor_copy(w_dca[:, :, :], w[:, 1]))
                for row in (0, 32, 64):
                    ch.link(dve.tensor_copy(part[:, :, :, :], bias[:, :, :, :]))
                    ch.done(dve.tensor_copy(bias_rows[row:row + 1], part[row:row + 1]))
                    ch.link(dve.tensor_tensor(bias[:, :, :, :], bias[:, :, :, :], part[:, :, :, :], ALU.subtract))

        rawT = sc.sb("rawT", [DC, SK])
        dcaT = sc.sb("dcaT", [DC, DCA])
        cT_hi = sc.sb("cT_hi", [DC, SK], F32R)
        cT_lo = sc.sb("cT_lo", [DC, SK], F32R)
        k_hi = [sc.sb(f"k_hi{p}", [WG, SK], F32R) for p in range(2)]
        k_lo = [sc.sb(f"k_lo{p}", [WG, SK], F32R) for p in range(2)]
        v_raw = [sc.sb(f"v_raw{p}", [KT, NKT, WG]) for p in range(2)]
        v_hi = sc.sb("v_hi", [KT, NKT, WG], F32R)
        v_lo = sc.sb("v_lo", [KT, NKT, WG], F32R)
        q_block = sc.sb("q_block", [WG, GH, S])
        q_hi = [sc.sb(f"q_hi{p}", [WG, GH * S], F32R) for p in range(2)]
        q_lo = [sc.sb(f"q_lo{p}", [WG, GH * S], F32R) for p in range(2)]
        k_raw = sc.sb("k_raw", [KT, NKT, WG])
        k_sq = sc.sb("k_sq", [KT, 4, WG])
        k_full = sc.sb("k_full", [WG, SK])
        var, k_r, t1, t2 = (sc.sb(n, [KT, NKT * GH]) for n in ("var", "k_r", "n1", "n2"))
        probs = [sc.sb(f"probs{p}", [TT, SK]) for p in range(2)]
        pT_hi = [sc.sb(f"pT_hi{p}", [KT, NKT, HALF], F32R) for p in range(2)]
        pT_lo = [sc.sb(f"pT_lo{p}", [KT, NKT, HALF], F32R) for p in range(2)]
        part_min = sc.sb("part_min", [TT, 2, NCH])
        row_min = sc.sb("row_min", [TT, 2])
        dca_s = sc.sb("dca_s", [TT, 2, DCA])
        dca_e = sc.sb("dca_e", [TT, 2, DCA])
        dca_min, dca_sum, dca_inv = (sc.sb(n, [TT, 2]) for n in ("dca_min", "dca_sum", "dca_inv"))
        sums = sc.sb("sums", [TT, 2, UNIT])
        inv = sc.sb("inv", [TT, UNIT])
        inv_diag = sc.sb("inv_diag", [TT, UNIT, TT])
        inv_block = sc.sb("inv_block", [WG, GH, S])
        s_ps = [sc.ps(f"s{k}", [128, 512]) for k in range(NS)]
        t_ps = [sc.ps(f"t{k}", [128, 512]) for k in range(NS)]
        o_ps = sc.ps("o_ps", [128, 512])
        kv_ps = x_ps = sc.ps("kv_ps", [128, 512])

        ctx_loaded = sc.sem("ctx_ld")
        hi_split, split_done = sc.sem("hi_split"), sc.sem("split_done")
        q_steps, q_ready = sc.sem("q_steps"), sc.sem("q_ready")
        kv_made, kv_kept = sc.sem("kv_made"), sc.sem("kv_kept")
        v_hi_made, values_ready = sc.sem("v_hi_made"), sc.sem("values_ready")
        squared, k_summed, k_normed = sc.sem("squared"), sc.sem("k_summed"), sc.sem("k_normed")
        k_turned, k_scaled = sc.sem("k_turned"), sc.sem("k_scaled")
        k_hi_made, keys_ready = sc.sem("k_hi_made"), sc.sem("keys_ready")
        scored, score_kept, dca_kept = sc.sem("scored"), sc.sem("score_kept"), sc.sem("dca_kept")
        row_max, dve_steps = sc.sem("row_max"), sc.sem("dve_steps")
        dca_exp, probs_made, dca_ready = sc.sem("dca_exp"), sc.sem("probs_made"), sc.sem("dca_ready")
        turned, turn_hi, turn_kept = sc.sem("turned"), sc.sem("turn_hi"), sc.sem("turn_kept")
        diag_made, inv_spread, inv_kept = sc.sem("diag_made"), sc.sem("inv_spread"), sc.sem("inv_kept")
        weighted, o_kept, o_done = sc.sem("weighted"), sc.sem("o_kept"), sc.sem("o_done")
        PAIRS = NKT // 2
        SCALED = NCH + 1
        block = ctx.enter_context(nc.Block())

        def bodies(eng, start, body, last):
            start()
            body(0, True, False)
            with eng.Fori(1, B - 1) as i:
                body(i, False, False)
            body(B - 1, False, True)
            last()

        @block.sync
        def _(sp):
            def load(b):
                wait(sp, split_done, NCH * b)
                sp.dma_start(rawT[:, :], ctxT_in[bass.ds(b, 1)].rearrange("b c k -> c (b k)")).then_inc(ctx_loaded, 16)

            def body(b, first, final):
                if not final:
                    load(b + 1)

            bodies(sp, lambda: load(0), body, lambda: None)

        @block.gpsimd
        def _(pool):
            def split(b, c):
                cols = slice(c * CK, (c + 1) * CK)
                pool.wait_ge(ctx_loaded, 16 * (b + 1))
                wait(pool, kv_made, PAIRS * (2 * b - 1) + 2 * c + 2)
                if c == 0:
                    upper_part(pool, dcaT[:, :], rawT[:, 0:DCA], ones).then_inc(hi_split, 1)
                upper_part(pool, cT_hi[:, cols], rawT[:, cols], ones).then_inc(hi_split, 1)
                pool.wait_ge(hi_split, (NCH + 1) * b + c + 2)
                pool.tensor_tensor(cT_lo[:, cols], rawT[:, cols], cT_hi[:, cols].bitcast(F32), ALU.subtract
                                   ).then_inc(split_done, 1)

            def queries(v, b, g):
                wait(pool, scored, UNIT * NCH * (v - 1))
                wait(pool, q_ready, v)
                pool.tensor_tensor(
                    q_block[:, :, :],
                    qT[:, g, bass.ds(b * S, S)].rearrange("p (a t) -> p a t", a=1).broadcast_to([WG, GH, S]),
                    blocks[:, :].rearrange("p (h a) -> p h a", a=1).broadcast_to([WG, GH, S]), ALU.mult
                ).then_inc(q_steps, 1)
                pool.wait_ge(q_steps, 2 * v + 1)
                q = q_block[:, :, :].rearrange("p h t -> p (h t)")
                upper_part(pool, q_hi[g][:, :], q, ones).then_inc(q_steps, 1)
                pool.wait_ge(q_steps, 2 * v + 2)
                pool.tensor_tensor(q_lo[g][:, :], q, q_hi[g][:, :].bitcast(F32), ALU.subtract).then_inc(q_ready, 1)

            def keys(v, g, c):
                cols = slice(c * CK, (c + 1) * CK)
                pool.wait_ge(k_scaled, SCALED * v + c + 2)
                if c == 0:
                    wait(pool, scored, UNIT * NCH * (v - 1))
                upper_part(pool, k_hi[g][:, cols], k_full[:, cols], ones).then_inc(k_hi_made, 1)
                pool.wait_ge(k_hi_made, NCH * v + c + 1)
                pool.tensor_tensor(k_lo[g][:, cols], k_full[:, cols], k_hi[g][:, cols].bitcast(F32), ALU.subtract
                                   ).then_inc(keys_ready, 1)

            def values(v, g, q):
                tiles = slice(QT * q, QT * (q + 1))
                n = UNIT * v + q
                pool.wait_ge(kv_kept, 2 * (PAIRS * v + (QT * (q + 1) + 1) // 2))
                wait(pool, weighted, n - UNIT + 1)
                upper_part(pool, v_hi[:, tiles, :].rearrange("p n c -> p (n c)"),
                           v_raw[g][:, tiles, :].rearrange("p n c -> p (n c)"), ones).then_inc(v_hi_made, 1)
                pool.wait_ge(v_hi_made, n + 1)
                pool.tensor_tensor(v_lo[:, tiles, :], v_raw[g][:, tiles, :], v_hi[:, tiles, :].bitcast(F32),
                                   ALU.subtract).then_inc(values_ready, 1)

            def start():
                for c in range(NCH):
                    split(0, c)
                queries(0, 0, 0)
                for c in range(NCH):
                    keys(0, 0, c)

            def body(b, first, final):
                for g in range(2):
                    u = 2 * b + g
                    v, vg = u + 1, (g + 1) % 2
                    if not (first and g == 0):
                        values(u - 1, vg, UNIT - 1)
                    if g == 0 and not final:
                        split(b + 1, 0)
                    if not (final and g == 1):
                        queries(v, b + g, vg)
                    values(u, g, 0)
                    if g == 0 and not final:
                        split(b + 1, 1)
                    values(u, g, 1)
                    if not (final and g == 1):
                        keys(v, vg, 0)
                        keys(v, vg, 1)
                    if g == 0 and not final:
                        split(b + 1, 2)
                    if not (final and g == 1):
                        keys(v, vg, 2)
                    values(u, g, 2)

            def last():
                values(2 * B - 1, 1, UNIT - 1)

            bodies(pool, start, body, last)

        @block.tensor
        def _(pe):
            def project(v, b, g, pair):
                if pair == 0:
                    wait(pe, k_scaled, SCALED * v)
                if pair % 2 == 0:
                    pe.wait_ge(split_done, NCH * b + pair // 2 + 1)
                wait(pe, kv_kept, 2 * (PAIRS * v + pair))
                for k in range(2):
                    j = 2 * pair + k
                    cols = slice(j * KT, (j + 1) * KT)
                    out = kv_ps[0:KT, k * 2 * WG:(k + 1) * 2 * WG]
                    pe.matmul(out, cT_hi[:, cols], w_hi[:, g, :], start=True, stop=False)
                    pe.matmul(out[:, 0:WG], one_rows[:, 0:KT], bias_rows[:, 0, g, :], start=False, stop=False)
                    pe.matmul(out, cT_hi[:, cols], w_lo[:, g, :], start=False, stop=False)
                    mm = pe.matmul(out, cT_lo[:, cols], w_hi[:, g, :], start=False, stop=True)
                    if j == 0:
                        top = kv_ps[0:DCA, :]
                        pe.matmul(top[:, WG:2 * WG], dcaT[:, :], w_dca[:, g, WG:2 * WG], start=True, stop=True)
                        pe.matmul(top[:, 0:WG], dcaT[:, :], w_dca[:, g, 0:WG], start=True, stop=False)
                        pe.matmul(top[:, 0:WG], one_rows[:, 0:DCA], bias_rows[:, 1, g, :], start=False, stop=True)
                mm.then_inc(kv_made, 1)

            def turn_keys(v, c):
                pe.wait_ge(k_normed, NCH * v + c + 1)
                if c == 0 and not (isinstance(v, int) and v == 0):
                    wait(pe, inv_kept, v - 1)
                wait(pe, k_scaled, SCALED * v + c + 1 if c else SCALED * v)
                for k in range(4):
                    mm = pe.transpose(x_ps[:, k * KT:(k + 1) * KT], k_raw[:, 4 * c + k, :], ident[0:KT, 0:KT])
                mm.then_inc(k_turned, 1)

            def scores(n, s, u):
                g, r = s // UNIT, s % UNIT
                rows = slice(r * TT, (r + 1) * TT)
                for c in range(NCH):
                    m = NCH * n + c
                    wait(pe, score_kept, m - NS + 1)
                    if c == 0:
                        wait(pe, dca_kept, n)
                    if r == 0:
                        pe.wait_ge(keys_ready, NCH * u + c + 1)
                    keys = slice(c * CK, (c + 1) * CK)
                    three_passes(pe, s_ps[c][0:TT, 0:CK], q_hi[g][:, rows], q_lo[g][:, rows],
                                 k_hi[g][:, keys], k_lo[g][:, keys], True, True).then_inc(scored, 1)

            def turn(n, s):
                pe.wait_ge(probs_made, n + 1)
                pe.wait_ge(dca_ready, n + 1)
                for f in range(NCH):
                    m = NCH * n + f
                    wait(pe, turn_kept, m - NS + 1)
                    for k in range(4):
                        j = 4 * f + k
                        mm = pe.transpose(t_ps[f][0:KT, k * TT:(k + 1) * TT],
                                          probs[s % 2][:, j * KT:(j + 1) * KT], ident[0:TT, 0:TT])
                    mm.then_inc(turned, 1)

            def spread(u, pairs_kept):
                pe.wait_ge(diag_made, u + 1)
                pe.wait_ge(kv_kept, pairs_kept)
                pe.matmul(x_ps[:, 0:HALF], ones[0:TT, :], inv_diag[:, :, :].rearrange("p k t -> p (k t)"),
                          start=True, stop=True).then_inc(inv_spread, 1)

            def weigh(u, g, r):
                pe.wait_ge(values_ready, UNIT * u + r + 1)
                if r == 0:
                    wait(pe, o_kept, u)
                for j in range(QT * r, QT * (r + 1)):
                    if j % 4 == 0 or j == QT * r:
                        pe.wait_ge(turn_kept, NCH * UNIT * u + NCH * (UNIT - 1) + j // 4 + 1)
                    mm = three_passes(pe, o_ps[:, 0:HALF], v_hi[:, j, :], v_lo[:, j, :],
                                      pT_hi[g][:, j, :], pT_lo[g][:, j, :], j == 0, j == NKT - 1)
                mm.then_inc(weighted, 1)

            def start():
                for pair in range(PAIRS):
                    project(0, 0, 0, pair)
                for c in range(NCH):
                    turn_keys(0, c)
                for pair in range(3):
                    project(1, 0, 1, pair)

            def body(b, first, final):
                for s in range(STEPS):
                    n, g, r = STEPS * b + s, s // UNIT, s % UNIT
                    u = 2 * b + g
                    v, vb, vg = u + 1, b + g, (g + 1) % 2
                    more = not (final and g == 1)

                    def extra_work(k):
                        if r == 0 and more and k >= 0:
                            project(v, vb, vg, 3 + k)
                        if r == 1 and k == 0 and not (first and s == 1):
                            spread(u - 1, 2 * PAIRS * (v + 1 if more else v))
                        if r == 2 and more and k > 0:
                            turn_keys(v, k - 1)
                        if r == 3 and more and k < 0:
                            turn_keys(v, 2)
                        if r == 3 and not final and k >= 0:
                            project(v + 1, b + 1, g, k)

                    extra_work(-1)
                    if r == 0:
                        pe.wait_ge(q_ready, u + 1)
                    scores(n, s, u)
                    extra_work(0)
                    if not (first and s == 0):
                        turn(n - 1, (s - 1) % STEPS)
                    extra_work(1)
                    if not (first and s < UNIT):
                        weigh(u - 1, (g + 1) % 2, r)
                    extra_work(2)

            def last():
                turn(STEPS * B - 1, STEPS - 1)
                spread(2 * B - 1, 2 * PAIRS * 2 * B)
                for r in range(UNIT):
                    weigh(2 * B - 1, 1, r)

            bodies(pe, start, body, last)

        @block.scalar
        def _(act):
            def keep(v, g, pair):
                act.wait_ge(kv_made, PAIRS * v + pair + 1)
                j = 2 * pair
                kv = kv_ps[0:KT, :].rearrange("p (k n) -> p k n", k=2)
                wait(act, k_turned, NCH * (v - 1) + pair // 2 + 1)
                act.copy(k_raw[:, j:j + 2, :], kv[:, :, 0:WG]).then_inc(kv_kept, 1)
                wait(act, values_ready, UNIT * (v - 2) + (j + 1) // QT + 1)
                act.copy(v_raw[g][:, j:j + 2, :], kv[:, :, WG:2 * WG]).then_inc(kv_kept, 1)

            def square(v, c):
                act.wait_ge(kv_kept, 2 * (PAIRS * v + 2 * c + 2))
                wait(act, k_summed, NCH * v + c)
                act.activation(k_sq[:, :, :], k_raw[:, 4 * c:4 * c + 4, :], ACT.Square).then_inc(squared, 1)

            def scale_keys(v, c):
                act.wait_ge(k_turned, NCH * v + c + 1)
                wait(act, keys_ready, NCH * (v - 1) + c + 1)
                lo = DCA if c == 0 else 0
                if c == 0:
                    act.activation(k_full[:, 0:DCA], x_ps[:, 0:DCA], ACT.Identity, scale=affine[:, 2:3],
                                   bias=affine[:, 3:4]).then_inc(k_scaled, 1)
                act.activation(k_full[:, c * CK + lo:(c + 1) * CK], x_ps[:, lo:CK], ACT.Identity,
                               scale=affine[:, 0:1], bias=affine[:, 1:2]).then_inc(k_scaled, 1)

            def upper(n, s, u):
                g, r = s // UNIT, s % UNIT
                for f in range(NCH):
                    act.wait_ge(turned, NCH * n + f + 1)
                    if f == 0 and r == 0:
                        wait(act, weighted, UNIT * (u - 1))
                    act.copy(pT_hi[g][:, 4 * f:4 * f + 4, r * TT:(r + 1) * TT],
                             t_ps[f][0:KT, 0:HALF].rearrange("p (k t) -> p k t", t=TT)
                             ).then_inc(turn_hi, 1)

            def exps(n, s):
                p = s % 2
                act.wait_ge(row_max, n + 1)
                act.activation(dca_e[:, p, :], dca_s[:, p, :], ACT.Exp, scale=-1.0, bias=dca_min[:, p:p + 1],
                               accum_out=dca_sum[:, p:p + 1]).then_inc(dca_exp, 1)
                act.activation(probs[p][:, DCA:SK], probs[p][:, DCA:SK], ACT.Exp, scale=-1.0,
                               bias=row_min[:, p:p + 1],
                               accum_out=sums[:, s // UNIT, s % UNIT:s % UNIT + 1]).then_inc(probs_made, 1)

            def start():
                for c in range(NCH):
                    keep(0, 0, 2 * c)
                    keep(0, 0, 2 * c + 1)
                    square(0, c)
                for c in range(NCH):
                    scale_keys(0, c)
                keep(1, 1, 0)
                keep(1, 1, 1)
                square(1, 0)
                keep(1, 1, 2)

            def body(b, first, final):
                for s in range(STEPS):
                    n, g, r = STEPS * b + s, s // UNIT, s % UNIT
                    u = 2 * b + g
                    v, vg = u + 1, (g + 1) % 2
                    more = not (final and g == 1)
                    if r == 0 and more:
                        keep(v, vg, 3)
                        square(v, 1)
                    if r == 3 and more:
                        scale_keys(v, 2)
                    if r == 3 and not final:
                        keep(v + 1, g, 0)
                    if not (first and s == 0):
                        upper(n - 1, (s - 1) % STEPS, 2 * b + (s - 1) // UNIT)
                    if r == 2 and more:
                        scale_keys(v, 0)
                    if r == 0 and more:
                        keep(v, vg, 4)
                    if r == 3 and not final:
                        keep(v + 1, g, 1)
                    exps(n, s)
                    if r == 0 and more:
                        keep(v, vg, 5)
                        square(v, 2)
                    if r == 2 and more:
                        scale_keys(v, 1)
                    if r == 3 and not final:
                        square(v + 1, 0)
                        keep(v + 1, g, 2)

            def last():
                upper(STEPS * B - 1, STEPS - 1, 2 * B - 1)

            bodies(act, start, body, last)

        @block.vector
        def _(dve):
            KEYS_N = 10
            UNIT_N = 1
            TILE_N = 1

            def heads(x):
                return x.rearrange("p n (h e) -> p (n h) e", e=HD1)

            def sum_squares(v, c):
                dve.wait_ge(squared, NCH * v + c + 1)
                dve.tensor_reduce(var[:, 4 * GH * c:4 * GH * (c + 1)], heads(k_sq[:, :, :]), AX.X, ALU.add
                                  ).then_inc(k_summed, 1)

            def key_norms(v, ch, between=lambda k: None):
                dve.wait_ge(k_summed, NCH * (v + 1))
                ch.link(dve.tensor_scalar(var[:, :], var[:, :], RSQRT / HD1, EPS_HEAD * RSQRT,
                                          ALU.mult, ALU.add))
                rsqrt(ch, k_r[:, :], var[:, :], t1[:, :], t2[:, :], between)

            def normalise(v, c):
                k = heads(k_raw[:, 4 * c:4 * c + 4, :])
                dve.tensor_tensor(k, k, k_r[:, 4 * GH * c:4 * GH * (c + 1)].rearrange("p (g a) -> p g a", a=1)
                                  .broadcast_to([KT, 4 * GH, HD1]), ALU.mult).then_inc(k_normed, 1)

            def negated(n, s):
                p = s % 2
                wait(dve, turned, NCH * (n - 1))
                for c in range(NCH):
                    dve.wait_ge(scored, NCH * n + c + 1)
                    lo = DCA if c == 0 else 0
                    if c == 0:
                        dve.tensor_scalar(dca_s[:, p, :], s_ps[0][0:TT, 0:DCA], -SCALE, BIG, ALU.mult, ALU.min,
                                          accum_out=dca_min[:, p:p + 1]).then_inc(dca_kept, 1)
                    dve.tensor_scalar(probs[p][:, c * CK + lo:(c + 1) * CK], s_ps[c][0:TT, lo:CK], -SCALE, BIG,
                                      ALU.mult, ALU.min, accum_out=part_min[:, p, c:c + 1]).then_inc(score_kept, 1)
                dve.wait_ge(score_kept, NCH * n + NCH)
                dve.wait_ge(dca_kept, n + 1)
                dve.tensor_reduce(row_min[:, p:p + 1], part_min[:, p, :], AX.X, ALU.min).then_inc(row_max, 1)

            def extra(n, s, ch):
                p = s % 2
                dve.wait_ge(dca_exp, n + 1)
                ch.link(dve.reciprocal(dca_inv[:, p:p + 1], dca_sum[:, p:p + 1]))
                dve.wait_ge(probs_made, n + 1)
                dve.tensor_scalar(probs[p][:, 0:DCA], dca_e[:, p, :], dca_inv[:, p:p + 1],
                                  sums[:, s // UNIT, s % UNIT:s % UNIT + 1], ALU.mult, ALU.mult
                                  ).then_inc(dca_ready, 1)

            def rest(n, s, fills=range(NCH)):
                g, r = s // UNIT, s % UNIT
                rows = slice(r * TT, (r + 1) * TT)
                for f in fills:
                    dve.wait_ge(turn_hi, NCH * n + f + 1)
                    dve.tensor_tensor(pT_lo[g][:, 4 * f:4 * f + 4, rows],
                                      t_ps[f][0:KT, 0:HALF].rearrange("p (k t) -> p k t", t=TT),
                                      pT_hi[g][:, 4 * f:4 * f + 4, rows].bitcast(F32), ALU.subtract
                                      ).then_inc(turn_kept, 1)

            def invert(u, s, ch):
                ch.link(dve.reciprocal(inv[:, :], sums[:, s // UNIT, :]))
                wait(dve, inv_spread, u)
                dve.tensor_tensor(inv_diag[:, :, :],
                                  ident[0:TT, 0:TT].rearrange("p (a t) -> p a t", a=1).broadcast_to([TT, UNIT, TT]),
                                  inv[:, :].rearrange("p (k a) -> p k a", a=1).broadcast_to([TT, UNIT, TT]),
                                  ALU.mult).then_inc(diag_made, 1)

            def take_inverse(u):
                dve.wait_ge(inv_spread, u + 1)
                wait(dve, o_kept, u)
                dve.tensor_tensor(inv_block[:, :, :], x_ps[:, 0:HALF].rearrange("p (h t) -> p h t", t=S),
                                  blocks[:, :].rearrange("p (h a) -> p h a", a=1).broadcast_to([WG, GH, S]),
                                  ALU.mult).then_inc(inv_kept, 1)

            def finish(u, b, g):
                dve.wait_ge(weighted, UNIT * (u + 1))
                dve.wait_ge(inv_kept, u + 1)
                blk = inv_block[:, :, :]
                dve.tensor_tensor(blk, o_ps[:, 0:HALF].rearrange("p (h t) -> p h t", t=S), blk, ALU.mult
                                  ).then_inc(o_kept, 1)
                dve.wait_ge(o_kept, u + 1)
                dve.tensor_reduce(qT[:, g, bass.ds(b * S, S)], blk.rearrange("p h t -> p t h"), AX.X, ALU.add
                                  ).then_inc(o_done, 1)
                dve.wait_ge(o_done, u + 1)

            def start():
                ch = Chain(dve, dve_steps)
                for c in range(NCH):
                    sum_squares(0, c)
                key_norms(0, ch)
                assert ch.n == KEYS_N
                for c in range(NCH):
                    normalise(0, c)
                sum_squares(1, 0)

            PER_BODY = 2 * (KEYS_N + UNIT_N) + STEPS * TILE_N

            def body(b, first, final):
                ch = Chain(dve, dve_steps, KEYS_N + PER_BODY * b - (0 if first else UNIT_N))
                for s in range(STEPS):
                    n, g, r = STEPS * b + s, s // UNIT, s % UNIT
                    u = 2 * b + g
                    v, vg = u + 1, (g + 1) % 2
                    more = not (final and g == 1)
                    if r == 0 and not (first and s < 2 * UNIT):
                        finish(u - 2, b - 1, g)
                    negated(n, s)
                    if r == 2 and not (first and s == 2):
                        take_inverse(u - 1)
                    if r == 2 and more:
                        normalise(v, 2)
                    if r == 1 and more:
                        def between(k):
                            if k < 2:
                                rest(n - 1, s - 1, (0,) if k == 0 else (1, 2))
                            else:
                                extra(n, s, ch)

                        sum_squares(v, 2)
                        key_norms(v, ch, between)
                        normalise(v, 0)
                        normalise(v, 1)
                        continue
                    if not (first and s == 0):
                        rest(n - 1, (s - 1) % STEPS)
                    if r == 0 and not (first and s == 0):
                        invert(u - 1, (s - 1) % STEPS, ch)
                    extra(n, s, ch)
                    if r == 0 and more:
                        sum_squares(v, 1)
                    if r == 3 and not final:
                        sum_squares(v + 1, 0)

            def last():
                ch = Chain(dve, dve_steps, PER_BODY * B - UNIT_N)
                finish(2 * B - 2, B - 1, 0)
                invert(2 * B - 1, STEPS - 1, ch)
                rest(STEPS * B - 1, STEPS - 1)
                take_inverse(2 * B - 1)
                finish(2 * B - 1, B - 1, 1)

            bodies(dve, start, body, last)


def close_heads(nc, wo, bv, bo, x2_d, qT, xs, gate):
    with ExitStack() as ctx:
        sc = Scope(nc, ctx, "c1")
        wo_sb = sc.sb("wo", [128, CH, D])
        bv_sb = sc.sb("bv", [128, 2, CH])
        bsum = sc.sb("bsum", [128, CH])
        bo_sb = sc.sb("bo", [TT, D])
        y = [sc.sb(f"y{k}", [TT, D]) for k in range(2)]
        y_ps = [sc.ps(f"y_ps{k}", [128, 512]) for k in range(4)]
        w_loaded, v_loaded, x_loaded = sc.sem("w_ld"), sc.sem("v_ld"), sc.sem("x_ld")
        dve_steps, biased = sc.sem("dve_steps"), sc.sem("biased")
        projected, with_bias, added = sc.sem("projected"), sc.sem("with_bias"), sc.sem("added")
        block = ctx.enter_context(nc.Block())

        @block.sync
        def _(sp):
            sp.dma_start(bv_sb[:, :, :], bv).then_inc(v_loaded, 16)
            sp.dma_start(wo_sb[:, :, :], wo.rearrange("(c p) d -> p c d", p=128)).then_inc(w_loaded, 16)
            sp.dma_start(bo_sb[:, :], bo.partition_broadcast(TT)).then_inc(v_loaded, 16)
            sp.dma_start(xs[:, :, :], x2_d.rearrange("(n p) d -> p n d", p=TT)).then_inc(x_loaded, 16)

        @block.tensor
        def _(pe):
            pe.wait_ge(w_loaded, 16)
            pe.wait_ge(biased, CH)
            for t in range(NTILE):
                if t >= 4:
                    pe.wait_ge(with_bias, t - 3)
                for c in range(CH):
                    mm = pe.matmul(y_ps[t % 4][0:TT, 0:D], qT[:, c, t * TT:(t + 1) * TT], wo_sb[:, c, :],
                                   start=(c == 0), stop=(c == CH - 1))
                mm.then_inc(projected, 1)

        @block.vector
        def _(dve):
            ch = Chain(dve, dve_steps)
            dve.wait_ge(v_loaded, 32)
            ch.link(dve.tensor_tensor(bsum[:, :], bv_sb[:, 0, :], bv_sb[:, 1, :], ALU.add))
            for c in range(CH):
                dve.tensor_scalar(qT[:, c, :], qT[:, c, :], bsum[:, c:c + 1], None, ALU.add).then_inc(biased, 1)
            dve.wait_ge(x_loaded, 16)
            for t in range(NTILE):
                dve.wait_ge(projected, t + 1)
                if t >= 2:
                    dve.wait_ge(added, t - 1)
                dve.tensor_tensor(y[t % 2][:, :], y_ps[t % 4][0:TT, 0:D], bo_sb[:, :], ALU.add).then_inc(with_bias, 1)
                dve.wait_ge(with_bias, t + 1)
                dve.scalar_tensor_tensor(xs[:, t, :], y[t % 2][:, :], gate[:, 2:3], xs[:, t, :],
                                         ALU.mult, ALU.add).then_inc(added, 1)


def route(nc, router_wT, expert_bias, ident_in, xs, x_hi, x_lo, p_d):
    with ExitStack() as ctx:
        sc = Scope(nc, ctx, "rt")
        ident = sc.sb("ident", [128, 128])
        wr = sc.sb("wr", [128, CH, E])
        eb = sc.sb("eb", [TT, E])
        xn = sc.sb("xn", [TT, NTILE, D])
        xnT = sc.sb("xnT", [128, CH, NT])
        z, e, s2, p, pw, score, choice, keep, tie, cnt, cnt2 = (
            sc.sb(n, [TT, NTILE, E]) for n in ("z", "e", "s2", "p", "pw", "score", "choice", "keep", "tie", "cnt", "cnt2"))
        top = sc.sb("top", [TT, NTILE, 8])
        room, total = sc.sb("room", [TT, NTILE]), sc.sb("total", [TT, NTILE])
        one = sc.sb("one", [1, NT])
        pT = sc.sb("pT", [E, NT])
        scratch = ln_scratch(sc)
        banks = [sc.ps(f"b{k}", [128, 512]) for k in range(5)]
        loaded, b_loaded = sc.sem("ld"), sc.sem("b_ld")
        dve_steps, xn_ready = sc.sem("dve_steps"), sc.sem("xn_ready")
        turned, turn_kept, split_hi, split_lo = (sc.sem(n) for n in ("turned", "turn_kept", "split_hi", "split_lo"))
        logits_made, abs_made, exp_made = sc.sem("logits_made"), sc.sem("abs_made"), sc.sem("exp_made")
        shares, p_turned, p_kept, p_stored, ones_set = (
            sc.sem(n) for n in ("shares", "p_turned", "p_kept", "p_stored", "ones_set"))
        block = ctx.enter_context(nc.Block())

        @block.sync
        def _(sp):
            sp.dma_start(ident[:, :], ident_in).then_inc(loaded, 16)
            sp.dma_start(wr[:, :, :], router_wT.rearrange("(c p) e -> p c e", p=128)).then_inc(loaded, 16)
            sp.dma_start(eb[:, :], expert_bias.partition_broadcast(TT)).then_inc(b_loaded, 16)
            sp.wait_ge(ones_set, 1)
            sp.dma_start(p_d[0:1, :], one[:, :]).then_inc(p_stored, 16)
            sp.wait_ge(p_kept, 2)
            sp.dma_start(p_d[1:E + 1, :], pT[:, :]).then_inc(p_stored, 16)
            sp.wait_ge(p_stored, 32)

        @block.gpsimd
        def _(pool):
            pool.memset(one[:, :], 1.0).then_inc(ones_set, 1)

        @block.tensor
        def _(pe):
            pe.wait_ge(loaded, 32)
            turn_tokens(pe, None, xn, xnT, banks[0:2], ident, xn_ready, turned, turn_kept)
            pe.wait_ge(turn_kept, 2 * CH)
            for t in range(NTILE):
                for c in range(CH):
                    mm = pe.matmul(banks[2][0:TT, t * E:(t + 1) * E], xnT[:, c, t * TT:(t + 1) * TT], wr[:, c, :],
                                   start=(c == 0), stop=(c == CH - 1))
            mm.then_inc(logits_made, 1)
            pe.wait_ge(shares, 1)
            for half in range(2):
                for k in range(4):
                    mm = pe.transpose(banks[3 + half][0:E, k * TT:(k + 1) * TT], p[:, 4 * half + k, :],
                                      ident[0:TT, 0:TT])
                mm.then_inc(p_turned, 1)

        @block.scalar
        def _(act):
            turn_tokens(None, act, xn, xnT, banks[0:2], ident, xn_ready, turned, turn_kept)
            act.wait_ge(turn_kept, 2 * CH)
            act.copy(x_hi[:, :, :], xnT[:, :, :]).then_inc(split_hi, 1)
            act.wait_ge(abs_made, 1)
            act.activation(e[:, :, :], z[:, :, :], ACT.Exp).then_inc(exp_made, 1)
            for half in range(2):
                act.wait_ge(p_turned, half + 1)
                act.copy(pT[:, half * HALF:(half + 1) * HALF], banks[3 + half][0:E, 0:HALF]).then_inc(p_kept, 1)

        @block.vector
        def _(dve):
            ch = Chain(dve, dve_steps)
            layer_norm(ch, xn[:, :, :], xs[:, :, :], *scratch, TT, xn_ready)
            dve.wait_ge(split_hi, 1)
            dve.tensor_tensor(x_lo[:, :, :], xnT[:, :, :], x_hi[:, :, :].bitcast(F32), ALU.subtract
                              ).then_inc(split_lo, 1)
            lg = banks[2][0:TT, 0:NTILE * E].rearrange("p (n e) -> p n e", e=E)

            def flat(x):
                return x[:, :, :]

            dve.wait_ge(logits_made, 1)
            ch.link(dve.tensor_copy(flat(s2), lg))
            ch.link(dve.tensor_scalar(flat(z), flat(s2), -1.0, None, ALU.mult))
            dve.tensor_tensor(flat(z), flat(s2), flat(z), ALU.min).then_inc(abs_made, 1)
            ch.link(dve.tensor_scalar(flat(score), flat(s2), 0.0, None, ALU.max))
            dve.wait_ge(exp_made, 1)
            ch.link(dve.tensor_scalar(flat(p), flat(e), 2.0, None, ALU.add))
            ch.link(dve.reciprocal(flat(p), flat(p)))
            ch.link(dve.tensor_tensor(flat(e), flat(e), flat(p), ALU.mult))
            ch.link(dve.tensor_tensor(flat(s2), flat(e), flat(e), ALU.mult))
            ch.link(dve.tensor_scalar(flat(pw), flat(s2), 2.0 / 17, 2.0 / 15, ALU.mult, ALU.add))
            for k in (13, 11, 9, 7, 5, 3, 1):
                ch.link(dve.tensor_tensor(flat(pw), flat(pw), flat(s2), ALU.mult))
                ch.link(dve.tensor_scalar(flat(pw), flat(pw), 2.0 / k, None, ALU.add))
            ch.link(dve.tensor_tensor(flat(pw), flat(pw), flat(e), ALU.mult))
            ch.link(dve.tensor_tensor(flat(z), flat(score), flat(pw), ALU.add))
            ch.link(dve.tensor_scalar(flat(z), flat(z), RSQRT, None, ALU.mult))
            rsqrt(ch, flat(p), flat(z), flat(s2), flat(pw))
            ch.link(dve.scalar_tensor_tensor(flat(score), flat(z), 1.0 / RSQRT, flat(p), ALU.mult, ALU.mult))
            dve.wait_ge(b_loaded, 16)
            ch.link(dve.tensor_tensor(flat(choice), flat(score),
                                      eb[:, :].rearrange("p (a e) -> p a e", a=1).broadcast_to([TT, NTILE, E]),
                                      ALU.add))
            for t in range(NTILE):
                ch.done(dve.max(top[:, t, :], choice[:, t, :]))
            ch.settle()
            fourth = top[:, :, TOPK - 1:TOPK].broadcast_to([TT, NTILE, E])
            ch.link(dve.tensor_tensor(flat(keep), flat(choice), fourth, ALU.is_gt))
            ch.link(dve.tensor_tensor(flat(tie), flat(choice), fourth, ALU.is_equal))
            ch.link(dve.tensor_reduce(room[:, :], flat(keep), AX.X, ALU.add))
            ch.link(dve.tensor_scalar(room[:, :], room[:, :], -1.0, float(TOPK), ALU.mult, ALU.add))
            a, b = tie, cnt
            for w in (1, 2, 4, 8, 16):
                ch.done(dve.tensor_copy(b[:, :, 0:w], a[:, :, 0:w]))
                ch.link(dve.tensor_tensor(b[:, :, w:E], a[:, :, w:E], a[:, :, 0:E - w], ALU.add))
                a, b = b, (cnt2 if b is cnt else cnt)
            ch.link(dve.tensor_tensor(flat(a), flat(a), room[:, :].rearrange("p (n a) -> p n a", a=1)
                                      .broadcast_to([TT, NTILE, E]), ALU.is_le))
            ch.link(dve.tensor_tensor(flat(tie), flat(tie), flat(a), ALU.mult))
            ch.link(dve.tensor_tensor(flat(keep), flat(keep), flat(tie), ALU.add))
            ch.link(dve.tensor_tensor(flat(score), flat(score), flat(keep), ALU.mult))
            ch.link(dve.tensor_reduce(total[:, :], flat(score), AX.X, ALU.add))
            ch.link(dve.tensor_scalar(total[:, :], total[:, :], 1e-20, None, ALU.add))
            ch.link(dve.reciprocal(total[:, :], total[:, :]))
            dve.tensor_tensor(flat(p), flat(score), total[:, :].rearrange("p (n a) -> p n a", a=1)
                              .broadcast_to([TT, NTILE, E]), ALU.mult).then_inc(shares, 1)


def experts(nc, weights_in, p_d, x_hi, x_lo, xs, gate, out):
    UP, DOWN = CH * I, 2 * CH * I
    WCOLS = DOWN + D
    LAG = 3
    NE = E + 1
    BODY = 3
    SLOTS = 2 * BODY
    assert NE % BODY == 0
    with ExitStack() as ctx:
        sc = Scope(nc, ctx, "ex")
        raw = [sc.sb(f"raw{p}", [128, WCOLS]) for p in range(BODY)]
        w_hi = [sc.sb(f"w_hi{p}", [128, WCOLS], F32R) for p in range(BODY)]
        w_lo = [sc.sb(f"w_lo{p}", [128, WCOLS], F32R) for p in range(BODY)]
        share = [sc.sb(f"share{p}", [128, NT]) for p in range(BODY)]
        zeros = sc.sb("zeros", [128, 512], BF16)
        gate_c, up_c, silu, up_p, h = ([sc.sb(f"{n}{p}", [I, HALF]) for p in range(2)]
                                       for n in ("gate_c", "up_c", "silu", "up_p", "h"))
        h_hi = [sc.sb(f"h_hi{p}", [I, HALF], F32R) for p in range(LAG)]
        h_lo = [sc.sb(f"h_lo{p}", [I, HALF], F32R) for p in range(LAG)]
        y_ps = [sc.ps(f"y{k}", [128, 512]) for k in range(4)]
        g_ps = [sc.ps(f"g{k}", [128, 512]) for k in range(2)]
        u_ps = [sc.ps(f"u{k}", [128, 512]) for k in range(2)]
        w_loaded = [sc.sem(f"w_ld{p}") for p in range(BODY)]
        p_loaded = [sc.sem(f"p_ld{p}") for p in range(BODY)]
        cleared, w_hi_made, w_ready = sc.sem("cleared"), sc.sem("w_hi_made"), sc.sem("w_ready")
        made, gate_clipped, clipped = sc.sem("made"), sc.sem("gate_clipped"), sc.sem("clipped")
        silu_made, scaled, h_made, h_hi_made, h_ready = (
            sc.sem(n) for n in ("silu_made", "scaled", "h_made", "h_hi_made", "h_ready"))
        downed, added, stored = sc.sem("downed"), sc.sem("added"), sc.sem("stored")
        block = ctx.enter_context(nc.Block())

        def bodies(eng, body, last):
            body(0, True, False)
            with eng.Fori(1, NE // BODY - 1) as i:
                body(i, False, False)
            body(NE // BODY - 1, False, True)
            last()

        @block.sync
        def _(sp):
            def body(i, first, final):
                for p in range(BODY):
                    e = BODY * i + p
                    wait(sp, w_ready, e - BODY + 1)
                    sp.dma_start(raw[p][:, :], weights_in[bass.ds(e, 1)].rearrange("e p w -> p (e w)")
                                 ).then_inc(w_loaded[p], 16)
                    wait(sp, scaled, 2 * (e - BODY) + 2)
                    sp.dma_start(share[p][:, :], p_d[bass.ds(e, 1)].rearrange("e t -> (e t)").partition_broadcast(128)
                                 ).then_inc(p_loaded[p], 16)

            def last():
                for t in range(NTILE):
                    sp.wait_ge(added, t + 1)
                    sp.dma_start(out[t * TT:(t + 1) * TT, :], xs[:, t, :]).then_inc(stored, 16)
                sp.wait_ge(stored, 16 * NTILE)

            bodies(sp, body, last)

        @block.gpsimd
        def _(pool):
            def weights_rest(e, p):
                pool.wait_ge(w_hi_made, e + 1)
                pool.tensor_tensor(w_lo[p][:, :], raw[p][:, :], w_hi[p][:, :].bitcast(F32), ALU.subtract
                                   ).then_inc(w_ready, 1)

            def body(i, first, final):
                if first:
                    pool.memset(zeros[:, :], 0.0).then_inc(cleared, 1)
                    weights_rest(0, 0)
                for k in range(SLOTS):
                    m, p, half = SLOTS * i + k, k // 2, k % 2
                    if half == 0:
                        pool.wait_ge(p_loaded[p], 16 * (i + 1))
                    pool.wait_ge(clipped, m + 1)
                    wait(pool, h_made, m - 1)
                    pool.tensor_tensor(up_p[half][:, :], up_c[half][:, :],
                                       share[p][:, half * HALF:(half + 1) * HALF], ALU.mult).then_inc(scaled, 1)
                    if half == 0 and not (final and p == BODY - 1):
                        weights_rest(BODY * i + p + 1, (p + 1) % BODY)

            bodies(pool, body, lambda: None)

        @block.tensor
        def _(pe):
            pe.wait_ge(cleared, 1)
            for k in range(4):
                pe.matmul(y_ps[k][0:TT, :], zeros[:, 0:TT], zeros[:, :], start=True, stop=True,
                          skip_group_check=True)

            def gate_up(e, m, p, half):
                if half == 0:
                    pe.wait_ge(w_ready, e + 1)
                wait(pe, clipped, m - 1)
                cols = slice(half * HALF, (half + 1) * HALF)
                for bank, base in ((g_ps[half], 0), (u_ps[half], UP)):
                    for c in range(CH):
                        w = slice(base + c * I, base + (c + 1) * I)
                        mm = three_passes(pe, bank[:, 0:HALF], w_hi[p][:, w], w_lo[p][:, w],
                                          x_hi[:, c, cols], x_lo[:, c, cols], c == 0, c == CH - 1)
                mm.then_inc(made, 1)

            def down(m, k):
                p, half, place = k // 2, k % 2, k % LAG
                pe.wait_ge(h_ready, m + 1)
                for t in range(4):
                    tile = 4 * half + t
                    rows = slice(t * TT, (t + 1) * TT)
                    y = y_ps[tile // 2][0:TT, (tile % 2) * D:(tile % 2 + 1) * D]
                    for a, b in ((h_hi, w_hi), (h_hi, w_lo), (h_lo, w_hi)):
                        mm = pe.matmul(y, a[place][:, rows], b[p][:, DOWN:WCOLS], start=False, stop=False,
                                       skip_group_check=True)
                mm.then_inc(downed, 1)

            def body(i, first, final):
                for k in range(SLOTS):
                    m = SLOTS * i + k
                    gate_up(BODY * i + k // 2, m, k // 2, k % 2)
                    if not (first and k < LAG):
                        down(m - LAG, (k - LAG) % SLOTS)

            def last():
                for k in range(SLOTS - LAG, SLOTS):
                    down(2 * NE - SLOTS + k, k)

            bodies(pe, body, last)

        @block.scalar
        def _(act):
            def weights_upper(e, i, p):
                act.wait_ge(w_loaded[p], 16 * (i + 1))
                wait(act, downed, 2 * (e - BODY) + 2)
                act.copy(w_hi[p][:, :], raw[p][:, :]).then_inc(w_hi_made, 1)

            def upper(m, k):
                act.wait_ge(h_made, m + 1)
                wait(act, downed, m - LAG + 1)
                act.copy(h_hi[k % LAG][:, :], h[k % 2][:, :]).then_inc(h_hi_made, 1)

            def body(i, first, final):
                if first:
                    weights_upper(0, 0, 0)
                for k in range(SLOTS):
                    m, p, half = SLOTS * i + k, k // 2, k % 2
                    act.wait_ge(gate_clipped, m + 1)
                    wait(act, h_made, m - 1)
                    act.activation(silu[half][:, :], gate_c[half][:, :], ACT.Silu).then_inc(silu_made, 1)
                    if not (first and k == 0):
                        upper(m - 1, (k - 1) % SLOTS)
                    if half == 0 and not (final and p == BODY - 1):
                        weights_upper(BODY * i + p + 1, i + (p + 1) // BODY, (p + 1) % BODY)

            bodies(act, body, lambda: upper(2 * NE - 1, SLOTS - 1))

        @block.vector
        def _(dve):
            def clip(m, k):
                half = k % 2
                dve.wait_ge(made, m + 1)
                wait(dve, silu_made, m - 1)
                dve.tensor_scalar(gate_c[half][:, :], g_ps[half][:, 0:HALF], -ALPHA, ALPHA, ALU.max, ALU.min
                                  ).then_inc(gate_clipped, 1)
                wait(dve, scaled, m - 1)
                dve.tensor_scalar(up_c[half][:, :], u_ps[half][:, 0:HALF], -ALPHA, ALPHA, ALU.max, ALU.min
                                  ).then_inc(clipped, 1)

            def hidden(m, k):
                half = k % 2
                dve.wait_ge(silu_made, m + 1)
                dve.wait_ge(scaled, m + 1)
                wait(dve, h_ready, m - 1)
                dve.tensor_tensor(h[half][:, :], silu[half][:, :], up_p[half][:, :], ALU.mult).then_inc(h_made, 1)

            def rest(m, k):
                dve.wait_ge(h_hi_made, m + 1)
                dve.tensor_tensor(h_lo[k % LAG][:, :], h[k % 2][:, :], h_hi[k % LAG][:, :].bitcast(F32), ALU.subtract
                                  ).then_inc(h_ready, 1)

            def body(i, first, final):
                for k in range(SLOTS):
                    m = SLOTS * i + k
                    clip(m, k)
                    if not (first and k < 2):
                        rest(m - 2, (k - 2) % SLOTS)
                    if not (first and k < 1):
                        hidden(m - 1, (k - 1) % SLOTS)

            def last():
                rest(2 * NE - 2, SLOTS - 2)
                hidden(2 * NE - 1, SLOTS - 1)
                rest(2 * NE - 1, SLOTS - 1)
                dve.wait_ge(downed, 2 * NE)
                for t in range(NTILE):
                    dve.scalar_tensor_tensor(xs[:, t, :], y_ps[t // 2][0:TT, (t % 2) * D:(t % 2 + 1) * D],
                                             gate[:, 3:4], xs[:, t, :], ALU.mult, ALU.add).then_inc(added, 1)

            bodies(dve, body, last)


def build(nc, a, out):
    def scratch(name, shape):
        return nc.dram_tensor(name, shape, F32).ap()

    q_hi_d, q_lo_d = scratch("q_hi_d", [DC, B, H0, S]), scratch("q_lo_d", [DC, B, H0, S])
    o_d, x2_d, p_d = scratch("o_d", [DC, H0, NT]), scratch("x2_d", [NT, D]), scratch("p_d", [E + 1, NT])
    project_queries(nc, a["x"], a["wqT"], a["wkT"], a["ident"], q_hi_d, q_lo_d)
    attend_context(nc, a["ctx"], a["ctxT"], a["mask"], a["ident"], q_hi_d, q_lo_d, o_d)
    with nc.sbuf_tensor("gate", [TT, 4], F32) as gate, nc.sbuf_tensor("qT", [128, CH, NT], F32) as qT:
        with nc.sbuf_tensor("x12", [TT, NTILE, D], F32) as xs, nc.semaphore("x2_stored") as x2_stored:
            close_attention(nc, o_d, a["x"], a["wvT"], a["wo0"], a["gates"], xs, gate)
            feed_forward(nc, a["w1T"], a["w3T"], a["w2T"], a["hadamard"], a["ident"], xs, gate)
            project_heads(nc, a["wq1"], a["bq1"], a["qn_w"], a["qn_b"], a["ident"], xs, qT)
            with nc.Block() as block:
                @block.sync
                def _(sp):
                    sp.dma_start(x2_d.rearrange("(n p) d -> p n d", p=TT), xs[:, :, :]).then_inc(x2_stored, 16)
                    sp.wait_ge(x2_stored, 16)
        attend_heads(nc, a["ctxT"], a["wkv"], a["bk"], a["affine"], a["blocks"], a["ident"], qT)
        with (nc.sbuf_tensor("x34", [TT, NTILE, D], F32) as xs, nc.sbuf_tensor("x_hi", [128, CH, NT], F32R) as x_hi,
              nc.sbuf_tensor("x_lo", [128, CH, NT], F32R) as x_lo):
            close_heads(nc, a["wo1"], a["bv"], a["bo"], x2_d, qT, xs, gate)
            route(nc, a["router_wT"], a["expert_bias"], a["ident"], xs, x_hi, x_lo, p_d)
            experts(nc, a["expert_w"], p_d, x_hi, x_lo, xs, gate, out)


def kernel(**inputs):
    import numpy as np
    import concourse.bacc as bacc
    from concourse.bass_utils import run_bass_kernel_spmd

    v = {k: np.asarray(x) for k, x in inputs.items()}

    def turned(x):
        return np.ascontiguousarray(np.swapaxes(x, -1, -2))

    def extra_first(x):
        return np.ascontiguousarray(np.concatenate([x[:, SK - DCA:], x[:, :SK - DCA]], axis=1))

    def main_groups(k, w):
        both = np.concatenate([k, w], axis=-1)
        n = both.shape[0]
        return both.reshape(n, 2, GH, 2, HD1).transpose(0, 1, 3, 2, 4).reshape(n, 2, 2 * WG)

    def extra_groups(w):
        n = w.shape[0]
        return w.reshape(n, 2, 2, GH, HD1).transpose(0, 2, 1, 3, 4).reshape(n, 2, 2 * WG)

    hadamard = np.ones((1, 1), np.float32)
    for _ in range(7):
        hadamard = np.block([[hadamard, hadamard], [hadamard, -hadamard]])
    context = extra_first(v["ctx_1024"])
    mask = extra_first(v["mask_BxS2_bf1"]).view(np.uint8)
    wkv = np.stack([main_groups(v["L1_xattn_Wk"], v["L1_xattn_Wv"]), extra_groups(v["L1_xattn_Wkv_dca"])], axis=1)
    bkv = np.stack([main_groups(v["L1_xattn_bk"][None], v["L1_xattn_bv"][None])[0],
                    extra_groups(v["L1_xattn_bkv_dca"][None])[0]])

    def expert_columns(gate, up, down):
        n = gate.shape[0]
        g, u = (turned(w).reshape(n, CH, 128, I).transpose(0, 2, 1, 3).reshape(n, 128, CH * I) for w in (gate, up))
        return np.concatenate([g, u, turned(down)], axis=2)

    arrays = {
        "x": v["x"].reshape(NT, D), "ctx": context, "ctxT": turned(context), "mask": mask,
        "gates": np.stack([v["g_xattn"], v["g_ffn"]], axis=1).reshape(4),
        "wqT": turned(v["L0_xattn_Wq"]), "wkT": turned(v["L0_xattn_Wk"]), "wvT": turned(v["L0_xattn_Wv"]),
        "wo0": v["L0_xattn_Wo"], "w1T": turned(v["L0_ffn_W1"]), "w3T": turned(v["L0_ffn_W3"]),
        "w2T": turned(v["L0_ffn_W2"]), "hadamard": hadamard, "ident": np.eye(128, dtype=np.float32),
        "wq1": v["L1_xattn_Wq"], "bq1": v["L1_xattn_bq"], "qn_w": v["L1_xattn_qn_w"], "qn_b": v["L1_xattn_qn_b"],
        "wkv": wkv, "bk": bkv[:, :, :WG].reshape(-1),
        "affine": np.stack([np.tile(v["L1_xattn_" + n], GH) for n in ("kn_w", "kn_b", "kn_dca_w", "kn_dca_b")], axis=1),
        "blocks": (np.arange(WG)[:, None] // HD1 == np.arange(GH)[None, :]).astype(np.float32),
        "bv": bkv[:, :, WG:].transpose(2, 0, 1), "wo1": v["L1_xattn_Wo"], "bo": v["L1_xattn_bo"],
        "router_wT": turned(v["L1_ffn_router_w"]), "expert_bias": v["L1_ffn_expert_bias"],
        "expert_w": np.concatenate([
            expert_columns(v["L1_ffn_shared_gate_w"][None], v["L1_ffn_shared_up_w"][None],
                           v["L1_ffn_shared_down_w"][None]),
            expert_columns(v["L1_ffn_gate_w"], v["L1_ffn_up_w"], v["L1_ffn_down_w"])]),
    }
    arrays = {f"in_{k}": np.ascontiguousarray(x) for k, x in arrays.items()}
    nc = bacc.Bacc("TRN2", target_bir_lowering=False, num_devices=1)
    tensors = {k[3:]: nc.dram_tensor(k, x.shape, mybir.dt.from_np(x.dtype), kind="ExternalInput").ap()
               for k, x in arrays.items()}
    out = nc.dram_tensor("out", (NT, D), F32, kind="ExternalOutput").ap()
    build(nc, tensors, out)
    r = run_bass_kernel_spmd(nc, [arrays], core_ids=[0])
    return r.results[0]["out"].reshape(B, S, D)
```

```python
from contextlib import ExitStack

import concourse.bass as bass
from concourse import mybir

F32 = mybir.dt.float32
F32R = mybir.dt.float32r
BF16 = mybir.dt.bfloat16
I32 = mybir.dt.int32
U8 = mybir.dt.uint8
ALU = mybir.AluOpType
ACT = mybir.ActivationFunctionType
AX = mybir.AxisListType

B, S, D = 16, 56, 256
SK, DC = 1500, 128
H0, G0, HD0 = 16, 2, 128
H1, HD1, DCA = 16, 16, 16
FF = 1024
E, I, TOPK = 32, 128, 4
ALPHA = 7.0
NT = B * S
TT = 2 * S
NTILE = NT // TT
CH = D // 128
KT, NKT = 125, SK // 125
CK, NCH = 500, SK // 500
HALF = 448
BIG = 3.0e38
EPS_LN, EPS_HEAD = 1e-5, 1e-6


def wait(eng, sem, value):
    if isinstance(value, int) and value <= 0:
        return
    eng.wait_ge(sem, value)


def upper_part(pool, out, x, ones):
    return pool.tensor_tensor(out, x, ones[0:x.shape[0], 0:1].broadcast_to(x.shape), ALU.mult)


class Chain:

    def __init__(self, eng, sem, base=0):
        self.eng, self.sem, self.base, self.n = eng, sem, base, 0

    def done(self, ins):
        ins.then_inc(self.sem, 1)
        self.n += 1

    def settle(self):
        wait(self.eng, self.sem, self.base + self.n)

    def link(self, ins):
        self.done(ins)
        self.settle()


RSQRT = 64.0 / 9.0


def rsqrt(ch, y, v, half_v, t, between=lambda k: None):
    dve = ch.eng
    ch.done(dve.tensor_scalar(half_v, v, -0.5, None, ALU.mult))
    ch.link(dve.tensor_scalar(y.bitcast(I32), v.bitcast(I32), -0.5, float(0x5F3759DF), ALU.mult, ALU.add))
    between(0)
    ch.link(dve.tensor_tensor(t, y, y, ALU.mult))
    ch.link(dve.tensor_tensor(t, t, half_v, ALU.mult))
    ch.link(dve.scalar_tensor_tensor(y, t, 1.5, y, ALU.add, ALU.mult))
    between(1)
    ch.link(dve.tensor_tensor(t, y, y, ALU.mult))
    ch.link(dve.tensor_tensor(t, t, v, ALU.mult))
    between(2)
    ch.link(dve.scalar_tensor_tensor(t, t, -10.0 / 3.0, t, ALU.add, ALU.mult))
    between(3)
    ch.link(dve.scalar_tensor_tensor(y, t, 5.0, y, ALU.add, ALU.mult))


def layer_norm(ch, xn, x, stats, mv, rs, tmp1, tmp2, rows, ready):
    dve = ch.eng
    tiles = x.shape[1]
    for t in range(tiles):
        ch.done(dve.bn_stats(stats[0:rows, t, :], x[:, t, :]))
    ch.settle()
    for t in range(tiles):
        ch.done(dve.bn_aggr(mv[0:rows, t, :], stats[0:rows, t, :]))
    ch.settle()
    ch.link(dve.tensor_scalar(rs[0:rows, :], mv[0:rows, :, 1], RSQRT, EPS_LN * RSQRT,
                              ALU.mult, ALU.add))
    rsqrt(ch, mv[0:rows, :, 1], rs[0:rows, :], tmp1[0:rows, :], tmp2[0:rows, :])
    for t in range(tiles):
        dve.tensor_scalar(xn[:, t, :], x[:, t, :], mv[0:rows, t, 0:1], mv[0:rows, t, 1:2],
                          ALU.subtract, ALU.mult).then_inc(ready, 1)


class Scope:

    def __init__(self, nc, ctx, tag):
        self.nc, self.ctx, self.tag = nc, ctx, tag

    def sb(self, name, shape, dt=F32):
        return self.ctx.enter_context(self.nc.sbuf_tensor(f"{self.tag}_{name}", shape, dt))

    def ps(self, name, shape, dt=F32):
        return self.ctx.enter_context(self.nc.psum_tensor(f"{self.tag}_{name}", shape, dt))

    def sem(self, name):
        return self.ctx.enter_context(self.nc.semaphore(f"{self.tag}_{name}"))


class ClearedScope(Scope):

    def __init__(self, nc, ctx, tag):
        super().__init__(nc, ctx, tag)
        self.sems = []

    def sem(self, name):
        self.sems.append(self.nc.alloc_semaphore(name=f"{self.tag}_{name}"))
        return self.sems[-1]

    def clear(self):
        self.nc.clear_and_free_semaphores(self.sems)
        self.nc.all_engine_barrier()


def ln_scratch(sc):
    return (sc.sb("ln_stats", [TT, NTILE, 6]), sc.sb("ln_mv", [TT, NTILE, 2]), sc.sb("ln_rs", [TT, NTILE]),
            sc.sb("ln_t1", [TT, NTILE]), sc.sb("ln_t2", [TT, NTILE]))


def three_passes(pe, out, w_hi, w_lo, m_hi, m_lo, first, last):
    pe.matmul(out, w_hi, m_hi, start=first, stop=False)
    pe.matmul(out, w_hi, m_lo, start=False, stop=False)
    return pe.matmul(out, w_lo, m_hi, start=False, stop=last)


class ContextParts:
    STEPS, SCORES_READY = 7, 5

    def __init__(self, sc, ctx_in, ctxT_in, mask_in, q_d):
        self.ctx_in, self.ctxT_in, self.mask_in, self.q_d = ctx_in, ctxT_in, mask_in, q_d
        self.ones = sc.sb("ones", [128, 128])
        self.raw = sc.sb("raw", [KT, NKT, DC])
        self.rawT = sc.sb("rawT", [DC, SK])
        self.q_raw = sc.sb("q_raw", [DC, H0 * S])
        self.mask_u8 = sc.sb("mask_u8", [RT, SK], U8)
        self.c_hi = [sc.sb(f"c_hi{p}", [KT, NKT, DC], F32R) for p in range(2)]
        self.c_lo = [sc.sb(f"c_lo{p}", [KT, NKT, DC], F32R) for p in range(2)]
        self.cT_hi = [sc.sb(f"cT_hi{p}", [DC, SK], F32R) for p in range(2)]
        self.cT_lo = [sc.sb(f"cT_lo{p}", [DC, SK], F32R) for p in range(2)]
        self.q_hi = [sc.sb(f"q_hi{p}", [DC, H0 * S], F32R) for p in range(2)]
        self.q_lo = [sc.sb(f"q_lo{p}", [DC, H0 * S], F32R) for p in range(2)]
        self.mask_add = [sc.sb(f"mask_add{p}", [RT, SK]) for p in range(2)]
        self.ones_set, self.ctx_loaded, self.q_loaded = sc.sem("ones_set"), sc.sem("ctx_ld"), sc.sem("q_ld")
        self.pool_steps = sc.sem("pool_steps")

    def load_context(self, sp, b):
        sp.dma_start(self.rawT[:, :], self.ctxT_in[bass.ds(b, 1)].rearrange("b c k -> c (b k)")
                     ).then_inc(self.ctx_loaded, 16)
        sp.dma_start(self.mask_u8[:, :], self.mask_in[bass.ds(b, 1)].rearrange("b k -> (b k)").partition_broadcast(RT)
                     ).then_inc(self.ctx_loaded, 16)
        sp.dma_start(self.raw[:, :, :], self.ctx_in[bass.ds(b, 1)].rearrange("b (n p) c -> p (b n) c", p=KT)
                     ).then_inc(self.ctx_loaded, 16)

    def load_queries(self, sp, b):
        sp.dma_start(self.q_raw[:, :], self.q_d[:, bass.ds(b, 1)].rearrange("c b h t -> c (b h t)")
                     ).then_inc(self.q_loaded, 16)

    def split_scores_part(self, pool, b, p):
        done = self.STEPS * b
        pool.wait_ge(self.ctx_loaded, 48 * (b + 1))
        upper_part(pool, self.cT_hi[p][:, :], self.rawT[:, :], self.ones).then_inc(self.pool_steps, 1)
        pool.tensor_scalar(self.mask_add[p][:, :], self.mask_u8[:, :], 1.0, BIG, ALU.subtract, ALU.mult
                           ).then_inc(self.pool_steps, 1)
        pool.wait_ge(self.pool_steps, done + 1)
        pool.tensor_tensor(self.cT_lo[p][:, :], self.rawT[:, :], self.cT_hi[p][:, :].bitcast(F32), ALU.subtract
                           ).then_inc(self.pool_steps, 1)

    def split_queries(self, pool, b, p):
        pool.wait_ge(self.q_loaded, 16 * (b + 1))
        upper_part(pool, self.q_hi[p][:, :], self.q_raw[:, :], self.ones).then_inc(self.pool_steps, 1)
        pool.wait_ge(self.pool_steps, self.STEPS * b + 4)
        pool.tensor_tensor(self.q_lo[p][:, :], self.q_raw[:, :], self.q_hi[p][:, :].bitcast(F32), ALU.subtract
                           ).then_inc(self.pool_steps, 1)

    def split_context(self, pool, b, p):
        upper_part(pool, self.c_hi[p][:, :, :].rearrange("p n c -> p (n c)"),
                   self.raw[:, :, :].rearrange("p n c -> p (n c)"), self.ones).then_inc(self.pool_steps, 1)
        pool.wait_ge(self.pool_steps, self.STEPS * b + 6)
        pool.tensor_tensor(self.c_lo[p][:, :, :], self.raw[:, :, :], self.c_hi[p][:, :, :].bitcast(F32), ALU.subtract
                           ).then_inc(self.pool_steps, 1)


def project_queries(nc, x_in, wqT, wkT, ident_in, cx):
    with ExitStack() as ctx:
        sc = ClearedScope(nc, ctx, "pq")
        ctx.callback(sc.clear)
        ident = sc.sb("ident", [128, 128])
        wqT_sb = sc.sb("wqT", [128, H0, D])
        wkT_sb = sc.sb("wkT", [128, H0 // G0, DC])
        wqk_hi = sc.sb("wqk_hi", [128, CH, H0, DC], F32R)
        wqk_lo = sc.sb("wqk_lo", [128, CH, H0, DC], F32R)
        x = sc.sb("x", [TT, NTILE, D])
        xn = x
        xnT_hi = sc.sb("xnT_hi", [128, CH, NT], F32R)
        xnT_lo = sc.sb("xnT_lo", [128, CH, NT], F32R)
        HQ = H0 // 2
        q = [sc.sb(f"q{k}", [128, B // 2, HQ, S]) for k in range(3)]
        scratch = ln_scratch(sc)
        fold_ps = [sc.ps(f"fold{k}", [128, 512]) for k in range(2)]
        tr_ps = [sc.ps(f"tr{k}", [128, 512]) for k in range(2)]
        q_ps = [sc.ps(f"q_ps{k}", [128, 512]) for k in range(4)]
        x_loaded, w_loaded, id_loaded = (sc.sem(n) for n in ("x_ld", "w_ld", "id_ld"))
        dve_steps, xn_ready = sc.sem("dve_steps"), sc.sem("xn_ready")
        folded, fold_hi, fold_kept = sc.sem("folded"), sc.sem("fold_hi"), sc.sem("fold_kept")
        turned, turn_hi, turn_kept = sc.sem("turned"), sc.sem("turn_hi"), sc.sem("turn_kept")
        q_made, q_kept, first_stored, q_stored = (sc.sem(n) for n in ("q_made", "q_kept", "first_stored", "q_stored"))
        NFOLD = H0 // 2
        FILLS = 2 * CH
        block = ctx.enter_context(nc.Block())

        @block.sync
        def _(sp):
            sp.dma_start(x[:, :, :], x_in.rearrange("(n p) d -> p n d", p=TT)).then_inc(x_loaded, 16)
            sp.dma_start(wkT_sb[:, :, :], wkT.rearrange("(h p) c -> p h c", p=HD0)).then_inc(w_loaded, 16)
            sp.dma_start(wqT_sb[:, :, :], wqT.rearrange("(h p) d -> p h d", p=HD0)).then_inc(w_loaded, 16)
            sp.dma_start(ident[:, :], ident_in).then_inc(id_loaded, 16)
            cx.load_context(sp, 0)
            for part in range(4):
                half, k = part // 2, part % 2
                sp.wait_ge(q_kept, HQ * (part + 1))
                sp.dma_start(cx.q_d[:, half * B // 2:(half + 1) * B // 2, k * HQ:(k + 1) * HQ, :], q[part % 3][:, :, :, :]
                             ).then_inc(q_stored if part else first_stored, 16)
            sp.wait_ge(q_stored, 48)

        @block.gpsimd
        def _(pool):
            pool.memset(cx.ones[:, :], 1.0).then_inc(cx.ones_set, 1)
            pool.wait_ge(cx.ones_set, 1)
            cx.split_scores_part(pool, 0, 0)

        @block.tensor
        def _(pe):
            pe.wait_ge(w_loaded, 32)
            for n in range(NFOLD):
                if n >= 2:
                    pe.wait_ge(fold_kept, n - 1)
                for k in range(2):
                    h = 2 * n + k
                    for c in range(CH):
                        mm = pe.matmul(fold_ps[n % 2][:, (k * CH + c) * 128:(k * CH + c + 1) * 128],
                                       wqT_sb[:, h, c * 128:(c + 1) * 128], wkT_sb[:, h // G0, :],
                                       start=True, stop=True)
                mm.then_inc(folded, 1)
            pe.wait_ge(id_loaded, 16)
            for f in range(FILLS):
                if f >= 2:
                    pe.wait_ge(turn_kept, f - 1)
                half, c = f // CH, f % CH
                pe.wait_ge(xn_ready, 4 * (half + 1))
                for k in range(4):
                    mm = pe.transpose(tr_ps[f % 2][:, k * TT:(k + 1) * TT],
                                      xn[:, 4 * half + k, c * 128:(c + 1) * 128], ident[0:TT, 0:TT])
                mm.then_inc(turned, 1)
            pe.wait_ge(fold_kept, NFOLD)
            for half in range(2):
                pe.wait_ge(turn_kept, CH * (half + 1))
                for h in range(H0):
                    n = half * H0 + h
                    if n >= 4:
                        pe.wait_ge(q_kept, n - 3)
                    cols = slice(half * HALF, (half + 1) * HALF)
                    for c in range(CH):
                        mm = three_passes(pe, q_ps[n % 4][:, 0:HALF], wqk_hi[:, c, h, :], wqk_lo[:, c, h, :],
                                          xnT_hi[:, c, cols], xnT_lo[:, c, cols], c == 0, c == CH - 1)
                    mm.then_inc(q_made, 1)

        @block.scalar
        def _(act):
            for n in range(NFOLD):
                act.wait_ge(folded, n + 1)
                act.copy(wqk_hi[:, :, 2 * n:2 * n + 2, :].rearrange("p c k n -> p k c n"),
                         fold_ps[n % 2][:, :].rearrange("p (k c n) -> p k c n", k=2, c=CH)).then_inc(fold_hi, 1)
            for f in range(FILLS):
                act.wait_ge(turned, f + 1)
                half, c = f // CH, f % CH
                act.copy(xnT_hi[:, c, half * HALF:(half + 1) * HALF], tr_ps[f % 2][:, 0:HALF]).then_inc(turn_hi, 1)
            for n in range(2 * H0):
                act.wait_ge(q_made, n + 1)
                if n == 3 * HQ:
                    act.wait_ge(first_stored, 16)
                act.copy(q[n // HQ % 3][:, :, n % HQ, :], q_ps[n % 4][:, 0:HALF].rearrange("p (b t) -> p b t", t=S)
                         ).then_inc(q_kept, 1)

        @block.vector
        def _(dve):
            ch = Chain(dve, dve_steps)
            dve.wait_ge(x_loaded, 16)
            layer_norm(ch, xn[:, :, :], x[:, :, :], *scratch, TT, xn_ready)
            for n in range(NFOLD):
                dve.wait_ge(fold_hi, n + 1)
                hs = slice(2 * n, 2 * n + 2)
                dve.tensor_tensor(wqk_lo[:, :, hs, :].rearrange("p c k n -> p k c n"),
                                  fold_ps[n % 2][:, :].rearrange("p (k c n) -> p k c n", k=2, c=CH),
                                  wqk_hi[:, :, hs, :].rearrange("p c k n -> p k c n").bitcast(F32), ALU.subtract
                                  ).then_inc(fold_kept, 1)
            for f in range(FILLS):
                dve.wait_ge(turn_hi, f + 1)
                cols = slice(f // CH * HALF, (f // CH + 1) * HALF)
                dve.tensor_tensor(xnT_lo[:, f % CH, cols], tr_ps[f % 2][:, 0:HALF],
                                  xnT_hi[:, f % CH, cols].bitcast(F32), ALU.subtract).then_inc(turn_kept, 1)


RT = 128
NRT = H0 * S // RT
UNIT_TILES = (4, 3)
UNIT = 4


def attend_context(nc, ident_in, cx, o_d):
    SCALE = float(HD0) ** -0.5
    NS = NCH
    STEPS = 2 * NRT
    FIRST = UNIT_TILES[0]
    with ExitStack() as ctx:
        sc = Scope(nc, ctx, "a0")
        ident = sc.sb("ident", [128, 128])
        any_key = sc.sb("any_key", [RT, 2])
        probs = [sc.sb(f"probs{p}", [RT, SK]) for p in range(2)]
        pT_hi = [sc.sb(f"pT_hi{h}", [KT, NKT, UNIT_TILES[h] * RT], F32R) for h in range(2)]
        pT_lo = [sc.sb(f"pT_lo{h}", [KT, NKT, UNIT_TILES[h] * RT], F32R) for h in range(2)]
        part_min = sc.sb("part_min", [RT, 2, NCH])
        row_min = sc.sb("row_min", [RT, 2])
        carrier = sc.sb("carrier", [1, 2, NCH])
        sums = sc.sb("sums", [RT, 2, FIRST])
        inv = sc.sb("inv", [RT, FIRST])
        inv_diag = sc.sb("inv_diag", [RT, FIRST, RT])
        inv_all = sc.sb("inv_all", [128, FIRST * RT])
        o_sb = sc.sb("o", [DC, FIRST * RT])
        s_ps = [sc.ps(f"s{k}", [128, 512]) for k in range(NS)]
        t_ps = [sc.ps(f"t{k}", [128, 512]) for k in range(NS)]
        o_ps = sc.ps("o_ps", [128, 512])
        i_ps = sc.ps("i_ps", [128, 512])

        id_loaded = sc.sem("id_ld")
        scored, score_kept = sc.sem("scored"), sc.sem("score_kept")
        row_max, dve_steps = sc.sem("row_max"), sc.sem("dve_steps")
        probs_made = sc.sem("probs_made")
        turned, turn_hi, turn_kept = sc.sem("turned"), sc.sem("turn_hi"), sc.sem("turn_kept")
        diag_made, inv_spread, inv_kept = sc.sem("diag_made"), sc.sem("inv_spread"), sc.sem("inv_kept")
        summed, o_kept, o_stored = sc.sem("summed"), sc.sem("o_kept"), sc.sem("o_stored")
        block = ctx.enter_context(nc.Block())

        def bodies(eng, body, last):
            body(0, True)
            with eng.Fori(1, B // 2) as i:
                body(i, False)
            last()

        def place(s):
            p, q = s // NRT, s % NRT
            return p, int(q >= FIRST), q - FIRST * (q >= FIRST)

        @block.sync
        def _(sp):
            sp.dma_start(ident[:, :], ident_in).then_inc(id_loaded, 16)

            def body(i, first):
                for p in range(2):
                    b = 2 * i + p
                    if not (first and p == 0):
                        sp.wait_ge(cx.pool_steps, cx.STEPS * b)
                        cx.load_context(sp, b)
                    cx.load_queries(sp, b)

            bodies(sp, body, lambda: None)

        @block.gpsimd
        def _(pool):
            def body(i, first):
                for p in range(2):
                    b = 2 * i + p
                    wait(pool, scored, NRT * NCH * (b - 1))
                    wait(pool, score_kept, NRT * NCH * (b - 1))
                    if not (first and p == 0):
                        cx.split_scores_part(pool, b, p)
                    cx.split_queries(pool, b, p)
                    wait(pool, summed, 2 * (b - 1))
                    cx.split_context(pool, b, p)

            bodies(pool, body, lambda: None)

        @block.tensor
        def _(pe):
            pe.wait_ge(id_loaded, 16)

            def scores(g, s):
                p, r = s // NRT, s % NRT
                rows = slice(r * RT, (r + 1) * RT)
                for c in range(NCH):
                    n = NCH * g + c
                    wait(pe, score_kept, n - NS + 1)
                    keys = slice(c * CK, (c + 1) * CK)
                    three_passes(pe, s_ps[c][:, 0:CK], cx.q_hi[p][:, rows], cx.q_lo[p][:, rows],
                                 cx.cT_hi[p][:, keys], cx.cT_lo[p][:, keys], True, True).then_inc(scored, 1)

            def turn(g, s):
                pe.wait_ge(probs_made, g + 1)
                for f in range(NCH):
                    n = NCH * g + f
                    wait(pe, turn_kept, n - NS + 1)
                    for k in range(4):
                        j = 4 * f + k
                        mm = pe.transpose(t_ps[f][0:KT, k * RT:(k + 1) * RT],
                                          probs[s % 2][:, j * KT:(j + 1) * KT], ident[:, :])
                    mm.then_inc(turned, 1)

            def spread(u, unit):
                n = UNIT_TILES[unit]
                pe.wait_ge(diag_made, u + 1)
                wait(pe, inv_kept, u)
                pe.matmul(i_ps[:, 0:n * RT], cx.ones[:, :], inv_diag[:, 0:n, :].rearrange("p k t -> p (k t)"),
                          start=True, stop=True).then_inc(inv_spread, 1)

            def weigh(g_last, p, unit, tiles):
                for j in tiles:
                    if j % 4 == 0 or j == tiles[0]:
                        pe.wait_ge(turn_kept, NCH * g_last + j // 4 + 1)
                    mm = three_passes(pe, o_ps[:, 0:UNIT_TILES[unit] * RT], cx.c_hi[p][:, j, :], cx.c_lo[p][:, j, :],
                                      pT_hi[unit][:, j, :], pT_lo[unit][:, j, :], j == 0, j == NKT - 1)
                if tiles[-1] == NKT - 1:
                    mm.then_inc(summed, 1)

            def body(i, first):
                for s in range(STEPS):
                    g, q, p = STEPS * i + s, s % NRT, s // NRT
                    b = 2 * i + p
                    if q == 0:
                        pe.wait_ge(cx.pool_steps, cx.STEPS * b + cx.SCORES_READY)
                    scores(g, s)
                    if not (first and s == 0):
                        turn(g - 1, (s - 1) % STEPS)
                    if q >= FIRST:
                        if q == FIRST:
                            wait(pe, o_kept, 2 * b)
                            pe.wait_ge(cx.pool_steps, cx.STEPS * (b + 1))
                        if q == FIRST + 1:
                            spread(2 * b, 0)
                        k = q - FIRST
                        weigh(g - 1 - k, p, 0, range(4 * k, 4 * (k + 1)))
                    elif not (first and p == 0):
                        if q == 0:
                            pe.wait_ge(o_kept, 2 * b - 1)
                        if q == 1:
                            spread(2 * b - 1, 1)
                        weigh(g - 1 - q, (p + 1) % 2, 1, range(3 * q, 3 * (q + 1)))

            def last():
                turn(NRT * B - 1, STEPS - 1)
                pe.wait_ge(o_kept, 2 * B - 1)
                spread(2 * B - 1, 1)
                weigh(NRT * B - 1, 1, 1, range(NKT))

            bodies(pe, body, last)

        @block.scalar
        def _(act):
            def upper(g, s, u):
                p, unit, r = place(s)
                for f in range(NCH):
                    act.wait_ge(turned, NCH * g + f + 1)
                    if f == 0 and r == 0:
                        wait(act, summed, u - 1)
                    act.copy(pT_hi[unit][:, 4 * f:4 * f + 4, r * RT:(r + 1) * RT],
                             t_ps[f][0:KT, :].rearrange("p (k t) -> p k t", t=RT)).then_inc(turn_hi, 1)

            def spread(u, unit):
                n = UNIT_TILES[unit] * RT
                act.wait_ge(inv_spread, u + 1)
                wait(act, o_kept, u)
                act.copy(inv_all[:, 0:n], i_ps[:, 0:n]).then_inc(inv_kept, 1)

            def store(u, b, unit):
                rows = slice(unit * FIRST * RT, (FIRST + unit * UNIT_TILES[1]) * RT)
                act.wait_ge(o_kept, u + 1)
                act.dma_start(o_d[:, bass.ds(b, 1), rows].rearrange("c b r -> c (b r)"),
                              o_sb[:, 0:UNIT_TILES[unit] * RT]).then_inc(o_stored, 16)

            def body(i, first):
                for s in range(STEPS):
                    g, q, p = STEPS * i + s, s % NRT, s // NRT
                    b = 2 * i + p
                    if not (first and s == 0):
                        pp, unit, _ = place((s - 1) % STEPS)
                        upper(g - 1, (s - 1) % STEPS, 2 * (2 * i + (s - 1) // NRT) + unit)
                    if q == 1 and not (first and p == 0):
                        store(2 * b - 2, b - 1, 0)
                    if q == FIRST + 1 and not (first and p == 0):
                        store(2 * b - 1, b - 1, 1)
                    act.wait_ge(row_max, g + 1)
                    _, unit, r = place(s)
                    act.activation(probs[s % 2][:, :], probs[s % 2][:, :], ACT.Exp, scale=-1.0,
                                   bias=row_min[:, s % 2:s % 2 + 1],
                                   accum_out=sums[:, unit, r:r + 1]).then_inc(probs_made, 1)
                    if q == 1 and not (first and p == 0):
                        spread(2 * b - 1, 1)
                    if q == FIRST + 1:
                        spread(2 * b, 0)

            def last():
                store(2 * B - 2, B - 1, 0)
                upper(NRT * B - 1, STEPS - 1, 2 * B - 1)
                spread(2 * B - 1, 1)
                store(2 * B - 1, B - 1, 1)
                act.wait_ge(o_stored, 16 * 2 * B)

            bodies(act, body, last)

        @block.vector
        def _(dve):
            FLAG_N, UNIT_N = 2, 2
            PER_BODY = 2 * FLAG_N + 4 * UNIT_N

            def masked(g, s):
                p = s // NRT
                wait(dve, turned, NCH * (g - 1))
                for c in range(NCH):
                    keys = slice(c * CK, (c + 1) * CK)
                    dve.wait_ge(scored, NCH * g + c + 1)
                    dve.memset(carrier[:, s % 2, c:c + 1], 0.0)
                    ins = dve.tensor_tensor_reduce(
                        probs[s % 2][:, keys], s_ps[c][:, 0:CK], cx.mask_add[p][:, keys],
                        -SCALE, BIG, ALU.add, ALU.min, part_min[:, s % 2, c:c + 1])
                    ins.then_inc(score_kept, 1)
                dve.wait_ge(score_kept, NCH * g + NCH)
                dve.tensor_reduce(row_min[:, s % 2:s % 2 + 1], part_min[:, s % 2, :], AX.X, ALU.min
                                  ).then_inc(row_max, 1)

            def rest(g, s):
                _, unit, r = place(s)
                for f in range(NCH):
                    dve.wait_ge(turn_hi, NCH * g + f + 1)
                    rows = slice(r * RT, (r + 1) * RT)
                    dve.tensor_tensor(pT_lo[unit][:, 4 * f:4 * f + 4, rows],
                                      t_ps[f][0:KT, :].rearrange("p (k t) -> p k t", t=RT),
                                      pT_hi[unit][:, 4 * f:4 * f + 4, rows].bitcast(F32), ALU.subtract
                                      ).then_inc(turn_kept, 1)

            def invert(u, p, unit, ch):
                n = UNIT_TILES[unit]
                ch.link(dve.reciprocal(inv[:, 0:n], sums[:, unit, 0:n]))
                ch.link(dve.tensor_scalar(inv[:, 0:n], inv[:, 0:n], any_key[:, p:p + 1], None, ALU.mult))
                wait(dve, inv_spread, u)
                dve.tensor_tensor(inv_diag[:, 0:n, :],
                                  ident[:, :].rearrange("p (a t) -> p a t", a=1).broadcast_to([RT, n, RT]),
                                  inv[:, 0:n].rearrange("p (k a) -> p k a", a=1).broadcast_to([RT, n, RT]),
                                  ALU.mult).then_inc(diag_made, 1)

            def finish(u, unit):
                n = UNIT_TILES[unit] * RT
                dve.wait_ge(summed, u + 1)
                dve.wait_ge(inv_kept, u + 1)
                wait(dve, o_stored, 16 * u)
                dve.tensor_tensor(o_sb[:, 0:n], o_ps[:, 0:n], inv_all[:, 0:n], ALU.mult).then_inc(o_kept, 1)

            def body(i, first):
                ch = Chain(dve, dve_steps, PER_BODY * i - (0 if first else UNIT_N))
                for s in range(STEPS):
                    g, q, p = STEPS * i + s, s % NRT, s // NRT
                    b = 2 * i + p
                    if q == 0:
                        dve.wait_ge(cx.pool_steps, cx.STEPS * b + cx.SCORES_READY)
                    if q == 0 and not (first and p == 0):
                        finish(2 * b - 2, 0)
                    if q == FIRST and not (first and p == 0):
                        finish(2 * b - 1, 1)
                    masked(g, s)
                    if not (first and s == 0):
                        rest(g - 1, (s - 1) % STEPS)
                    if q == 0 and not (first and p == 0):
                        dve.wait_ge(probs_made, g)
                        invert(2 * b - 1, (p + 1) % 2, 1, ch)
                    if q == FIRST:
                        dve.wait_ge(probs_made, g)
                        invert(2 * b, p, 0, ch)
                    if q == 1:
                        ch.link(dve.tensor_reduce(any_key[:, p:p + 1], cx.mask_add[p][:, :], AX.X, ALU.max))
                        ch.link(dve.tensor_scalar(any_key[:, p:p + 1], any_key[:, p:p + 1], 0.0, None, ALU.is_ge))

            def last():
                ch = Chain(dve, dve_steps, PER_BODY * (B // 2) - UNIT_N)
                finish(2 * B - 2, 0)
                dve.wait_ge(probs_made, NRT * B)
                invert(2 * B - 1, 1, 1, ch)
                rest(NRT * B - 1, STEPS - 1)
                finish(2 * B - 1, 1)

            bodies(dve, body, last)


class FeedForwardWeights:

    def __init__(self, sc, w1T, w3T, w2T, hadamard, ident):
        self.sources = w1T, w3T, w2T, hadamard, ident
        self.ident = sc.sb("ident", [128, 128])
        self.had = sc.sb("had", [128, 128])
        self.w1 = sc.sb("w1", [128, CH, FF])
        self.w3 = sc.sb("w3", [128, CH, FF])
        self.w2 = sc.sb("w2", [128, FF // 128, D])
        self.id_loaded, self.w2_loaded, self.w_loaded = sc.sem("id_ld"), sc.sem("w2_ld"), sc.sem("w_ld")

    def load(self, sp):
        w1T, w3T, w2T, hadamard, ident = self.sources
        sp.dma_start(self.ident[:, :], ident).then_inc(self.id_loaded, 16)
        sp.dma_start(self.had[:, :], hadamard).then_inc(self.w2_loaded, 16)
        sp.dma_start(self.w2[:, :, :], w2T.rearrange("(k p) d -> p k d", p=128)).then_inc(self.w2_loaded, 16)
        sp.dma_start(self.w1[:, :, :], w1T.rearrange("(c p) h -> p c h", p=128)).then_inc(self.w_loaded, 16)
        sp.dma_start(self.w3[:, :, :], w3T.rearrange("(c p) h -> p c h", p=128)).then_inc(self.w_loaded, 16)


def close_attention(nc, o_d, x_in, wvT, wo, gates_in, xs, gate, fw):
    BQ = B // 4
    with ExitStack() as ctx:
        sc = Scope(nc, ctx, "c0")
        wvT_sb = sc.sb("wvT", [128, H0 // G0, DC])
        wo_sb = sc.sb("wo", [128, H0, D])
        wvo_hi = sc.sb("wvo_hi", [DC, H0, D], F32R)
        wvo_lo = sc.sb("wvo_lo", [DC, H0, D], F32R)
        raw = [sc.sb(f"raw{k}", [DC, BQ, H0, S]) for k in range(2)]
        oT_hi = [sc.sb(f"oT_hi{k}", [DC, H0, BQ, S], F32R) for k in range(2)]
        oT_lo = [sc.sb(f"oT_lo{k}", [DC, H0, BQ, S], F32R) for k in range(2)]
        x = sc.sb("x", [TT, NTILE, D])
        gates = sc.sb("gates", [TT, 4])
        f_ps = [sc.ps(f"f{k}", [128, 512]) for k in range(4)]
        y_ps = [sc.ps(f"y{k}", [128, 512]) for k in range(4)]
        w_loaded = [sc.sem(f"w_ld{k}") for k in range(2)]
        x_loaded, g_loaded = sc.sem("x_ld"), sc.sem("g_ld")
        o_loaded = [sc.sem(f"o_ld{k}") for k in range(4)]
        folded, fold_hi, fold_kept = sc.sem("folded"), sc.sem("fold_hi"), sc.sem("fold_kept")
        gate_made, oT_hi_made, oT_ready = sc.sem("gate_made"), sc.sem("oT_hi_made"), sc.sem("oT_ready")
        projected, added = sc.sem("projected"), sc.sem("added")
        block = ctx.enter_context(nc.Block())

        @block.sync
        def _(sp):
            sp.dma_start(gates[:, :], gates_in.partition_broadcast(TT)).then_inc(g_loaded, 16)
            def weights():
                sp.dma_start(wvT_sb[:, :, :], wvT.rearrange("(g p) c -> p g c", p=HD0)).then_inc(w_loaded[0], 16)
                for k in range(2):
                    hs = slice(k * H0 // 2, (k + 1) * H0 // 2)
                    sp.dma_start(wo_sb[:, hs, :], wo.rearrange("(h p) d -> p h d", p=HD0)[:, hs, :]
                                 ).then_inc(w_loaded[k], 16)

            for k in range(4):
                if k == 1:
                    weights()
                if k >= 2:
                    sp.wait_ge(oT_ready, k - 1)
                sp.dma_start(raw[k % 2][:, :, :, :].rearrange("c b h t -> c b (h t)"),
                             o_d[:, k * BQ:(k + 1) * BQ, :]).then_inc(o_loaded[k], 16)
            sp.dma_start(x[:, :, :], x_in.rearrange("(n p) d -> p n d", p=TT)).then_inc(x_loaded, 16)
            fw.load(sp)

        @block.tensor
        def _(pe):
            pe.wait_ge(w_loaded[0], 32)
            for n in range(H0 // 2):
                if n == H0 // 4:
                    pe.wait_ge(w_loaded[1], 16)
                if n >= 4:
                    pe.wait_ge(fold_kept, n - 3)
                for k in range(2):
                    h = 2 * n + k
                    mm = pe.matmul(f_ps[n % 4][:, k * D:(k + 1) * D], wvT_sb[:, h // G0, :], wo_sb[:, h, :],
                                   start=True, stop=True)
                mm.then_inc(folded, 1)
            pe.wait_ge(fold_kept, H0 // 2)
            for t in range(NTILE):
                k, bs = t // 2, slice(2 * (t % 2), 2 * (t % 2) + 2)
                pe.wait_ge(oT_ready, k + 1)
                if t >= 4:
                    pe.wait_ge(added, t - 3)
                for h in range(H0):
                    mm = three_passes(pe, y_ps[t % 4][0:TT, 0:D],
                                      oT_hi[k % 2][:, h, bs, :].rearrange("c b t -> c (b t)"),
                                      oT_lo[k % 2][:, h, bs, :].rearrange("c b t -> c (b t)"),
                                      wvo_hi[:, h, :], wvo_lo[:, h, :], h == 0, h == H0 - 1)
                mm.then_inc(projected, 1)

        @block.scalar
        def _(act):
            def oT_upper(k):
                act.wait_ge(o_loaded[k], 16)
                if k >= 2:
                    act.wait_ge(projected, 2 * (k - 1))
                act.copy(oT_hi[k % 2][:, :, :, :], raw[k % 2][:, :, :, :].rearrange("c b h t -> c h b t")
                         ).then_inc(oT_hi_made, 1)

            act.wait_ge(g_loaded, 16)
            act.activation(gate[:, :], gates[:, :], ACT.Tanh).then_inc(gate_made, 1)
            oT_upper(0)
            for n in range(H0 // 2):
                act.wait_ge(folded, n + 1)
                act.copy(wvo_hi[:, 2 * n:2 * n + 2, :], f_ps[n % 4][:, :].rearrange("p (k d) -> p k d", k=2)
                         ).then_inc(fold_hi, 1)
            for k in range(1, 4):
                oT_upper(k)

        @block.vector
        def _(dve):
            def rest(k):
                dve.wait_ge(oT_hi_made, k + 1)
                dve.tensor_tensor(oT_lo[k % 2][:, :, :, :], raw[k % 2][:, :, :, :].rearrange("c b h t -> c h b t"),
                                  oT_hi[k % 2][:, :, :, :].bitcast(F32), ALU.subtract).then_inc(oT_ready, 1)

            rest(0)
            for n in range(H0 // 2):
                dve.wait_ge(fold_hi, n + 1)
                dve.tensor_tensor(wvo_lo[:, 2 * n:2 * n + 2, :], f_ps[n % 4][:, :].rearrange("p (k d) -> p k d", k=2),
                                  wvo_hi[:, 2 * n:2 * n + 2, :].bitcast(F32), ALU.subtract).then_inc(fold_kept, 1)
            rest(1)
            dve.wait_ge(gate_made, 1)
            dve.wait_ge(x_loaded, 16)
            for t in range(NTILE):
                if t in (2, 4):
                    rest(t // 2 + 1)
                dve.wait_ge(projected, t + 1)
                dve.scalar_tensor_tensor(xs[:, t, :], y_ps[t % 4][0:TT, 0:D], gate[:, 0:1], x[:, t, :],
                                         ALU.mult, ALU.add).then_inc(added, 1)


def turn_tokens(pe, act, xn, xnT, banks, ident, ready, turned, taken, kept, affine=None):
    if pe is not None:
        for f in range(2 * CH):
            half, c = f // CH, f % CH
            pe.wait_ge(ready, 4 * (half + 1))
            if f >= 2:
                pe.wait_ge(kept, f - 1)
            for k in range(4):
                mm = pe.transpose(banks[f % 2][:, k * TT:(k + 1) * TT], xn[:, 4 * half + k, c * 128:(c + 1) * 128],
                                  ident[0:TT, 0:TT])
            mm.then_inc(turned, 1)
    if act is not None:
        for f in range(2 * CH):
            half, c = f // CH, f % CH
            act.wait_ge(turned, f + 1)
            out = xnT[:, c, half * HALF:(half + 1) * HALF]
            if affine is None:
                act.copy(out, banks[f % 2][:, 0:HALF]).then_inc(taken, 1)
            else:
                act.activation(out, banks[f % 2][:, 0:HALF], ACT.Identity, scale=affine[:, 0:1], bias=affine[:, 1:2]
                               ).then_inc(taken, 1)


def feed_forward(nc, fw, xs, gate):
    NH = FF // 128
    with ExitStack() as ctx:
        sc = Scope(nc, ctx, "ff")
        ident, had, w1, w3, w2 = fw.ident, fw.had, fw.w1, fw.w3, fw.w2
        w_hi = sc.sb("w_hi", [128, 2, CH, FF], F32R)
        w_lo = sc.sb("w_lo", [128, 2, CH, FF], F32R)
        w2_hi = sc.sb("w2_hi", [128, NH, D], F32R)
        w2_lo = sc.sb("w2_lo", [128, NH, D], F32R)
        fly = [sc.sb(f"fly{k}", [128, NH, D]) for k in range(2)]
        xn = sc.sb("xn", [TT, NTILE, D])
        xnT_hi = sc.sb("xnT_hi", [128, CH, NT], F32R)
        xnT_lo = sc.sb("xnT_lo", [128, CH, NT], F32R)
        act_g = [sc.sb(f"act_g{k}", [128, HALF]) for k in range(2)]
        hidden = [sc.sb(f"hidden{k}", [128, HALF]) for k in range(2)]
        h_hi = sc.sb("h_hi", [128, NH, NT], F32R)
        h_lo = sc.sb("h_lo", [128, NH, NT], F32R)
        scratch = ln_scratch(sc)
        banks = [sc.ps(f"b{k}", [128, 512]) for k in range(8)]
        dve_steps, xn_ready = sc.sem("dve_steps"), sc.sem("xn_ready")
        mixed, mix_kept = sc.sem("mixed"), sc.sem("mix_kept")
        turned, turn_hi, turn_kept = sc.sem("turned"), sc.sem("turn_hi"), sc.sem("turn_kept")
        gate_up, silu_made, hidden_made = sc.sem("gate_up"), sc.sem("silu_made"), sc.sem("hidden_made")
        w_upper, w_rest, h_upper, h_rest = (sc.sem(n) for n in ("w_upper", "w_rest", "h_upper", "h_rest"))
        w2_made, w2_upper, w2_ready = sc.sem("w2_made"), sc.sem("w2_upper"), sc.sem("w2_ready")
        projected, added = sc.sem("projected"), sc.sem("added")
        block = ctx.enter_context(nc.Block())

        @block.tensor
        def _(pe):
            pe.wait_ge(fw.id_loaded, 16)
            pe.wait_ge(fw.w2_loaded, 32)
            for k in range(NH // 2):
                for c in range(2):
                    mm = pe.matmul(banks[4 + k][:, c * D:(c + 1) * D], had[:, :], w2[:, 2 * k + c, :],
                                   start=True, stop=True)
                mm.then_inc(mixed, 1)
            turn_tokens(pe, None, xn, xnT_hi, banks[0:2], ident, xn_ready, turned, turn_hi, turn_kept)
            pe.wait_ge(w_rest, 2)
            pe.wait_ge(turn_kept, 2 * CH)
            pe.wait_ge(mix_kept, NH // 2)
            for n in range(2 * NH):
                half, k = n // NH, n % NH
                if n >= 4:
                    pe.wait_ge(hidden_made, n - 3)
                units, cols = slice(k * 128, (k + 1) * 128), slice(half * HALF, (half + 1) * HALF)
                for w, bank in ((0, banks[n % 4]), (1, banks[4 + n % 4])):
                    for c in range(CH):
                        mm = three_passes(pe, bank[:, 0:HALF], w_hi[:, w, c, units], w_lo[:, w, c, units],
                                          xnT_hi[:, c, cols], xnT_lo[:, c, cols], c == 0, c == CH - 1)
                mm.then_inc(gate_up, 1)
            pe.wait_ge(w2_ready, 1)
            for t in range(NTILE):
                pe.wait_ge(h_rest, 2 * NH)
                if t >= 4:
                    pe.wait_ge(added, t - 3)
                toks = slice(t * TT, (t + 1) * TT)
                for k in range(NH):
                    mm = three_passes(pe, banks[t % 4][0:TT, 0:D], h_hi[:, k, toks], h_lo[:, k, toks],
                                      w2_hi[:, k, :], w2_lo[:, k, :], k == 0, k == NH - 1)
                mm.then_inc(projected, 1)

        @block.scalar
        def _(act):
            act.wait_ge(fw.w_loaded, 32)
            act.copy(w_hi[:, 1], w3[:, :, :]).then_inc(w_upper, 1)
            act.copy(w_hi[:, 0], w1[:, :, :]).then_inc(w_upper, 1)
            for k in range(NH // 2):
                act.wait_ge(mixed, k + 1)
                act.mul(fly[0][:, 2 * k:2 * k + 2, :], banks[4 + k][:, :].rearrange("p (c d) -> p c d", c=2),
                        float(FF) ** -0.5).then_inc(mix_kept, 1)
            turn_tokens(None, act, xn, xnT_hi, banks[0:2], ident, xn_ready, turned, turn_hi, turn_kept)

            def hidden_upper(n):
                half, k = n // NH, n % NH
                act.wait_ge(hidden_made, n + 1)
                act.copy(h_hi[:, k, half * HALF:(half + 1) * HALF], hidden[n % 2][:, :]).then_inc(h_upper, 1)

            for n in range(2 * NH):
                if n == 4:
                    act.wait_ge(w2_made, 1)
                    act.copy(w2_hi[:, :, :], fly[1][:, :, :]).then_inc(w2_upper, 1)
                if n > 0:
                    hidden_upper(n - 1)
                act.wait_ge(gate_up, n + 1)
                if n >= 2:
                    act.wait_ge(hidden_made, n - 1)
                act.activation(act_g[n % 2][:, :], banks[n % 4][:, 0:HALF], ACT.Silu).then_inc(silu_made, 1)
            hidden_upper(2 * NH - 1)

        @block.gpsimd
        def _(pool):
            pool.wait_ge(w_upper, 1)
            pool.tensor_tensor(w_lo[:, 1], w3[:, :, :], w_hi[:, 1].bitcast(F32), ALU.subtract).then_inc(w_rest, 1)

        @block.vector
        def _(dve):
            ch = Chain(dve, dve_steps)
            layer_norm(ch, xn[:, :, :], xs[:, :, :], *scratch, TT, xn_ready)
            dve.wait_ge(w_upper, 2)
            dve.tensor_tensor(w_lo[:, 0], w1[:, :, :], w_hi[:, 0].bitcast(F32), ALU.subtract).then_inc(w_rest, 1)
            for f in range(2 * CH):
                cols = slice(f // CH * HALF, (f // CH + 1) * HALF)
                dve.wait_ge(turn_hi, f + 1)
                dve.tensor_tensor(xnT_lo[:, f % CH, cols], banks[f % 2][:, 0:HALF],
                                  xnT_hi[:, f % CH, cols].bitcast(F32), ALU.subtract).then_inc(turn_kept, 1)
            dve.wait_ge(mix_kept, NH // 2)
            src, dst = 0, 1
            for st in range(3):
                w = 1 << st
                a = fly[src][:, :, :].rearrange("p (n s w) d -> p n s (w d)", s=2, w=w)
                b = fly[dst][:, :, :].rearrange("p (n s w) d -> p n s (w d)", s=2, w=w)
                ins1 = dve.tensor_tensor(b[:, :, 0, :], a[:, :, 0, :], a[:, :, 1, :], ALU.add)
                ins2 = dve.tensor_tensor(b[:, :, 1, :], a[:, :, 0, :], a[:, :, 1, :], ALU.subtract)
                ch.done(ins1)
                if st < 2:
                    ch.link(ins2)
                else:
                    ch.settle()
                    ins2.then_inc(w2_made, 1)
                src, dst = dst, src

            def hidden_rest(n):
                cols = slice(n // NH * HALF, (n // NH + 1) * HALF)
                dve.wait_ge(h_upper, n + 1)
                dve.tensor_tensor(h_lo[:, n % NH, cols], hidden[n % 2][:, :], h_hi[:, n % NH, cols].bitcast(F32),
                                  ALU.subtract).then_inc(h_rest, 1)

            for n in range(2 * NH):
                if n == 6:
                    dve.wait_ge(w2_upper, 1)
                    dve.tensor_tensor(w2_lo[:, :, :], fly[1][:, :, :], w2_hi[:, :, :].bitcast(F32), ALU.subtract
                                      ).then_inc(w2_ready, 1)
                dve.wait_ge(silu_made, n + 1)
                if n >= 2:
                    dve.wait_ge(h_rest, n - 1)
                dve.tensor_tensor(hidden[n % 2][:, :], banks[4 + n % 4][:, 0:HALF], act_g[n % 2][:, :], ALU.mult
                                  ).then_inc(hidden_made, 1)
                if n > 0:
                    hidden_rest(n - 1)
            hidden_rest(2 * NH - 1)
            for t in range(NTILE):
                dve.wait_ge(projected, t + 1)
                dve.scalar_tensor_tensor(xs[:, t, :], banks[t % 4][0:TT, 0:D], gate[:, 1:2], xs[:, t, :],
                                         ALU.mult, ALU.add).then_inc(added, 1)


GH = H1 // 2
WG = GH * HD1


def project_heads(nc, wq, bq, affine_in, ident_in, xs, qT, x2_d):
    NG = NTILE * H1
    with ExitStack() as ctx:
        sc = Scope(nc, ctx, "p1")
        ident = sc.sb("ident", [128, 128])
        wq_sb = sc.sb("wq", [128, CH, D])
        bq_sb = sc.sb("bq", [TT, D])
        affine = sc.sb("affine", [128, 2])
        xn = sc.sb("xn", [TT, NTILE, D])
        xnT = sc.sb("xnT", [128, CH, NT])
        q = sc.sb("q", [TT, NTILE, D])
        sq = sc.sb("sq", [TT, NTILE, D])
        mean, var, r, t1, t2 = (sc.sb(n, [TT, NG]) for n in ("mean", "var", "r", "t1", "t2"))
        scratch = ln_scratch(sc)
        banks = [sc.ps(f"b{k}", [128, 512]) for k in range(6)]
        loaded, v_loaded, x_stored = sc.sem("ld"), sc.sem("v_ld"), sc.sem("x_stored")
        dve_steps, xn_ready = sc.sem("dve_steps"), sc.sem("xn_ready")
        turned, turn_kept = sc.sem("turned"), sc.sem("turn_kept")
        projected, q_kept, q_ready = sc.sem("projected"), sc.sem("q_kept"), sc.sem("q_ready")
        q_turned, q_turn_kept = sc.sem("q_turned"), sc.sem("q_turn_kept")
        block = ctx.enter_context(nc.Block())

        @block.sync
        def _(sp):
            sp.dma_start(ident[:, :], ident_in).then_inc(loaded, 16)
            sp.dma_start(wq_sb[:, :, :], wq.rearrange("(c p) d -> p c d", p=128)).then_inc(loaded, 16)
            sp.dma_start(bq_sb[:, :], bq.partition_broadcast(TT)).then_inc(v_loaded, 16)
            sp.dma_start(affine[:, :], affine_in).then_inc(loaded, 16)
            sp.dma_start(x2_d.rearrange("(n p) d -> p n d", p=TT), xs[:, :, :]).then_inc(x_stored, 16)
            sp.wait_ge(x_stored, 16)

        @block.tensor
        def _(pe):
            pe.wait_ge(loaded, 48)
            turn_tokens(pe, None, xn, xnT, banks[0:2], ident, xn_ready, turned, turn_kept, turn_kept)
            for t in range(NTILE):
                pe.wait_ge(turn_kept, CH * (t // 4 + 1))
                if t >= 4:
                    pe.wait_ge(q_kept, t - 3)
                for c in range(CH):
                    mm = pe.matmul(banks[2 + t % 4][0:TT, 0:D], xnT[:, c, t * TT:(t + 1) * TT], wq_sb[:, c, :],
                                   start=(c == 0), stop=(c == CH - 1))
                mm.then_inc(projected, 1)
            turn_tokens(pe, None, q, qT, banks[0:2], ident, q_ready, q_turned, q_turn_kept, q_turn_kept)

        @block.scalar
        def _(act):
            turn_tokens(None, act, xn, xnT, banks[0:2], ident, xn_ready, turned, turn_kept, turn_kept)
            act.wait_ge(loaded, 48)
            turn_tokens(None, act, q, qT, banks[0:2], ident, q_ready, q_turned, q_turn_kept, q_turn_kept, affine)

        @block.vector
        def _(dve):
            ch = Chain(dve, dve_steps)
            layer_norm(ch, xn[:, :, :], xs[:, :, :], *scratch, TT, xn_ready)
            dve.wait_ge(v_loaded, 16)
            for t in range(NTILE):
                dve.wait_ge(projected, t + 1)
                dve.tensor_tensor(q[:, t, :], banks[2 + t % 4][0:TT, 0:D], bq_sb[:, :], ALU.add).then_inc(q_kept, 1)
            dve.wait_ge(q_kept, NTILE)

            def heads(x):
                return x[:, :, :].rearrange("p n (h e) -> p (n h) e", e=HD1)

            def of_head(x):
                return x[:, :].rearrange("p (g a) -> p g a", a=1).broadcast_to([TT, NG, HD1])

            ch.link(dve.tensor_reduce(mean[:, :], heads(q), AX.X, ALU.add))
            ch.link(dve.tensor_scalar(mean[:, :], mean[:, :], 1.0 / HD1, None, ALU.mult))
            ch.link(dve.tensor_tensor(heads(q), heads(q), of_head(mean), ALU.subtract))
            ch.link(dve.tensor_tensor(heads(sq), heads(q), heads(q), ALU.mult))
            ch.link(dve.tensor_reduce(var[:, :], heads(sq), AX.X, ALU.add))
            ch.link(dve.tensor_scalar(var[:, :], var[:, :], RSQRT / HD1, EPS_HEAD * RSQRT,
                                          ALU.mult, ALU.add))
            rsqrt(ch, r[:, :], var[:, :], t1[:, :], t2[:, :])
            for half in range(2):
                qh = q[:, 4 * half:4 * half + 4, :].rearrange("p n (h e) -> p (n h) e", e=HD1)
                rh = r[:, half * NG // 2:(half + 1) * NG // 2].rearrange("p (g a) -> p g a", a=1)
                dve.tensor_tensor(qh, qh, rh.broadcast_to([TT, NG // 2, HD1]), ALU.mult).then_inc(q_ready, 4)


def attend_heads(nc, ctxT_in, wkv, bk, affine_in, blocks_in, ident_in, qT):
    SCALE = float(HD1) ** -0.5
    PIECES = (0, 2, 7, 10, 12)
    NS = 3
    STEPS = 2 * UNIT
    with ExitStack() as ctx:
        sc = Scope(nc, ctx, "a1")
        ident = sc.sb("ident", [128, 128])
        w_hi = sc.sb("w_hi", [DC, 2, 2 * WG], F32R)
        w_lo = sc.sb("w_lo", [DC, 2, 2 * WG], F32R)
        w_dca = sc.sb("w_dca", [DC, 2, 2 * WG])
        bias_rows = sc.sb("bias_rows", [96, 2, 2, WG], BF16)
        one_rows = sc.sb("one_rows", [96, 128], BF16)
        affine = sc.sb("affine", [128, 4])
        blocks = sc.sb("blocks", [128, GH])
        ones = sc.sb("ones", [128, 128])
        rawT = sc.sb("rawT", [DC, SK])
        dcaT = sc.sb("dcaT", [DC, DCA])
        cT_hi = sc.sb("cT_hi", [DC, SK], F32R)
        cT_lo = sc.sb("cT_lo", [DC, SK], F32R)
        ctx_loaded, hi_split, split_done = sc.sem("ctx_ld"), sc.sem("hi_split"), sc.sem("split_done")

        def load(sp, b):
            wait(sp, split_done, NCH * b)
            sp.dma_start(rawT[:, :], ctxT_in[bass.ds(b, 1)].rearrange("b c k -> c (b k)")).then_inc(ctx_loaded, 16)

        def split(pool, b, c):
            cols = slice(c * CK, (c + 1) * CK)
            pool.wait_ge(ctx_loaded, 16 * (b + 1))
            if c == 0:
                upper_part(pool, dcaT[:, :], rawT[:, 0:DCA], ones).then_inc(hi_split, 1)
            upper_part(pool, cT_hi[:, cols], rawT[:, cols], ones).then_inc(hi_split, 1)
            pool.wait_ge(hi_split, (NCH + 1) * b + c + 2)
            pool.tensor_tensor(cT_lo[:, cols], rawT[:, cols], cT_hi[:, cols].bitcast(F32), ALU.subtract
                               ).then_inc(split_done, 1)

        with ExitStack() as prep:
            pc = Scope(nc, prep, "w1")
            w = pc.sb("w", [DC, 2, 2, 2 * WG])
            bias = pc.sb("bias", [96, 2, 2, WG])
            part = pc.sb("part", [96, 2, 2, WG], BF16)
            mean = pc.sb("mean", [128, 4, GH])
            bmean = pc.sb("bmean", [96, 4, GH])
            loaded, b_loaded, cleared = pc.sem("ld"), pc.sem("b_ld"), pc.sem("cleared")
            dve_steps = pc.sem("dve_steps")
            block = prep.enter_context(nc.Block())

            @block.sync
            def _(sp):
                load(sp, 0)
                sp.dma_start(w[:, :, :, :], wkv).then_inc(loaded, 16)
                sp.dma_start(ident[:, :], ident_in).then_inc(loaded, 16)
                sp.dma_start(affine[:, :], affine_in).then_inc(loaded, 16)
                sp.dma_start(blocks[:, :], blocks_in).then_inc(loaded, 16)
                sp.wait_ge(cleared, 2)
                for row in (0, 32, 64):
                    sp.dma_start(bias[row:row + 1, :, :, :].rearrange("p a b c -> p (a b c)"),
                                 bk.rearrange("(o a) -> o a", o=1)).then_inc(b_loaded, 16)

            @block.gpsimd
            def _(pool):
                pool.memset(bias[:, :, :, :], 0.0).then_inc(cleared, 1)
                pool.memset(bias_rows[:, :, :, :], 0.0).then_inc(cleared, 1)
                pool.memset(one_rows[:, :], 1.0).then_inc(cleared, 1)
                pool.memset(ones[:, :], 1.0).then_inc(cleared, 1)
                pool.wait_ge(cleared, 4)
                for c in range(NCH):
                    split(pool, 0, c)

            @block.vector
            def _(dve):
                ch = Chain(dve, dve_steps)
                dve.wait_ge(loaded, 64)
                dve.wait_ge(b_loaded, 48)
                for m, x, n in ((mean, w, 128), (bmean, bias, 96)):
                    keys = x[:, :, :, 0:WG].rearrange("p a b (h e) -> p (a b) h e", e=HD1)
                    ch.link(dve.tensor_reduce(m[:, :, :], keys, AX.X, ALU.add))
                    ch.link(dve.tensor_scalar(m[:, :, :], m[:, :, :], 1.0 / HD1, None, ALU.mult))
                    ch.link(dve.tensor_tensor(keys, keys, m[:, :, :].rearrange("p k (h a) -> p k h a", a=1)
                                              .broadcast_to([n, 4, GH, HD1]), ALU.subtract))
                ch.link(dve.tensor_copy(w_hi[:, :, :], w[:, 0]))
                ch.done(dve.tensor_tensor(w_lo[:, :, :], w[:, 0], w_hi[:, :, :].bitcast(F32), ALU.subtract))
                ch.done(dve.tensor_copy(w_dca[:, :, :], w[:, 1]))
                for row in (0, 32, 64):
                    ch.link(dve.tensor_copy(part[:, :, :, :], bias[:, :, :, :]))
                    ch.done(dve.tensor_copy(bias_rows[row:row + 1], part[row:row + 1]))
                    ch.link(dve.tensor_tensor(bias[:, :, :, :], bias[:, :, :, :], part[:, :, :, :], ALU.subtract))

        k_hi = [sc.sb(f"k_hi{p}", [WG, SK], F32R) for p in range(2)]
        k_lo = [sc.sb(f"k_lo{p}", [WG, SK], F32R) for p in range(2)]
        v_raw = [sc.sb(f"v_raw{p}", [KT, NKT, WG]) for p in range(2)]
        v_hi = sc.sb("v_hi", [KT, NKT, WG], F32R)
        v_lo = sc.sb("v_lo", [KT, NKT, WG], F32R)
        q_block = sc.sb("q_block", [WG, GH, S])
        q_hi = [sc.sb(f"q_hi{p}", [WG, GH * S], F32R) for p in range(2)]
        q_lo = [sc.sb(f"q_lo{p}", [WG, GH * S], F32R) for p in range(2)]
        k_raw = sc.sb("k_raw", [KT, NKT, WG])
        k_sq = sc.sb("k_sq", [KT, 4, WG])
        k_full = sc.sb("k_full", [WG, SK])
        var, k_r, t1, t2 = (sc.sb(n, [KT, NKT * GH]) for n in ("var", "k_r", "n1", "n2"))
        probs = [sc.sb(f"probs{p}", [TT, SK]) for p in range(2)]
        pT_hi = [sc.sb(f"pT_hi{p}", [KT, NKT, HALF], F32R) for p in range(2)]
        pT_lo = [sc.sb(f"pT_lo{p}", [KT, NKT, HALF], F32R) for p in range(2)]
        part_min = sc.sb("part_min", [TT, 2, NCH])
        row_min = sc.sb("row_min", [TT, 2])
        dca_s = sc.sb("dca_s", [TT, 2, DCA])
        dca_e = sc.sb("dca_e", [TT, 2, DCA])
        dca_min, dca_sum, dca_inv = (sc.sb(n, [TT, 2]) for n in ("dca_min", "dca_sum", "dca_inv"))
        sums = sc.sb("sums", [TT, 2, UNIT])
        inv = sc.sb("inv", [TT, UNIT])
        inv_diag = sc.sb("inv_diag", [TT, UNIT, TT])
        inv_all = sc.sb("inv_all", [WG, HALF])
        inv_block = sc.sb("inv_block", [WG, GH, S])
        s_ps = [sc.ps(f"s{k}", [128, 512]) for k in range(NS)]
        t_ps = [sc.ps(f"t{k}", [128, 512]) for k in range(NS)]
        o_ps = sc.ps("o_ps", [128, 512])
        kv_ps = x_ps = sc.ps("kv_ps", [128, 512])

        q_steps, q_ready = sc.sem("q_steps"), sc.sem("q_ready")
        kv_made, kv_kept = sc.sem("kv_made"), sc.sem("kv_kept")
        v_hi_made, values_ready = sc.sem("v_hi_made"), sc.sem("values_ready")
        squared, k_summed, k_normed = sc.sem("squared"), sc.sem("k_summed"), sc.sem("k_normed")
        k_turned, k_scaled = sc.sem("k_turned"), sc.sem("k_scaled")
        k_hi_made, keys_ready = sc.sem("k_hi_made"), sc.sem("keys_ready")
        scored, score_kept, dca_kept = sc.sem("scored"), sc.sem("score_kept"), sc.sem("dca_kept")
        row_max, dve_steps = sc.sem("row_max"), sc.sem("dve_steps")
        dca_exp, probs_made, dca_ready = sc.sem("dca_exp"), sc.sem("probs_made"), sc.sem("dca_ready")
        turned, turn_hi, turn_kept = sc.sem("turned"), sc.sem("turn_hi"), sc.sem("turn_kept")
        diag_made, inv_spread = sc.sem("diag_made"), sc.sem("inv_spread")
        inv_taken, inv_kept = sc.sem("inv_taken"), sc.sem("inv_kept")
        weighted, o_kept, o_done = sc.sem("weighted"), sc.sem("o_kept"), sc.sem("o_done")
        PAIRS = NKT // 2
        SCALED = NCH + 1
        block = ctx.enter_context(nc.Block())

        def bodies(eng, start, body, last):
            start()
            body(0, True, False)
            with eng.Fori(1, B - 1) as i:
                body(i, False, False)
            body(B - 1, False, True)
            last()

        @block.sync
        def _(sp):
            def body(b, first, final):
                if not final:
                    load(sp, b + 1)

            bodies(sp, lambda: None, body, lambda: None)

        @block.gpsimd
        def _(pool):
            def next_split(b, c):
                wait(pool, kv_made, PAIRS * (2 * b - 1) + 2 * c + 2)
                split(pool, b, c)

            def queries(v, b, g):
                wait(pool, scored, UNIT * NCH * (v - 1))
                wait(pool, q_ready, v)
                pool.tensor_tensor(
                    q_block[:, :, :],
                    qT[:, g, bass.ds(b * S, S)].rearrange("p (a t) -> p a t", a=1).broadcast_to([WG, GH, S]),
                    blocks[:, :].rearrange("p (h a) -> p h a", a=1).broadcast_to([WG, GH, S]), ALU.mult
                ).then_inc(q_steps, 1)
                pool.wait_ge(q_steps, 2 * v + 1)
                q = q_block[:, :, :].rearrange("p h t -> p (h t)")
                upper_part(pool, q_hi[g][:, :], q, ones).then_inc(q_steps, 1)
                pool.wait_ge(q_steps, 2 * v + 2)
                pool.tensor_tensor(q_lo[g][:, :], q, q_hi[g][:, :].bitcast(F32), ALU.subtract).then_inc(q_ready, 1)

            def keys(v, g, c):
                cols = slice(c * CK, (c + 1) * CK)
                pool.wait_ge(k_scaled, SCALED * v + c + 2)
                if c == 0:
                    wait(pool, scored, UNIT * NCH * (v - 1))
                upper_part(pool, k_hi[g][:, cols], k_full[:, cols], ones).then_inc(k_hi_made, 1)
                pool.wait_ge(k_hi_made, NCH * v + c + 1)
                pool.tensor_tensor(k_lo[g][:, cols], k_full[:, cols], k_hi[g][:, cols].bitcast(F32), ALU.subtract
                                   ).then_inc(keys_ready, 1)

            def values(v, g, q):
                tiles = slice(PIECES[q], PIECES[q + 1])
                n = UNIT * v + q
                pool.wait_ge(kv_kept, 2 * (PAIRS * v + (PIECES[q + 1] + 1) // 2))
                wait(pool, weighted, n - UNIT + 1)
                upper_part(pool, v_hi[:, tiles, :].rearrange("p n c -> p (n c)"),
                           v_raw[g][:, tiles, :].rearrange("p n c -> p (n c)"), ones).then_inc(v_hi_made, 1)
                pool.wait_ge(v_hi_made, n + 1)
                pool.tensor_tensor(v_lo[:, tiles, :], v_raw[g][:, tiles, :], v_hi[:, tiles, :].bitcast(F32),
                                   ALU.subtract).then_inc(values_ready, 1)

            def own_blocks(u):
                pool.wait_ge(inv_taken, u + 1)
                wait(pool, o_done, u)
                pool.tensor_tensor(inv_block[:, :, :], inv_all[:, :].rearrange("p (h t) -> p h t", t=S),
                                   blocks[:, :].rearrange("p (h a) -> p h a", a=1).broadcast_to([WG, GH, S]),
                                   ALU.mult).then_inc(inv_kept, 1)

            def start():
                queries(0, 0, 0)
                for c in range(NCH):
                    keys(0, 0, c)

            def body(b, first, final):
                for g in range(2):
                    u = 2 * b + g
                    v, vg = u + 1, (g + 1) % 2
                    if not (first and g == 0):
                        values(u - 1, vg, UNIT - 1)
                    if g == 0 and not final:
                        next_split(b + 1, 0)
                    if not (final and g == 1):
                        queries(v, b + g, vg)
                    values(u, g, 0)
                    if g == 0 and not final:
                        next_split(b + 1, 1)
                    values(u, g, 1)
                    if not (first and g == 0):
                        own_blocks(u - 1)
                    if not (final and g == 1):
                        keys(v, vg, 0)
                        keys(v, vg, 1)
                    if g == 0 and not final:
                        next_split(b + 1, 2)
                    if not (final and g == 1):
                        keys(v, vg, 2)
                    values(u, g, 2)

            def last():
                values(2 * B - 1, 1, UNIT - 1)
                own_blocks(2 * B - 1)

            bodies(pool, start, body, last)

        @block.tensor
        def _(pe):
            def project(v, b, g, pair):
                if pair == 0:
                    wait(pe, k_scaled, SCALED * v)
                if pair % 2 == 0:
                    pe.wait_ge(split_done, NCH * b + pair // 2 + 1)
                wait(pe, kv_kept, 2 * (PAIRS * v + pair))
                for k in range(2):
                    j = 2 * pair + k
                    cols = slice(j * KT, (j + 1) * KT)
                    out = kv_ps[0:KT, k * 2 * WG:(k + 1) * 2 * WG]
                    pe.matmul(out, cT_hi[:, cols], w_hi[:, g, :], start=True, stop=False)
                    pe.matmul(out[:, 0:WG], one_rows[:, 0:KT], bias_rows[:, 0, g, :], start=False, stop=False)
                    pe.matmul(out, cT_hi[:, cols], w_lo[:, g, :], start=False, stop=False)
                    mm = pe.matmul(out, cT_lo[:, cols], w_hi[:, g, :], start=False, stop=True)
                    if j == 0:
                        top = kv_ps[0:DCA, :]
                        pe.matmul(top[:, WG:2 * WG], dcaT[:, :], w_dca[:, g, WG:2 * WG], start=True, stop=True)
                        pe.matmul(top[:, 0:WG], dcaT[:, :], w_dca[:, g, 0:WG], start=True, stop=False)
                        pe.matmul(top[:, 0:WG], one_rows[:, 0:DCA], bias_rows[:, 1, g, :], start=False, stop=True)
                mm.then_inc(kv_made, 1)

            def turn_keys(v, c):
                pe.wait_ge(k_normed, NCH * v + c + 1)
                if c == 0 and not (isinstance(v, int) and v == 0):
                    wait(pe, inv_taken, v - 1)
                wait(pe, k_scaled, SCALED * v + c + 1 if c else SCALED * v)
                for k in range(4):
                    mm = pe.transpose(x_ps[:, k * KT:(k + 1) * KT], k_raw[:, 4 * c + k, :], ident[0:KT, 0:KT])
                mm.then_inc(k_turned, 1)

            def scores(n, s, u, after_first=None):
                g, r = s // UNIT, s % UNIT
                rows = slice(r * TT, (r + 1) * TT)
                for c in range(NCH):
                    m = NCH * n + c
                    wait(pe, score_kept, m - NS + 1)
                    if c == 0:
                        wait(pe, dca_kept, n)
                    if r == 0:
                        pe.wait_ge(keys_ready, NCH * u + c + 1)
                    keys = slice(c * CK, (c + 1) * CK)
                    three_passes(pe, s_ps[c][0:TT, 0:CK], q_hi[g][:, rows], q_lo[g][:, rows],
                                 k_hi[g][:, keys], k_lo[g][:, keys], True, True).then_inc(scored, 1)
                    if c == 0 and after_first:
                        after_first()

            def turn(n, s):
                pe.wait_ge(probs_made, n + 1)
                pe.wait_ge(dca_ready, n + 1)
                for f in range(NCH):
                    m = NCH * n + f
                    wait(pe, turn_kept, m - NS + 1)
                    for k in range(4):
                        j = 4 * f + k
                        mm = pe.transpose(t_ps[f][0:KT, k * TT:(k + 1) * TT],
                                          probs[s % 2][:, j * KT:(j + 1) * KT], ident[0:TT, 0:TT])
                    mm.then_inc(turned, 1)

            def spread(u, pairs_kept):
                pe.wait_ge(diag_made, u + 1)
                pe.wait_ge(kv_kept, pairs_kept)
                pe.matmul(x_ps[:, 0:HALF], ones[0:TT, :], inv_diag[:, :, :].rearrange("p k t -> p (k t)"),
                          start=True, stop=True).then_inc(inv_spread, 1)

            def weigh(u, g, r, amid=None):
                pe.wait_ge(values_ready, UNIT * u + r + 1)
                if r == 0:
                    wait(pe, o_kept, u)
                for j in range(PIECES[r], PIECES[r + 1]):
                    if j % 4 == 0 or j == PIECES[r]:
                        pe.wait_ge(turn_kept, NCH * UNIT * u + NCH * (UNIT - 1) + j // 4 + 1)
                    if j == PIECES[r] + 2 and amid:
                        amid()
                    mm = three_passes(pe, o_ps[:, 0:HALF], v_hi[:, j, :], v_lo[:, j, :],
                                      pT_hi[g][:, j, :], pT_lo[g][:, j, :], j == 0, j == NKT - 1)
                mm.then_inc(weighted, 1)

            def start():
                for pair in range(PAIRS):
                    project(0, 0, 0, pair)
                for c in range(NCH):
                    turn_keys(0, c)
                for pair in range(3):
                    project(1, 0, 1, pair)

            def body(b, first, final):
                for s in range(STEPS):
                    n, g, r = STEPS * b + s, s // UNIT, s % UNIT
                    u = 2 * b + g
                    v, vb, vg = u + 1, b + g, (g + 1) % 2
                    more = not (final and g == 1)

                    def extra_work(k):
                        if r == 0 and more:
                            project(v, vb, vg, 3 + k)
                        if r == 1 and k == 0 and not (first and s == 1):
                            spread(u - 1, 2 * PAIRS * (v + 1 if more else v))
                        if r == 2 and more and k == 1:
                            turn_keys(v, 0)

                        if r == 3 and not final:
                            project(v + 1, b + 1, g, k)

                    if r == 0:
                        pe.wait_ge(q_ready, u + 1)
                    scores(n, s, u, (lambda: turn_keys(v, 2)) if r == 3 and more else None)
                    extra_work(0)
                    if not (first and s == 0):
                        turn(n - 1, (s - 1) % STEPS)
                    extra_work(1)
                    if not (first and s < UNIT):
                        weigh(u - 1, (g + 1) % 2, r, (lambda: turn_keys(v, 1)) if r == 2 and more else None)
                    elif r == 2:
                        turn_keys(v, 1)
                    extra_work(2)

            def last():
                turn(STEPS * B - 1, STEPS - 1)
                spread(2 * B - 1, 2 * PAIRS * 2 * B)
                for r in range(UNIT):
                    weigh(2 * B - 1, 1, r)

            bodies(pe, start, body, last)

        @block.scalar
        def _(act):
            def keep(v, g, pair):
                act.wait_ge(kv_made, PAIRS * v + pair + 1)
                j = 2 * pair
                kv = kv_ps[0:KT, :].rearrange("p (k n) -> p k n", k=2)
                wait(act, k_turned, NCH * (v - 1) + pair // 2 + 1)
                act.copy(k_raw[:, j:j + 2, :], kv[:, :, 0:WG]).then_inc(kv_kept, 1)
                wait(act, values_ready, UNIT * (v - 2) + sum(j + 1 >= t for t in PIECES[:-1]))
                act.copy(v_raw[g][:, j:j + 2, :], kv[:, :, WG:2 * WG]).then_inc(kv_kept, 1)

            def square(v, c):
                act.wait_ge(kv_kept, 2 * (PAIRS * v + 2 * c + 2))
                wait(act, k_summed, NCH * v + c)
                act.activation(k_sq[:, :, :], k_raw[:, 4 * c:4 * c + 4, :], ACT.Square).then_inc(squared, 1)

            def scale_keys(v, c):
                act.wait_ge(k_turned, NCH * v + c + 1)
                wait(act, keys_ready, NCH * (v - 1) + c + 1)
                lo = DCA if c == 0 else 0
                if c == 0:
                    act.activation(k_full[:, 0:DCA], x_ps[:, 0:DCA], ACT.Identity, scale=affine[:, 2:3],
                                   bias=affine[:, 3:4]).then_inc(k_scaled, 1)
                act.activation(k_full[:, c * CK + lo:(c + 1) * CK], x_ps[:, lo:CK], ACT.Identity,
                               scale=affine[:, 0:1], bias=affine[:, 1:2]).then_inc(k_scaled, 1)

            def take_inverse(u):
                act.wait_ge(inv_spread, u + 1)
                wait(act, inv_kept, u)
                act.copy(inv_all[:, :], x_ps[:, 0:HALF]).then_inc(inv_taken, 1)

            def upper(n, s, u):
                g, r = s // UNIT, s % UNIT
                for f in range(NCH):
                    act.wait_ge(turned, NCH * n + f + 1)
                    if f == 0 and r == 0:
                        wait(act, weighted, UNIT * (u - 1))
                    act.copy(pT_hi[g][:, 4 * f:4 * f + 4, r * TT:(r + 1) * TT],
                             t_ps[f][0:KT, 0:HALF].rearrange("p (k t) -> p k t", t=TT)
                             ).then_inc(turn_hi, 1)

            def exps(n, s):
                p = s % 2
                act.wait_ge(row_max, n + 1)
                act.activation(dca_e[:, p, :], dca_s[:, p, :], ACT.Exp, scale=-1.0, bias=dca_min[:, p:p + 1],
                               accum_out=dca_sum[:, p:p + 1]).then_inc(dca_exp, 1)
                act.activation(probs[p][:, DCA:SK], probs[p][:, DCA:SK], ACT.Exp, scale=-1.0,
                               bias=row_min[:, p:p + 1],
                               accum_out=sums[:, s // UNIT, s % UNIT:s % UNIT + 1]).then_inc(probs_made, 1)

            def start():
                for c in range(NCH):
                    keep(0, 0, 2 * c)
                    keep(0, 0, 2 * c + 1)
                    square(0, c)
                for c in range(NCH):
                    scale_keys(0, c)
                keep(1, 1, 0)
                keep(1, 1, 1)
                square(1, 0)
                keep(1, 1, 2)

            def body(b, first, final):
                for s in range(STEPS):
                    n, g, r = STEPS * b + s, s // UNIT, s % UNIT
                    u = 2 * b + g
                    v, vg = u + 1, (g + 1) % 2
                    more = not (final and g == 1)
                    if r == 0 and more:
                        keep(v, vg, 3)
                    if r == 3 and more:
                        scale_keys(v, 2)
                    if r == 3 and not final:
                        keep(v + 1, g, 0)
                    if r == 1 and not (first and s == 1):
                        take_inverse(u - 1)
                    if not (first and s == 0):
                        upper(n - 1, (s - 1) % STEPS, 2 * b + (s - 1) // UNIT)
                    if r == 0 and more:
                        square(v, 1)
                    if r == 2 and more:
                        scale_keys(v, 0)
                        scale_keys(v, 1)
                    if r == 0 and more:
                        keep(v, vg, 4)
                    if r == 3 and not final:
                        keep(v + 1, g, 1)
                        square(v + 1, 0)
                    exps(n, s)
                    if r == 0 and more:
                        keep(v, vg, 5)
                        square(v, 2)
                    if r == 3 and not final:
                        keep(v + 1, g, 2)

            def last():
                upper(STEPS * B - 1, STEPS - 1, 2 * B - 1)
                take_inverse(2 * B - 1)

            bodies(act, start, body, last)

        @block.vector
        def _(dve):
            KEYS_N = 10
            UNIT_N = 1
            TILE_N = 1

            def heads(x):
                return x.rearrange("p n (h e) -> p (n h) e", e=HD1)

            def sum_squares(v, c):
                dve.wait_ge(squared, NCH * v + c + 1)
                dve.tensor_reduce(var[:, 4 * GH * c:4 * GH * (c + 1)], heads(k_sq[:, :, :]), AX.X, ALU.add
                                  ).then_inc(k_summed, 1)

            def key_norms(v, ch, between=lambda k: None):
                dve.wait_ge(k_summed, NCH * (v + 1))
                ch.link(dve.tensor_scalar(var[:, :], var[:, :], RSQRT / HD1, EPS_HEAD * RSQRT,
                                          ALU.mult, ALU.add))
                rsqrt(ch, k_r[:, :], var[:, :], t1[:, :], t2[:, :], between)

            def normalise(v, c):
                k = heads(k_raw[:, 4 * c:4 * c + 4, :])
                dve.tensor_tensor(k, k, k_r[:, 4 * GH * c:4 * GH * (c + 1)].rearrange("p (g a) -> p g a", a=1)
                                  .broadcast_to([KT, 4 * GH, HD1]), ALU.mult).then_inc(k_normed, 1)

            def negated(n, s):
                p = s % 2
                wait(dve, turned, NCH * (n - 1))
                for c in range(NCH):
                    dve.wait_ge(scored, NCH * n + c + 1)
                    lo = DCA if c == 0 else 0
                    if c == 0:
                        dve.tensor_scalar(dca_s[:, p, :], s_ps[0][0:TT, 0:DCA], -SCALE, BIG, ALU.mult, ALU.min,
                                          accum_out=dca_min[:, p:p + 1]).then_inc(dca_kept, 1)
                    dve.tensor_scalar(probs[p][:, c * CK + lo:(c + 1) * CK], s_ps[c][0:TT, lo:CK], -SCALE, BIG,
                                      ALU.mult, ALU.min, accum_out=part_min[:, p, c:c + 1]).then_inc(score_kept, 1)
                dve.wait_ge(score_kept, NCH * n + NCH)
                dve.wait_ge(dca_kept, n + 1)
                dve.tensor_reduce(row_min[:, p:p + 1], part_min[:, p, :], AX.X, ALU.min).then_inc(row_max, 1)

            def extra(n, s, ch):
                p = s % 2
                dve.wait_ge(dca_exp, n + 1)
                ch.link(dve.reciprocal(dca_inv[:, p:p + 1], dca_sum[:, p:p + 1]))
                dve.wait_ge(probs_made, n + 1)
                dve.tensor_scalar(probs[p][:, 0:DCA], dca_e[:, p, :], dca_inv[:, p:p + 1],
                                  sums[:, s // UNIT, s % UNIT:s % UNIT + 1], ALU.mult, ALU.mult
                                  ).then_inc(dca_ready, 1)

            def rest(n, s, fills=range(NCH)):
                g, r = s // UNIT, s % UNIT
                rows = slice(r * TT, (r + 1) * TT)
                for f in fills:
                    dve.wait_ge(turn_hi, NCH * n + f + 1)
                    dve.tensor_tensor(pT_lo[g][:, 4 * f:4 * f + 4, rows],
                                      t_ps[f][0:KT, 0:HALF].rearrange("p (k t) -> p k t", t=TT),
                                      pT_hi[g][:, 4 * f:4 * f + 4, rows].bitcast(F32), ALU.subtract
                                      ).then_inc(turn_kept, 1)

            def invert(u, s, ch):
                ch.link(dve.reciprocal(inv[:, :], sums[:, s // UNIT, :]))
                wait(dve, inv_spread, u)
                dve.tensor_tensor(inv_diag[:, :, :],
                                  ident[0:TT, 0:TT].rearrange("p (a t) -> p a t", a=1).broadcast_to([TT, UNIT, TT]),
                                  inv[:, :].rearrange("p (k a) -> p k a", a=1).broadcast_to([TT, UNIT, TT]),
                                  ALU.mult).then_inc(diag_made, 1)

            def scale_sums(u):
                dve.wait_ge(weighted, UNIT * (u + 1))
                dve.wait_ge(inv_kept, u + 1)
                blk = inv_block[:, :, :]
                dve.tensor_tensor(blk, o_ps[:, 0:HALF].rearrange("p (h t) -> p h t", t=S), blk, ALU.mult
                                  ).then_inc(o_kept, 1)

            def finish(u, b, g):
                dve.wait_ge(o_kept, u + 1)
                dve.tensor_reduce(qT[:, g, bass.ds(b * S, S)], inv_block[:, :, :].rearrange("p h t -> p t h"),
                                  AX.X, ALU.add).then_inc(o_done, 1)
                dve.wait_ge(o_done, u + 1)

            def start():
                ch = Chain(dve, dve_steps)
                for c in range(NCH):
                    sum_squares(0, c)
                key_norms(0, ch)
                assert ch.n == KEYS_N
                for c in range(NCH):
                    normalise(0, c)
                sum_squares(1, 0)

            PER_BODY = 2 * (KEYS_N + UNIT_N) + STEPS * TILE_N

            def body(b, first, final):
                ch = Chain(dve, dve_steps, KEYS_N + PER_BODY * b - (0 if first else UNIT_N))
                for s in range(STEPS):
                    n, g, r = STEPS * b + s, s // UNIT, s % UNIT
                    u = 2 * b + g
                    v, vg = u + 1, (g + 1) % 2
                    more = not (final and g == 1)
                    if r == 0 and not (first and s < 2 * UNIT):
                        scale_sums(u - 2)
                    negated(n, s)
                    if r == 2 and more:
                        normalise(v, 2)
                    if r == 1 and more:
                        def between(k):
                            if k < NCH:
                                rest(n - 1, s - 1, (k,))
                            if k == 1:
                                extra(n, s, ch)

                        sum_squares(v, 2)
                        key_norms(v, ch, between)
                        normalise(v, 0)
                        normalise(v, 1)
                        continue
                    if not (first and s == 0):
                        rest(n - 1, (s - 1) % STEPS)
                    if r == 0 and not (first and s == 0):
                        invert(u - 1, (s - 1) % STEPS, ch)
                    if r == 0 and more:
                        sum_squares(v, 1)
                    if r == 3 and not final:
                        sum_squares(v + 1, 0)
                    extra(n, s, ch)
                    if r == 0 and not (first and s < 2 * UNIT):
                        finish(u - 2, b - 1, g)

            def last():
                ch = Chain(dve, dve_steps, PER_BODY * B - UNIT_N)
                scale_sums(2 * B - 2)
                finish(2 * B - 2, B - 1, 0)
                invert(2 * B - 1, STEPS - 1, ch)
                rest(STEPS * B - 1, STEPS - 1)
                scale_sums(2 * B - 1)
                finish(2 * B - 1, B - 1, 1)

            bodies(dve, start, body, last)


def close_heads(nc, wo, bv, bo, x2_d, qT, xs, gate):
    with ExitStack() as ctx:
        sc = Scope(nc, ctx, "c1")
        wo_sb = sc.sb("wo", [128, CH, D])
        bv_sb = sc.sb("bv", [128, 2, CH])
        bsum = sc.sb("bsum", [128, CH])
        bo_sb = sc.sb("bo", [TT, D])
        y = [sc.sb(f"y{k}", [TT, D]) for k in range(2)]
        y_ps = [sc.ps(f"y_ps{k}", [128, 512]) for k in range(4)]
        w_loaded, v_loaded, x_loaded = sc.sem("w_ld"), sc.sem("v_ld"), sc.sem("x_ld")
        dve_steps, biased = sc.sem("dve_steps"), sc.sem("biased")
        projected, with_bias, added = sc.sem("projected"), sc.sem("with_bias"), sc.sem("added")
        block = ctx.enter_context(nc.Block())

        @block.sync
        def _(sp):
            sp.dma_start(bv_sb[:, :, :], bv).then_inc(v_loaded, 16)
            sp.dma_start(wo_sb[:, :, :], wo.rearrange("(c p) d -> p c d", p=128)).then_inc(w_loaded, 16)
            sp.dma_start(bo_sb[:, :], bo.partition_broadcast(TT)).then_inc(v_loaded, 16)
            sp.dma_start(xs[:, :, :], x2_d.rearrange("(n p) d -> p n d", p=TT)).then_inc(x_loaded, 16)

        @block.tensor
        def _(pe):
            pe.wait_ge(w_loaded, 16)
            pe.wait_ge(biased, CH)
            for t in range(NTILE):
                if t >= 4:
                    pe.wait_ge(with_bias, t - 3)
                for c in range(CH):
                    mm = pe.matmul(y_ps[t % 4][0:TT, 0:D], qT[:, c, t * TT:(t + 1) * TT], wo_sb[:, c, :],
                                   start=(c == 0), stop=(c == CH - 1))
                mm.then_inc(projected, 1)

        @block.vector
        def _(dve):
            ch = Chain(dve, dve_steps)
            dve.wait_ge(v_loaded, 32)
            ch.link(dve.tensor_tensor(bsum[:, :], bv_sb[:, 0, :], bv_sb[:, 1, :], ALU.add))
            for c in range(CH):
                dve.tensor_scalar(qT[:, c, :], qT[:, c, :], bsum[:, c:c + 1], None, ALU.add).then_inc(biased, 1)
            dve.wait_ge(x_loaded, 16)
            for t in range(NTILE):
                dve.wait_ge(projected, t + 1)
                if t >= 2:
                    dve.wait_ge(added, t - 1)
                dve.tensor_tensor(y[t % 2][:, :], y_ps[t % 4][0:TT, 0:D], bo_sb[:, :], ALU.add).then_inc(with_bias, 1)
                dve.wait_ge(with_bias, t + 1)
                dve.scalar_tensor_tensor(xs[:, t, :], y[t % 2][:, :], gate[:, 2:3], xs[:, t, :],
                                         ALU.mult, ALU.add).then_inc(added, 1)


BODY = 3
WCOLS = 2 * CH * I + D


class ExpertWeights:

    def __init__(self, sc, weights_in):
        self.weights_in = weights_in
        self.raw = [sc.sb(f"raw{p}", [128, WCOLS]) for p in range(BODY)]
        self.loaded = [sc.sem(f"ld{p}") for p in range(BODY)]

    def load(self, sp, e, p):
        sp.dma_start(self.raw[p][:, :], self.weights_in[bass.ds(e, 1)].rearrange("e p w -> p (e w)")
                     ).then_inc(self.loaded[p], 16)


def route(nc, router_wT, expert_bias, ident_in, xs, x_hi, x_lo, p_d, ew):
    with ExitStack() as ctx:
        sc = Scope(nc, ctx, "rt")
        ident = sc.sb("ident", [128, 128])
        wr = sc.sb("wr", [128, CH, E])
        eb = sc.sb("eb", [TT, E])
        xn = sc.sb("xn", [TT, NTILE, D])
        xnT = sc.sb("xnT", [128, CH, NT])
        z, e, s2, p, pw, score, choice, keep, tie, cnt, cnt2 = (
            sc.sb(n, [TT, NTILE, E]) for n in ("z", "e", "s2", "p", "pw", "score", "choice", "keep", "tie", "cnt", "cnt2"))
        top = sc.sb("top", [TT, NTILE, 8])
        room, total = sc.sb("room", [TT, NTILE]), sc.sb("total", [TT, NTILE])
        one = sc.sb("one", [1, NT])
        pT = sc.sb("pT", [E, NT])
        scratch = ln_scratch(sc)
        banks = [sc.ps(f"b{k}", [128, 512]) for k in range(5)]
        loaded, b_loaded = sc.sem("ld"), sc.sem("b_ld")
        dve_steps, xn_ready = sc.sem("dve_steps"), sc.sem("xn_ready")
        turned, turn_kept, split_hi, split_lo = (sc.sem(n) for n in ("turned", "turn_kept", "split_hi", "split_lo"))
        logits_made, abs_made, exp_made = sc.sem("logits_made"), sc.sem("abs_made"), sc.sem("exp_made")
        shares, p_turned, p_kept, p_stored, ones_set = (
            sc.sem(n) for n in ("shares", "p_turned", "p_kept", "p_stored", "ones_set"))
        block = ctx.enter_context(nc.Block())

        @block.sync
        def _(sp):
            sp.dma_start(ident[:, :], ident_in).then_inc(loaded, 16)
            sp.dma_start(wr[:, :, :], router_wT.rearrange("(c p) e -> p c e", p=128)).then_inc(loaded, 16)
            sp.dma_start(eb[:, :], expert_bias.partition_broadcast(TT)).then_inc(b_loaded, 16)
            for p in range(BODY):
                ew.load(sp, p, p)
            sp.wait_ge(ones_set, 1)
            sp.dma_start(p_d[0:1, :], one[:, :]).then_inc(p_stored, 16)
            sp.wait_ge(p_kept, 2)
            sp.dma_start(p_d[1:E + 1, :], pT[:, :]).then_inc(p_stored, 16)
            sp.wait_ge(p_stored, 32)

        @block.gpsimd
        def _(pool):
            pool.memset(one[:, :], 1.0).then_inc(ones_set, 1)

        @block.tensor
        def _(pe):
            pe.wait_ge(loaded, 32)
            turn_tokens(pe, None, xn, xnT, banks[0:2], ident, xn_ready, turned, turn_kept, turn_kept)
            pe.wait_ge(turn_kept, 2 * CH)
            for t in range(NTILE):
                for c in range(CH):
                    mm = pe.matmul(banks[2][0:TT, t * E:(t + 1) * E], xnT[:, c, t * TT:(t + 1) * TT], wr[:, c, :],
                                   start=(c == 0), stop=(c == CH - 1))
            mm.then_inc(logits_made, 1)
            pe.wait_ge(shares, 1)
            for half in range(2):
                for k in range(4):
                    mm = pe.transpose(banks[3 + half][0:E, k * TT:(k + 1) * TT], p[:, 4 * half + k, :],
                                      ident[0:TT, 0:TT])
                mm.then_inc(p_turned, 1)

        @block.scalar
        def _(act):
            turn_tokens(None, act, xn, xnT, banks[0:2], ident, xn_ready, turned, turn_kept, turn_kept)
            act.wait_ge(turn_kept, 2 * CH)
            act.copy(x_hi[:, :, :], xnT[:, :, :]).then_inc(split_hi, 1)
            act.wait_ge(abs_made, 1)
            act.activation(e[:, :, :], z[:, :, :], ACT.Exp).then_inc(exp_made, 1)
            for half in range(2):
                act.wait_ge(p_turned, half + 1)
                act.copy(pT[:, half * HALF:(half + 1) * HALF], banks[3 + half][0:E, 0:HALF]).then_inc(p_kept, 1)

        @block.vector
        def _(dve):
            ch = Chain(dve, dve_steps)
            layer_norm(ch, xn[:, :, :], xs[:, :, :], *scratch, TT, xn_ready)
            dve.wait_ge(split_hi, 1)
            dve.tensor_tensor(x_lo[:, :, :], xnT[:, :, :], x_hi[:, :, :].bitcast(F32), ALU.subtract
                              ).then_inc(split_lo, 1)
            lg = banks[2][0:TT, 0:NTILE * E].rearrange("p (n e) -> p n e", e=E)

            def flat(x):
                return x[:, :, :]

            dve.wait_ge(logits_made, 1)
            ch.link(dve.tensor_copy(flat(s2), lg))
            ch.link(dve.tensor_scalar(flat(z), flat(s2), -1.0, None, ALU.mult))
            dve.tensor_tensor(flat(z), flat(s2), flat(z), ALU.min).then_inc(abs_made, 1)
            ch.link(dve.tensor_scalar(flat(score), flat(s2), 0.0, None, ALU.max))
            dve.wait_ge(exp_made, 1)
            ch.link(dve.tensor_scalar(flat(p), flat(e), 2.0, None, ALU.add))
            ch.link(dve.reciprocal(flat(p), flat(p)))
            ch.link(dve.tensor_tensor(flat(e), flat(e), flat(p), ALU.mult))
            ch.link(dve.tensor_tensor(flat(s2), flat(e), flat(e), ALU.mult))
            ch.link(dve.tensor_scalar(flat(pw), flat(s2), 2.0 / 17, 2.0 / 15, ALU.mult, ALU.add))
            for k in (13, 11, 9, 7, 5, 3, 1):
                ch.link(dve.tensor_tensor(flat(pw), flat(pw), flat(s2), ALU.mult))
                ch.link(dve.tensor_scalar(flat(pw), flat(pw), 2.0 / k, None, ALU.add))
            ch.link(dve.tensor_tensor(flat(pw), flat(pw), flat(e), ALU.mult))
            ch.link(dve.tensor_tensor(flat(z), flat(score), flat(pw), ALU.add))
            ch.link(dve.tensor_scalar(flat(z), flat(z), RSQRT, None, ALU.mult))
            rsqrt(ch, flat(p), flat(z), flat(s2), flat(pw))
            ch.link(dve.scalar_tensor_tensor(flat(score), flat(z), 1.0 / RSQRT, flat(p), ALU.mult, ALU.mult))
            dve.wait_ge(b_loaded, 16)
            ch.link(dve.tensor_tensor(flat(choice), flat(score),
                                      eb[:, :].rearrange("p (a e) -> p a e", a=1).broadcast_to([TT, NTILE, E]),
                                      ALU.add))
            for t in range(NTILE):
                ch.done(dve.max(top[:, t, :], choice[:, t, :]))
            ch.settle()
            fourth = top[:, :, TOPK - 1:TOPK].broadcast_to([TT, NTILE, E])
            ch.link(dve.tensor_tensor(flat(keep), flat(choice), fourth, ALU.is_gt))
            ch.link(dve.tensor_tensor(flat(tie), flat(choice), fourth, ALU.is_equal))
            ch.link(dve.tensor_reduce(room[:, :], flat(keep), AX.X, ALU.add))
            ch.link(dve.tensor_scalar(room[:, :], room[:, :], -1.0, float(TOPK), ALU.mult, ALU.add))
            a, b = tie, cnt
            for w in (1, 2, 4, 8, 16):
                ch.done(dve.tensor_copy(b[:, :, 0:w], a[:, :, 0:w]))
                ch.link(dve.tensor_tensor(b[:, :, w:E], a[:, :, w:E], a[:, :, 0:E - w], ALU.add))
                a, b = b, (cnt2 if b is cnt else cnt)
            ch.link(dve.tensor_tensor(flat(a), flat(a), room[:, :].rearrange("p (n a) -> p n a", a=1)
                                      .broadcast_to([TT, NTILE, E]), ALU.is_le))
            ch.link(dve.tensor_tensor(flat(tie), flat(tie), flat(a), ALU.mult))
            ch.link(dve.tensor_tensor(flat(keep), flat(keep), flat(tie), ALU.add))
            ch.link(dve.tensor_tensor(flat(score), flat(score), flat(keep), ALU.mult))
            ch.link(dve.tensor_reduce(total[:, :], flat(score), AX.X, ALU.add))
            ch.link(dve.tensor_scalar(total[:, :], total[:, :], 1e-20, None, ALU.add))
            ch.link(dve.reciprocal(total[:, :], total[:, :]))
            dve.tensor_tensor(flat(p), flat(score), total[:, :].rearrange("p (n a) -> p n a", a=1)
                              .broadcast_to([TT, NTILE, E]), ALU.mult).then_inc(shares, 1)


def experts(nc, ew, p_d, x_hi, x_lo, xs, gate, out):
    UP, DOWN = CH * I, 2 * CH * I
    LAG = 3
    NE = E + 1
    SLOTS = 2 * BODY
    assert NE % BODY == 0
    with ExitStack() as ctx:
        sc = Scope(nc, ctx, "ex")
        raw, w_loaded = ew.raw, ew.loaded
        w_hi = [sc.sb(f"w_hi{p}", [128, WCOLS], F32R) for p in range(BODY)]
        w_lo = [sc.sb(f"w_lo{p}", [128, WCOLS], F32R) for p in range(BODY)]
        share = [sc.sb(f"share{p}", [128, NT]) for p in range(BODY)]
        zeros = sc.sb("zeros", [128, 512], BF16)
        gate_c, up_c, silu, up_p, h = ([sc.sb(f"{n}{p}", [I, HALF]) for p in range(2)]
                                       for n in ("gate_c", "up_c", "silu", "up_p", "h"))
        h_hi = [sc.sb(f"h_hi{p}", [I, HALF], F32R) for p in range(LAG)]
        h_lo = [sc.sb(f"h_lo{p}", [I, HALF], F32R) for p in range(LAG)]
        y_ps = [sc.ps(f"y{k}", [128, 512]) for k in range(4)]
        g_ps = [sc.ps(f"g{k}", [128, 512]) for k in range(2)]
        u_ps = [sc.ps(f"u{k}", [128, 512]) for k in range(2)]
        p_loaded = [sc.sem(f"p_ld{p}") for p in range(BODY)]
        cleared, w_hi_made, w_ready = sc.sem("cleared"), sc.sem("w_hi_made"), sc.sem("w_ready")
        made, gate_clipped, clipped = sc.sem("made"), sc.sem("gate_clipped"), sc.sem("clipped")
        silu_made, scaled, h_made, h_hi_made, h_ready = (
            sc.sem(n) for n in ("silu_made", "scaled", "h_made", "h_hi_made", "h_ready"))
        downed, added, stored = sc.sem("downed"), sc.sem("added"), sc.sem("stored")
        block = ctx.enter_context(nc.Block())

        def bodies(eng, body, last):
            body(0, True, False)
            with eng.Fori(1, NE // BODY - 1) as i:
                body(i, False, False)
            body(NE // BODY - 1, False, True)
            last()

        @block.sync
        def _(sp):
            def body(i, first, final):
                for p in range(BODY):
                    e = BODY * i + p
                    if not first:
                        wait(sp, w_ready, e - BODY + 1)
                        ew.load(sp, e, p)
                    wait(sp, scaled, 2 * (e - BODY) + 2)
                    sp.dma_start(share[p][:, :], p_d[bass.ds(e, 1)].rearrange("e t -> (e t)").partition_broadcast(128)
                                 ).then_inc(p_loaded[p], 16)

            def last():
                for t in range(NTILE):
                    sp.wait_ge(added, t + 1)
                    sp.dma_start(out[t * TT:(t + 1) * TT, :], xs[:, t, :]).then_inc(stored, 16)
                sp.wait_ge(stored, 16 * NTILE)

            bodies(sp, body, last)

        @block.gpsimd
        def _(pool):
            def weights_rest(e, p):
                pool.wait_ge(w_hi_made, e + 1)
                pool.tensor_tensor(w_lo[p][:, :], raw[p][:, :], w_hi[p][:, :].bitcast(F32), ALU.subtract
                                   ).then_inc(w_ready, 1)

            def body(i, first, final):
                if first:
                    pool.memset(zeros[:, :], 0.0).then_inc(cleared, 1)
                    weights_rest(0, 0)
                for k in range(SLOTS):
                    m, p, half = SLOTS * i + k, k // 2, k % 2
                    if half == 0:
                        pool.wait_ge(p_loaded[p], 16 * (i + 1))
                    pool.wait_ge(clipped, m + 1)
                    wait(pool, h_made, m - 1)
                    pool.tensor_tensor(up_p[half][:, :], up_c[half][:, :],
                                       share[p][:, half * HALF:(half + 1) * HALF], ALU.mult).then_inc(scaled, 1)
                    if half == 0 and not (final and p == BODY - 1):
                        weights_rest(BODY * i + p + 1, (p + 1) % BODY)

            bodies(pool, body, lambda: None)

        @block.tensor
        def _(pe):
            pe.wait_ge(cleared, 1)
            for k in range(4):
                pe.matmul(y_ps[k][0:TT, :], zeros[:, 0:TT], zeros[:, :], start=True, stop=True,
                          skip_group_check=True)

            def gate_up(e, m, p, half):
                if half == 0:
                    pe.wait_ge(w_ready, e + 1)
                wait(pe, clipped, m - 1)
                cols = slice(half * HALF, (half + 1) * HALF)
                for bank, base in ((g_ps[half], 0), (u_ps[half], UP)):
                    for c in range(CH):
                        w = slice(base + c * I, base + (c + 1) * I)
                        mm = three_passes(pe, bank[:, 0:HALF], w_hi[p][:, w], w_lo[p][:, w],
                                          x_hi[:, c, cols], x_lo[:, c, cols], c == 0, c == CH - 1)
                mm.then_inc(made, 1)

            def down(m, k):
                p, half, place = k // 2, k % 2, k % LAG
                pe.wait_ge(h_ready, m + 1)
                for t in range(4):
                    tile = 4 * half + t
                    rows = slice(t * TT, (t + 1) * TT)
                    y = y_ps[tile // 2][0:TT, (tile % 2) * D:(tile % 2 + 1) * D]
                    for a, b in ((h_hi, w_hi), (h_hi, w_lo), (h_lo, w_hi)):
                        mm = pe.matmul(y, a[place][:, rows], b[p][:, DOWN:WCOLS], start=False, stop=False,
                                       skip_group_check=True)
                mm.then_inc(downed, 1)

            def body(i, first, final):
                for k in range(SLOTS):
                    m = SLOTS * i + k
                    gate_up(BODY * i + k // 2, m, k // 2, k % 2)
                    if not (first and k < LAG):
                        down(m - LAG, (k - LAG) % SLOTS)

            def last():
                for k in range(SLOTS - LAG, SLOTS):
                    down(2 * NE - SLOTS + k, k)

            bodies(pe, body, last)

        @block.scalar
        def _(act):
            def weights_upper(e, i, p):
                act.wait_ge(w_loaded[p], 16 * (i + 1))
                wait(act, downed, 2 * (e - BODY) + 2)
                act.copy(w_hi[p][:, :], raw[p][:, :]).then_inc(w_hi_made, 1)

            def upper(m, k):
                act.wait_ge(h_made, m + 1)
                wait(act, downed, m - LAG + 1)
                act.copy(h_hi[k % LAG][:, :], h[k % 2][:, :]).then_inc(h_hi_made, 1)

            def body(i, first, final):
                if first:
                    weights_upper(0, 0, 0)
                for k in range(SLOTS):
                    m, p, half = SLOTS * i + k, k // 2, k % 2
                    act.wait_ge(gate_clipped, m + 1)
                    wait(act, h_made, m - 1)
                    act.activation(silu[half][:, :], gate_c[half][:, :], ACT.Silu).then_inc(silu_made, 1)
                    if half == 0 and not (final and p == BODY - 1):
                        weights_upper(BODY * i + p + 1, i + (p + 1) // BODY, (p + 1) % BODY)
                    if not (first and k == 0):
                        upper(m - 1, (k - 1) % SLOTS)

            bodies(act, body, lambda: upper(2 * NE - 1, SLOTS - 1))

        @block.vector
        def _(dve):
            def clip(m, k):
                half = k % 2
                dve.wait_ge(made, m + 1)
                wait(dve, silu_made, m - 1)
                dve.tensor_scalar(gate_c[half][:, :], g_ps[half][:, 0:HALF], -ALPHA, ALPHA, ALU.max, ALU.min
                                  ).then_inc(gate_clipped, 1)
                wait(dve, scaled, m - 1)
                dve.tensor_scalar(up_c[half][:, :], u_ps[half][:, 0:HALF], -ALPHA, ALPHA, ALU.max, ALU.min
                                  ).then_inc(clipped, 1)

            def hidden(m, k):
                half = k % 2
                dve.wait_ge(silu_made, m + 1)
                dve.wait_ge(scaled, m + 1)
                wait(dve, h_ready, m - 1)
                dve.tensor_tensor(h[half][:, :], silu[half][:, :], up_p[half][:, :], ALU.mult).then_inc(h_made, 1)

            def rest(m, k):
                dve.wait_ge(h_hi_made, m + 1)
                dve.tensor_tensor(h_lo[k % LAG][:, :], h[k % 2][:, :], h_hi[k % LAG][:, :].bitcast(F32), ALU.subtract
                                  ).then_inc(h_ready, 1)

            def body(i, first, final):
                for k in range(SLOTS):
                    m = SLOTS * i + k
                    clip(m, k)
                    if not (first and k < 2):
                        rest(m - 2, (k - 2) % SLOTS)
                    if not (first and k < 1):
                        hidden(m - 1, (k - 1) % SLOTS)

            def last():
                rest(2 * NE - 2, SLOTS - 2)
                hidden(2 * NE - 1, SLOTS - 1)
                rest(2 * NE - 1, SLOTS - 1)
                dve.wait_ge(downed, 2 * NE)
                for t in range(NTILE):
                    dve.scalar_tensor_tensor(xs[:, t, :], y_ps[t // 2][0:TT, (t % 2) * D:(t % 2 + 1) * D],
                                             gate[:, 3:4], xs[:, t, :], ALU.mult, ALU.add).then_inc(added, 1)

            bodies(dve, body, last)


def build(nc, a, out):
    def scratch(name, shape):
        return nc.dram_tensor(name, shape, F32).ap()

    q_d, o_d = scratch("q_d", [DC, B, H0, S]), scratch("o_d", [DC, B, H0 * S])
    x2_d, p_d = scratch("x2_d", [NT, D]), scratch("p_d", [E + 1, NT])
    with ExitStack() as ctx:
        cx = ContextParts(Scope(nc, ctx, "cx"), a["ctx"], a["ctxT"], a["mask"], q_d)
        project_queries(nc, a["x"], a["wqT"], a["wkT"], a["ident"], cx)
        attend_context(nc, a["ident"], cx, o_d)
    with nc.sbuf_tensor("gate", [TT, 4], F32) as gate, nc.sbuf_tensor("qT", [128, CH, NT], F32) as qT:
        with nc.sbuf_tensor("x12", [TT, NTILE, D], F32) as xs:
            with ExitStack() as ctx:
                fw = FeedForwardWeights(Scope(nc, ctx, "fw"), a["w1T"], a["w3T"], a["w2T"], a["hadamard"], a["ident"])
                close_attention(nc, o_d, a["x"], a["wvT"], a["wo0"], a["gates"], xs, gate, fw)
                feed_forward(nc, fw, xs, gate)
            project_heads(nc, a["wq1"], a["bq1"], a["q_affine"], a["ident"], xs, qT, x2_d)
        attend_heads(nc, a["ctxT"], a["wkv"], a["bk"], a["affine"], a["blocks"], a["ident"], qT)
        with (nc.sbuf_tensor("x34", [TT, NTILE, D], F32) as xs, nc.sbuf_tensor("x_hi", [128, CH, NT], F32R) as x_hi,
              nc.sbuf_tensor("x_lo", [128, CH, NT], F32R) as x_lo):
            close_heads(nc, a["wo1"], a["bv"], a["bo"], x2_d, qT, xs, gate)
            with ExitStack() as ctx:
                ew = ExpertWeights(Scope(nc, ctx, "ew"), a["expert_w"])
                route(nc, a["router_wT"], a["expert_bias"], a["ident"], xs, x_hi, x_lo, p_d, ew)
                experts(nc, ew, p_d, x_hi, x_lo, xs, gate, out)


def kernel(**inputs):
    import numpy as np
    import concourse.bacc as bacc
    from concourse.bass_utils import run_bass_kernel_spmd

    v = {k: np.asarray(x) for k, x in inputs.items()}

    def turned(x):
        return np.ascontiguousarray(np.swapaxes(x, -1, -2))

    def extra_first(x):
        return np.ascontiguousarray(np.concatenate([x[:, SK - DCA:], x[:, :SK - DCA]], axis=1))

    def main_groups(k, w):
        both = np.concatenate([k, w], axis=-1)
        n = both.shape[0]
        return both.reshape(n, 2, GH, 2, HD1).transpose(0, 1, 3, 2, 4).reshape(n, 2, 2 * WG)

    def extra_groups(w):
        n = w.shape[0]
        return w.reshape(n, 2, 2, GH, HD1).transpose(0, 2, 1, 3, 4).reshape(n, 2, 2 * WG)

    hadamard = np.ones((1, 1), np.float32)
    for _ in range(7):
        hadamard = np.block([[hadamard, hadamard], [hadamard, -hadamard]])
    context = extra_first(v["ctx_1024"])
    mask = extra_first(v["mask_BxS2_bf1"]).view(np.uint8)
    wkv = np.stack([main_groups(v["L1_xattn_Wk"], v["L1_xattn_Wv"]), extra_groups(v["L1_xattn_Wkv_dca"])], axis=1)
    bkv = np.stack([main_groups(v["L1_xattn_bk"][None], v["L1_xattn_bv"][None])[0],
                    extra_groups(v["L1_xattn_bkv_dca"][None])[0]])

    def expert_columns(gate, up, down):
        n = gate.shape[0]
        g, u = (turned(w).reshape(n, CH, 128, I).transpose(0, 2, 1, 3).reshape(n, 128, CH * I) for w in (gate, up))
        return np.concatenate([g, u, turned(down)], axis=2)

    arrays = {
        "x": v["x"].reshape(NT, D), "ctx": context, "ctxT": turned(context), "mask": mask,
        "gates": np.stack([v["g_xattn"], v["g_ffn"]], axis=1).reshape(4),
        "wqT": turned(v["L0_xattn_Wq"]), "wkT": turned(v["L0_xattn_Wk"]), "wvT": turned(v["L0_xattn_Wv"]),
        "wo0": v["L0_xattn_Wo"], "w1T": turned(v["L0_ffn_W1"]), "w3T": turned(v["L0_ffn_W3"]),
        "w2T": turned(v["L0_ffn_W2"]), "hadamard": hadamard, "ident": np.eye(128, dtype=np.float32),
        "wq1": v["L1_xattn_Wq"], "bq1": v["L1_xattn_bq"],
        "q_affine": np.stack([np.tile(v["L1_xattn_qn_w"], GH), np.tile(v["L1_xattn_qn_b"], GH)], axis=1),
        "wkv": wkv, "bk": bkv[:, :, :WG].reshape(-1),
        "affine": np.stack([np.tile(v["L1_xattn_" + n], GH) for n in ("kn_w", "kn_b", "kn_dca_w", "kn_dca_b")], axis=1),
        "blocks": (np.arange(WG)[:, None] // HD1 == np.arange(GH)[None, :]).astype(np.float32),
        "bv": bkv[:, :, WG:].transpose(2, 0, 1), "wo1": v["L1_xattn_Wo"], "bo": v["L1_xattn_bo"],
        "router_wT": turned(v["L1_ffn_router_w"]), "expert_bias": v["L1_ffn_expert_bias"],
        "expert_w": np.concatenate([
            expert_columns(v["L1_ffn_shared_gate_w"][None], v["L1_ffn_shared_up_w"][None],
                           v["L1_ffn_shared_down_w"][None]),
            expert_columns(v["L1_ffn_gate_w"], v["L1_ffn_up_w"], v["L1_ffn_down_w"])]),
    }
    arrays = {f"in_{k}": np.ascontiguousarray(x) for k, x in arrays.items()}
    nc = bacc.Bacc("TRN2", target_bir_lowering=False, num_devices=1)
    tensors = {k[3:]: nc.dram_tensor(k, x.shape, mybir.dt.from_np(x.dtype), kind="ExternalInput").ap()
               for k, x in arrays.items()}
    out = nc.dram_tensor("out", (NT, D), F32, kind="ExternalOutput").ap()
    build(nc, tensors, out)
    r = run_bass_kernel_spmd(nc, [arrays], core_ids=[0])
    return r.results[0]["out"].reshape(B, S, D)
```
